# Optimizing a Trainium2 kernel written in Bass

```python
import numpy as np
import jax
import jax.numpy as jnp

def _softmax(x, axis=-1):
    return jax.nn.softmax(x, axis=axis)

def _gelu(x):
    return jax.nn.gelu(x, approximate=True)

def _silu(x):
    return jax.nn.silu(x)

def _sigmoid(x):
    return jax.nn.sigmoid(x)

def _layernorm(x, axis=-1, eps=1e-05):
    m = jnp.mean(x, axis=axis, keepdims=True)
    v = jnp.var(x, axis=axis, keepdims=True)
    return (x - m) / jnp.sqrt(v + eps)

def _scatter_add(tgt, idx, src, axis=0):
    return tgt.at[idx].add(src)

def _segment_sum(src, seg, n):
    return jax.ops.segment_sum(src, seg, n)
kernel_name = 'mk_xattn_ffn_d2_seqx_r8_ca89b7'

def setup_inputs(seed: int=0):
    np.random.seed(seed)
    _w = jnp.asarray

    def _rec_inputs():
        import jax
        import jax.numpy as jnp
        _rk = jax.random.key(seed)
        x = 7.22e-05 + 1 * jax.random.normal(jax.random.fold_in(_rk, 1), (64, 128, 128), jnp.float32)
        _lenS = 128 - jax.random.randint(jax.random.fold_in(_rk, 7), (64,), 0, max(1, 128 // 4) + 1, jnp.int32)
        _lenS2 = 120 - jax.random.randint(jax.random.fold_in(_rk, 8), (64,), 0, max(1, 120 // 4) + 1, jnp.int32)
        fside_BxSxS_0 = 4.13588e-05 + 0.999923 * jax.random.normal(jax.random.fold_in(_rk, 11), (64, 128, 128), jnp.float32)
        _ctx_1024P = jax.random.normal(jax.random.fold_in(_rk, 12), (64, 16, 128), jnp.float32)
        _ctx_1024c = jax.random.dirichlet(jax.random.fold_in(_rk, 512), 0.3 * jnp.ones((16,), jnp.float32), (64, 120))
        _ctx_1024t = jnp.einsum('bsk,bkd->bsd', _ctx_1024c, _ctx_1024P)
        _ctx_1024t = _ctx_1024t * jax.lax.rsqrt(jnp.mean(jnp.square(_ctx_1024t)) + 1e-12) * 0.953939
        ctx_1024 = -0.000761806 + 0.999296 * (_ctx_1024t + 0.3 * jax.random.normal(jax.random.fold_in(_rk, 612), (64, 120, 128), jnp.float32))
        return (x, fside_BxSxS_0, ctx_1024)
    x, fside_BxSxS_0, ctx_1024 = _rec_inputs()

    def _L0_xattn_setup():
        import jax, jax.numpy as jnp
        import numpy as np
        DIM = 128
        HEADS = 16
        HEAD_DIM = DIM // HEADS
        B, N1, N2, SLOTS = (8, 128, 128, 64)
        key = jax.random.key(seed)
        ks = jax.random.split(key, 12)
        s = 1.0 / np.sqrt(DIM)
        return {'x1': jax.random.normal(ks[0], (B, N1, DIM), dtype=jnp.float32), 'x2': jax.random.normal(ks[1], (B, N2, DIM), dtype=jnp.float32), 'memory_k': jax.random.normal(ks[2], (B, SLOTS, DIM), dtype=jnp.float32), 'memory_v': jax.random.normal(ks[3], (B, SLOTS, DIM), dtype=jnp.float32), 'Wq': jax.random.normal(ks[4], (DIM, DIM), dtype=jnp.float32) * s, 'bq': jnp.zeros((DIM,), dtype=jnp.float32), 'Wk': jax.random.normal(ks[5], (DIM, DIM), dtype=jnp.float32) * s, 'bk': jnp.zeros((DIM,), dtype=jnp.float32), 'Wv': jax.random.normal(ks[6], (DIM, DIM), dtype=jnp.float32) * s, 'bv': jnp.zeros((DIM,), dtype=jnp.float32), 'Wp': jax.random.normal(ks[7], (DIM, DIM), dtype=jnp.float32) * s, 'bp': jnp.zeros((DIM,), dtype=jnp.float32)}
    _L0_xattn_all = _L0_xattn_setup()
    _L0_xattn_in = {k: v for k, v in _L0_xattn_all.items() if k in ('Wq', 'bq', 'Wk', 'bk', 'Wv', 'bv', 'Wp', 'bp')}
    del _L0_xattn_all

    def _L0_ffn_setup():
        import jax, jax.numpy as jnp
        import numpy as np
        TOP_K = 2
        key = jax.random.key(seed)
        k1, k2, k3, k4 = jax.random.split(key, 4)
        B, S, H, F, E = (2, 256, 128, 352, 8)
        hidden_states = jax.random.normal(k1, (B, S, H), dtype=jnp.float32)
        wqkv = jax.random.normal(k2, (3 * E, H), dtype=jnp.float32) * 0.02
        w1 = jax.random.normal(k3, (E, 2 * F, H), dtype=jnp.float32) * 0.02
        w2 = jax.random.normal(k4, (E, H, F), dtype=jnp.float32) * 0.02
        return {'hidden_states': hidden_states, 'wqkv': wqkv, 'w1': w1, 'w2': w2}
    _L0_ffn_all = _L0_ffn_setup()
    _L0_ffn_in = {k: v for k, v in _L0_ffn_all.items() if k in ('wqkv', 'w1', 'w2')}
    del _L0_ffn_all

    def _L1_xattn_setup():
        import jax, jax.numpy as jnp
        import numpy as np
        D_MODEL = 128
        NUM_HEADS = 16

        def _split_heads(x, num_heads):
            B, S, D = x.shape
            return x.reshape(B, S, num_heads, D // num_heads).transpose(0, 2, 1, 3)
        key = jax.random.key(seed)
        ks = jax.random.split(key, 11)
        B, S, D = (2, 256, D_MODEL)
        s = 1.0 / np.sqrt(D)
        return {'queries': jax.random.normal(ks[0], (B, S, D), jnp.float32), 'keys': jax.random.normal(ks[1], (B, S, D), jnp.float32), 'values': jax.random.normal(ks[2], (B, S, D), jnp.float32), 'W_q': jax.random.normal(ks[3], (D, D), jnp.float32) * s, 'b_q': jnp.zeros((D,), jnp.float32), 'W_k': jax.random.normal(ks[4], (D, D), jnp.float32) * s, 'b_k': jnp.zeros((D,), jnp.float32), 'W_v': jax.random.normal(ks[5], (D, D), jnp.float32) * s, 'b_v': jnp.zeros((D,), jnp.float32), 'W_o': jax.random.normal(ks[6], (D, D), jnp.float32) * s, 'b_o': jnp.zeros((D,), jnp.float32)}
    _L1_xattn_all = _L1_xattn_setup()
    _L1_xattn_in = {k: v for k, v in _L1_xattn_all.items() if k in ('W_q', 'b_q', 'W_k', 'b_k', 'W_v', 'b_v', 'W_o', 'b_o')}
    del _L1_xattn_all

    def _L1_ffn_setup():
        import jax, jax.numpy as jnp
        import numpy as np
        E = 8
        K = 2
        R = 64
        ALPHA = 128.0
        SCALING = ALPHA / R
        key = jax.random.key(seed)
        k0, k1, k2, k3 = jax.random.split(key, 4)
        B, S, D = (4, 512, 128)
        x = jax.random.normal(k0, (B, S, D), jnp.float32)
        Wg = jax.random.normal(k1, (E, D), jnp.float32) * 0.02
        bg = jnp.zeros((E,), jnp.float32)
        W1 = jax.random.normal(k2, (E, R, D), jnp.float32) * (1.0 / np.sqrt(D))
        W2 = jax.random.normal(k3, (E, D, R), jnp.float32) * 0.02
        return {'x': x, 'Wg': Wg, 'bg': bg, 'W1': W1, 'W2': W2}
    _L1_ffn_all = _L1_ffn_setup()
    _L1_ffn_in = {k: v for k, v in _L1_ffn_all.items() if k in ('Wg', 'bg', 'W1', 'W2')}
    del _L1_ffn_all
    return {'x': x, 'fside_BxSxS_0': fside_BxSxS_0, 'ctx_1024': ctx_1024, 'L0_xattn_Wq': _L0_xattn_in['Wq'], 'L0_xattn_bq': _L0_xattn_in['bq'], 'L0_xattn_Wk': _L0_xattn_in['Wk'], 'L0_xattn_bk': _L0_xattn_in['bk'], 'L0_xattn_Wv': _L0_xattn_in['Wv'], 'L0_xattn_bv': _L0_xattn_in['bv'], 'L0_xattn_Wp': _L0_xattn_in['Wp'], 'L0_xattn_bp': _L0_xattn_in['bp'], 'L0_ffn_wqkv': _L0_ffn_in['wqkv'], 'L0_ffn_w1': _L0_ffn_in['w1'], 'L0_ffn_w2': _L0_ffn_in['w2'], 'L1_xattn_W_q': _L1_xattn_in['W_q'], 'L1_xattn_b_q': _L1_xattn_in['b_q'], 'L1_xattn_W_k': _L1_xattn_in['W_k'], 'L1_xattn_b_k': _L1_xattn_in['b_k'], 'L1_xattn_W_v': _L1_xattn_in['W_v'], 'L1_xattn_b_v': _L1_xattn_in['b_v'], 'L1_xattn_W_o': _L1_xattn_in['W_o'], 'L1_xattn_b_o': _L1_xattn_in['b_o'], 'L1_ffn_Wg': _L1_ffn_in['Wg'], 'L1_ffn_bg': _L1_ffn_in['bg'], 'L1_ffn_W1': _L1_ffn_in['W1'], 'L1_ffn_W2': _L1_ffn_in['W2']}

def reference(x, fside_BxSxS_0, ctx_1024, L0_xattn_Wq, L0_xattn_bq, L0_xattn_Wk, L0_xattn_bk, L0_xattn_Wv, L0_xattn_bv, L0_xattn_Wp, L0_xattn_bp, L0_ffn_wqkv, L0_ffn_w1, L0_ffn_w2, L1_xattn_W_q, L1_xattn_b_q, L1_xattn_W_k, L1_xattn_b_k, L1_xattn_W_v, L1_xattn_b_v, L1_xattn_W_o, L1_xattn_b_o, L1_ffn_Wg, L1_ffn_bg, L1_ffn_W1, L1_ffn_W2):
    import jax
    import jax.numpy as jnp

    def _L0_xattn_ref(x1, x2, memory_k, memory_v, Wq, bq, Wk, bk, Wv, bv, Wp, bp):
        import jax, jax.numpy as jnp
        import numpy as np
        DIM = 128
        HEADS = 16
        HEAD_DIM = DIM // HEADS
        B, N1, N2, SLOTS = (8, 128, 128, 64)
        Bn, Nq, C = x1.shape
        H, D = (HEADS, HEAD_DIM)
        scale = D ** (-0.5)
        q = (x1 @ Wq + bq).reshape(Bn, Nq, H, D).transpose(0, 2, 1, 3)
        k = x2 @ Wk + bk
        v = x2 @ Wv + bv
        k = jnp.concatenate([k, memory_k], axis=1)
        v = jnp.concatenate([v, memory_v], axis=1)
        Nkv = k.shape[1]
        k = k.reshape(Bn, Nkv, H, D).transpose(0, 2, 1, 3)
        v = v.reshape(Bn, Nkv, H, D).transpose(0, 2, 1, 3)
        attn = jnp.einsum('bhqd,bhkd->bhqk', q, k) * scale
        attn = jax.nn.softmax(attn, axis=-1)
        out = jnp.einsum('bhqk,bhkd->bhqd', attn, v)
        out = out.transpose(0, 2, 1, 3).reshape(Bn, Nq, C)
        return out @ Wp + bp

    def _L0_ffn_ref(hidden_states, wqkv, w1, w2):
        import jax, jax.numpy as jnp
        import numpy as np
        TOP_K = 2
        b, s, h = hidden_states.shape
        E = w1.shape[0]
        mixed = hidden_states @ wqkv.T
        q, k, v = jnp.split(mixed, 3, axis=-1)
        q = q.astype(jnp.float32)
        k = k.astype(jnp.float32)
        v = v.astype(jnp.float32)
        attn = jax.nn.softmax(q[..., :, None] * k[..., None, :], axis=-1)
        logits = jnp.einsum('bsej,bsj->bse', attn, v).reshape(-1, E)
        top_logits, idx = jax.lax.top_k(logits, TOP_K)
        scores = jax.nn.softmax(top_logits.astype(jnp.float32), axis=-1).astype(hidden_states.dtype)
        N = b * s
        x = hidden_states.reshape(N, h)
        token_ids = jnp.repeat(jnp.arange(N), TOP_K)
        expert_ids = idx.reshape(-1)
        x_rep = x[token_ids]
        out = jnp.zeros_like(x_rep)
        for e in range(E):
            h1 = x_rep @ w1[e].T
            a, g = jnp.split(h1, 2, axis=-1)
            he = jax.nn.silu(a) * g @ w2[e].T
            out = out + jnp.where((expert_ids == e)[:, None], he, jnp.zeros((), out.dtype))
        out = out * scores.reshape(-1, 1)
        combined = out.reshape(N, TOP_K, h).sum(axis=1)
        return combined.reshape(b, s, h)

    def _L1_xattn_ref(queries, keys, values, W_q, b_q, W_k, b_k, W_v, b_v, W_o, b_o):
        import jax, jax.numpy as jnp
        import numpy as np
        D_MODEL = 128
        NUM_HEADS = 16

        def _split_heads(x, num_heads):
            B, S, D = x.shape
            return x.reshape(B, S, num_heads, D // num_heads).transpose(0, 2, 1, 3)
        H = NUM_HEADS
        Q = _split_heads(queries @ W_q.T + b_q, H)
        K = _split_heads(keys @ W_k.T + b_k, H)
        V = _split_heads(values @ W_v.T + b_v, H)
        d = Q.shape[-1]
        scores = jnp.einsum('bhqd,bhkd->bhqk', Q, K) / jnp.sqrt(jnp.asarray(d, Q.dtype))
        attn = jax.nn.softmax(scores, axis=-1)
        out = jnp.einsum('bhqk,bhkd->bhqd', attn, V)
        B, _, S, _ = out.shape
        out = out.transpose(0, 2, 1, 3).reshape(B, S, -1)
        return out @ W_o.T + b_o

    def _L1_ffn_ref(x, Wg, bg, W1, W2):
        import jax, jax.numpy as jnp
        import numpy as np
        E = 8
        K = 2
        R = 64
        ALPHA = 128.0
        SCALING = ALPHA / R
        orig_shape = x.shape
        D = orig_shape[-1]
        xf = x.reshape(-1, D)
        logits = xf @ Wg.T + bg
        top_gates, top_idx = jax.lax.top_k(logits, K)
        top_gates = jax.nn.softmax(top_gates, axis=-1)
        h = jax.nn.gelu(jnp.einsum('nd,erd->enr', xf, W1), approximate=False)
        eout = SCALING * jnp.einsum('enr,edr->ned', h, W2)
        sel = jnp.take_along_axis(eout, top_idx[:, :, None], axis=1)
        out = jnp.sum(top_gates[:, :, None] * sel, axis=1)
        return out.reshape(orig_shape)
    x = x + _L0_xattn_ref(_layernorm(x, axis=-1), fside_BxSxS_0, ctx_1024, ctx_1024, L0_xattn_Wq, L0_xattn_bq, L0_xattn_Wk, L0_xattn_bk, L0_xattn_Wv, L0_xattn_bv, L0_xattn_Wp, L0_xattn_bp)
    x = x + _L0_ffn_ref(_layernorm(x, axis=-1), L0_ffn_wqkv, L0_ffn_w1, L0_ffn_w2)
    x = x + _L1_xattn_ref(_layernorm(x, axis=-1), ctx_1024, ctx_1024, L1_xattn_W_q, L1_xattn_b_q, L1_xattn_W_k, L1_xattn_b_k, L1_xattn_W_v, L1_xattn_b_v, L1_xattn_W_o, L1_xattn_b_o)
    x = x + _L1_ffn_ref(_layernorm(x, axis=-1), L1_ffn_Wg, L1_ffn_bg, L1_ffn_W1, L1_ffn_W2)
    return x

_drawn_inputs = setup_inputs


def setup_inputs(seed=0):
    import zlib

    import numpy as np

    out = dict(_drawn_inputs(seed))
    spreads = {'L0_xattn_bq': (0.0, 0.282),
     'L0_xattn_bk': (0.0, 0.433),
     'L0_xattn_bv': (0.0, 0.1),
     'L0_xattn_bp': (0.0, 0.1),
     'L1_xattn_b_q': (0.0, 0.324),
     'L1_xattn_b_k': (0.0, 0.8),
     'L1_xattn_b_v': (0.0, 0.1),
     'L1_xattn_b_o': (0.0, 0.1),
     'L1_ffn_bg': (0.0, 0.1)}
    factors = {'L0_ffn_wqkv': 6.669, 'L0_ffn_w1': 6.176, 'L0_ffn_w2': 5.792}
    for name, (base, spread) in spreads.items():
        noise = np.random.default_rng([zlib.crc32(name.encode()), seed]).standard_normal(out[name].shape)
        drawn = base * np.exp(spread * noise) if base else spread * noise
        out[name] = jnp.asarray(drawn.astype(out[name].dtype))
    for name, factor in factors.items():
        out[name] = (out[name] * factor).astype(out[name].dtype)
    return out
```

```python
import concourse.bass as bass
from concourse import mybir
from contextlib import ExitStack, contextmanager
import numpy as np

F32 = mybir.dt.float32
BF16 = mybir.dt.bfloat16
I32 = mybir.dt.int32
ACT = mybir.ActivationFunctionType
ALU = mybir.AluOpType
AX = mybir.AxisListType

B, S, D = 64, 128, 128
H, DH = 16, 8
SC = 120
E = 8
GB = 4
NG = B // GB
EPS = 1e-5
ONE_ONE = 0x3F803F80
NPART = 3
TERM_ROWS = NPART * NPART * DH
SHIFT_ROW = 96
STACK_ROWS = SHIFT_ROW + 2
HALF = H // 2


@contextmanager
def phase_semaphores(nc, tag):
    held = []

    def sem(name):
        held.append(nc.alloc_semaphore(tag + name))
        return held[-1]
    yield sem
    nc.clear_and_free_semaphores(held)
    nc.all_engine_barrier()


class Group:

    def __init__(self, pair, par):
        self.pair, self.par = pair, par

    def __add__(self, k):
        t = self.par + k
        return Group(self.pair + t // 2 if t // 2 else self.pair, t % 2)

    @property
    def n(self):
        return self.pair * 2 + self.par

    @property
    def exists(self):
        return not isinstance(self.pair, int) or 0 <= self.n < NG


def wait(eng, sem, value):
    if isinstance(value, int) and value <= 0:
        return
    eng.wait_ge(sem, value)


def wait_apart(eng, sem, value, passed):
    if isinstance(value, int):
        return wait(eng, sem, value)
    eng.wait_ge(sem, value)
    eng.sem_inc(passed, 1)


def run_steps(eng, step):
    for n in (-2, -1, 0, 1):
        step(Group(n // 2, n % 2))
    with eng.Fori(1, NG // 2 - 2) as pair:
        step(Group(pair, 0))
        step(Group(pair, 1))
    for n in range(NG - 4, NG + 1):
        step(Group(n // 2, n % 2))


def attention_layer(nc, x_in, x_out, side, ctx_in, layer, consts):
    first = layer == 0
    KEYS = [S, SC] if first else [SC]
    NT = len(KEYS)
    NK = sum(KEYS)
    HPB = 2 if first else 4
    MT_PER_B = H // HPB
    MT_PER_U = MT_PER_B // 2
    tag = f"L{layer}_"
    ident, ident_bf, wq, wk, wv, wo, bq, bk, bv_bc, bo_bc, half_neg = consts

    q_scr = nc.dram_tensor(tag + "q_parts", (2, GB, NPART, D, S), BF16, kind="Internal").ap()
    k_scr = nc.dram_tensor(tag + "k_parts", (2, GB, NPART, D, NK), BF16, kind="Internal").ap()
    x_v = x_in.rearrange("(n b) s d -> n s b d", b=GB)
    xo_v = x_out.rearrange("(n b) s d -> n s b d", b=GB)
    side_v = side.rearrange("(n b) s d -> n s b d", b=GB)
    ctx_v = ctx_in.rearrange("(n b) s d -> n s b d", b=GB)

    jobs = []
    for u in range(8):
        if u % 2 == 0:
            jobs.append((u, "AT", (u // 2 + 2) % 4))
        s1 = {0: ["XT"], 1: ["QP"], 2: ["FT"], 3: ["KP"], 4: ["CX"] if first else [], 5: ["VP"]}.get(u, [])
        for name in s1:
            jobs.append((u, name, 0))
        if u % 2 == 1:
            jobs.append((u, "OB", ((u - 3) // 2) % 4))
        else:
            jobs.append((u, "OP", (u // 2 + 2) % 4))
            jobs.append((u, "MT", (u // 2 + 3) % 4))
    def job_group(u, name, b):
        if name in ("XT", "QP", "FT", "KP", "CX"):
            return 2
        if name == "VP":
            return 1
        if name in ("AT", "OP"):
            return -1 if u < 4 else 0
        if name == "OB":
            return -1 if u < 3 else 0
        return 1 if u >= 2 else 0
    def job_runs(g, job):
        return (g + job_group(*job)).exists

    NJ = len(jobs)
    peeled = {}
    total = 0
    for n in list(range(-2, NG + 1)):
        peeled[n] = total
        total += sum(job_runs(Group(n // 2, n % 2), j) for j in jobs)
    LOOP0 = 2
    def job_no(g, k):
        if isinstance(g.pair, int):
            return peeled[g.n] + sum(job_runs(g, j) for j in jobs[:k])
        return g.n * NJ + (peeled[LOOP0] - LOOP0 * NJ + k)
    def job_done(gj, name, b=0):
        k = [j[1:] for j in jobs].index((name, b))
        return job_no(gj + -job_group(*jobs[k]), k) + 1 if gj.exists else 0

    with ExitStack() as c:
        sb = lambda name, shape, dt=F32: c.enter_context(nc.sbuf_tensor(tag + name, shape, dt))
        pb = lambda name, shape, dt=F32: c.enter_context(nc.psum_tensor(tag + name, shape, dt))
        sem = c.enter_context(phase_semaphores(nc, tag))
        two = lambda f: [f(0), f(1)]

        x_t = two(lambda p: sb(f"x{p}", [S, GB, D]))
        res_t = two(lambda p: sb(f"res{p}", [S, GB, D]))
        side_t = two(lambda p: sb(f"side{p}", [S, GB, D])) if first else None
        ctx_t = two(lambda p: sb(f"ctx{p}", [SC, GB, D]))
        stats = sb("stats", [S, GB, 6])
        mv = sb("mv", [S, GB, 2])
        rstd = sb("rstd", [S, GB])
        xn = sb("xn", [S, GB, D])
        ctx_o = sb("ctx_o", [SC, GB, D]) if first else None
        xnT = sb("xnT", [D, GB * S])
        srcT = two(lambda p: sb(f"srcT{p}", [D, GB, KEYS[0]]))
        qf = sb("qf", [D, GB, S])
        kf = sb("kf", [D, GB, NK])
        rem = sb("rem", [D, GB, max(NK, S)])
        q_parts = sb("q_parts_sb", [D, GB, NPART, S], BF16)
        k_parts = sb("k_parts_sb", [D, GB, NPART, NK], BF16)
        q_st = two(lambda p: sb(f"q_stack{p}", [STACK_ROWS, GB, H, S], BF16))
        k_st = two(lambda p: sb(f"k_stack{p}", [STACK_ROWS, GB, H, NK], BF16))
        v_t = [two(lambda p: sb(f"v{t}_{p}", [KEYS[t], GB, H, DH + 1])) for t in range(NT)]
        p_t = [two(lambda p: sb(f"p{t}_{p}", [KEYS[t], HALF * S])) for t in range(NT)]
        neg_max = two(lambda p: sb(f"neg_max{p}", [S, H]))
        m_parts = two(lambda p: sb(f"m_parts{p}", [S, 2 * H], BF16))
        mT = two(lambda p: sb(f"mT{p}", [2 * H, S], BF16))
        o_sb = sb("o_sb", [D, 4 * S])
        rden = sb("rden", [S, H])
        att = sb("att", [S, H, DH])
        attT = sb("attT", [D, S])
        out_t = two(lambda p: sb(f"out{p}", [S, GB, D]))

        ps_sc = two(lambda p: pb(f"ps_sc{p}", [S, HALF * S]))
        ps_mx = two(lambda p: pb(f"ps_mx{p}", [S, 512]))
        ps_o = pb("ps_o", [D, 512])
        misc = pb("misc", [D, 512])
        misc_bf = misc[0:2 * H, 0:S // 2].bitcast(BF16)

        x_loaded = two(lambda p: sem(f"x_loaded{p}"))
        res_loaded = two(lambda p: sem(f"res_loaded{p}"))
        side_loaded = two(lambda p: sem(f"side_loaded{p}")) if first else None
        ctx_loaded = two(lambda p: sem(f"ctx_loaded{p}"))
        stored = two(lambda p: sem(f"stored{p}"))
        q_written, k_written = sem("q_written"), sem("k_written")
        st_loaded = [[sem(f"st_loaded{p}{b}") for b in range(GB)] for p in range(2)]
        shift_loaded = [[sem(f"shift_loaded{p}{b}") for b in range(GB)] for p in range(2)]
        aggregated, rstd_ready, normed = sem("aggregated"), sem("rstd_ready"), sem("normed")
        stats_ready, eps_added = sem("stats_ready"), sem("eps_added")
        misc_filled, misc_emptied = sem("misc_filled"), sem("misc_emptied")
        q_split, k_split, v_ctx_ready = sem("q_split"), sem("k_split"), sem("v_ctx_ready")
        res_ready, split_step = sem("res_ready"), sem("split_step")
        q_cleared = sem("q_cleared")
        passed = sem("passed")
        stack_cleared, ctx_ordered = sem("stack_cleared"), sem("ctx_ordered")
        max_filled, max_read = sem("max_filled"), sem("max_read")
        sc_filled, sc_read = sem("sc_filled"), sem("sc_read")
        pv_done, o_read = sem("pv_done"), sem("o_read")
        m_first, m_ready = sem("m_first"), sem("m_ready")
        recip_ready = sem("recip_ready")

        UPS = 8
        sc_no = lambda g, u, t: (g.n * UPS + u) * NT + t
        mx_no = lambda g, b, k: (g.n * GB + b) * MT_PER_B + k
        def prev_unit(g, u):
            return (g, u - 1) if u else (g + -1, UPS - 1)

        def unit_jobs(u):
            return [(k, j) for k, j in enumerate(jobs) if j[0] == u]

        ON_ACT = ("QP", "KP", "CX", "MT", "FT") if first else ("QP", "KP", "MT", "FT", "XT")

        block = c.enter_context(nc.Block())

        @block.sync
        def _(sp):
            def step(g):
                p, g1, g2, g3, gm = g.par, g + 1, g + 2, g + 3, g + -1
                if g.exists:
                    wait_apart(sp, misc_emptied, job_done(g + -2, "OP", GB - 1), passed)
                    sp.dma_start(res_t[p][:], x_v[g.n]).then_inc(res_loaded[p], 16)
                for gl in ([g2, g3] if isinstance(g.pair, int) and g.n == -2 else [g3]):
                    if gl.exists:
                        q = gl.par
                        wait_apart(sp, normed, gl.n - 1, passed)
                        sp.dma_start(x_t[q][:], x_v[gl.n]).then_inc(x_loaded[q], 16)
                        if first:
                            wait_apart(sp, misc_filled, job_done(gl + -2, "FT"), passed)
                            sp.dma_start(side_t[q][:], side_v[gl.n]).then_inc(side_loaded[q], 16)
                            wait_apart(sp, v_ctx_ready, gl.n - 1, passed)
                            wait_apart(sp, ctx_ordered, gl.n - 1, passed)
                        else:
                            wait_apart(sp, misc_filled, job_done(gl + -2, "FT"), passed)
                        sp.dma_start(ctx_t[q][:], ctx_v[gl.n]).then_inc(ctx_loaded[q], 16)
                if gm.exists:
                    wait_apart(sp, misc_emptied, job_done(gm, "OP", GB - 1), passed)
                    sp.dma_start(xo_v[gm.n], out_t[gm.par][:]).then_inc(stored[gm.par], 16)
                if g2.exists:
                    if g.exists:
                        for b in range(GB):
                            wait_apart(sp, st_loaded[p][b], (g.pair + 1) * 16 * (NPART + 1), passed)
                    wait_apart(sp, q_split, g2.n + 1, passed)
                    sp.dma_start(q_scr[p].rearrange("b a r s -> r (b a) s"),
                                 q_parts[:].rearrange("r b a s -> r (b a) s")).then_inc(q_written, 16)
                    wait_apart(sp, k_split, g2.n + 1, passed)
                    sp.dma_start(k_scr[p].rearrange("b a r s -> r (b a) s"),
                                 k_parts[:].rearrange("r b a s -> r (b a) s")).then_inc(k_written, 16)
                    wait_apart(sp, q_written, (g2.n + 1) * 16, passed)
                    wait_apart(sp, k_written, (g2.n + 1) * 16, passed)
                    if isinstance(g.pair, int) and g.n == -2:
                        sp.wait_ge(stack_cleared, 4)
                        sp.wait_ge(q_cleared, 2)
                    for b in range(GB):
                        wait_apart(sp, sc_filled, sc_no(g, 2 * b + 1, NT - 1) + 1 if not isinstance(g.pair, int) or g.n >= 0 else 0, passed)
                        for a in range(NPART):
                            rows = slice(a * NPART * DH, (a + 1) * NPART * DH)
                            sp.dma_start(
                                q_st[p][rows, b].rearrange("r h s -> r (h s)"),
                                q_scr[p, b, a].rearrange("(d h) s -> d (h s)", d=DH).unsqueeze(0)
                                .to_broadcast([NPART, DH, H * S])).then_inc(st_loaded[p][b], 16)
                        sp.dma_start(
                            k_st[p][0:TERM_ROWS, b].rearrange("r h s -> r (h s)"),
                            k_scr[p, b].rearrange("a (d h) s -> (a d) (h s)", d=DH).unsqueeze(0)
                            .to_broadcast([NPART, NPART * DH, H * NK])).then_inc(st_loaded[p][b], 16)
            run_steps(sp, step)
            sp.wait_ge(stored[0], NG // 2 * 16)
            sp.wait_ge(stored[1], NG // 2 * 16)

        @block.gpsimd
        def _(pool):
            def split(src, parts, done):
                n = src.shape[-1]
                r = rem[:, :, 0:n]
                steps = [
                    lambda: nc.gpsimd.tensor_copy(parts[:, :, 0], src),
                    lambda: nc.gpsimd.tensor_tensor(r, src, parts[:, :, 0], ALU.subtract),
                    lambda: nc.gpsimd.tensor_copy(parts[:, :, 1], r),
                ]
                for f in steps:
                    f().then_inc(split_step, 1)
                    split_count[0] = split_count[0] + 1
                    wait_apart(pool, split_step, split_count[0], passed)
                nc.gpsimd.tensor_tensor(parts[:, :, 2], r, parts[:, :, 1], ALU.subtract).then_inc(done, 1)
            split_count = [0]
            for p in range(2):
                for i, (r0, r1, v) in enumerate(((64, SHIFT_ROW, 0), (SHIFT_ROW, STACK_ROWS, ONE_ONE))):
                    nc.gpsimd.memset(k_st[p][r0:r1].rearrange("r b h s -> r (b h s)").bitcast(I32), v).then_inc(stack_cleared, 1)
                    pool.wait_ge(stack_cleared, 2 * p + i + 1)

            def step(g):
                g1, g2 = g + 1, g + 2
                if g2.exists:
                    wait_apart(pool, aggregated, g2.n + 1, passed)
                    nc.gpsimd.tensor_scalar(rstd[:], mv[:, :, 1], EPS, None, ALU.add).then_inc(eps_added, 1)
                    wait_apart(pool, eps_added, g2.n + 1, passed)
                    nc.gpsimd.tensor_tensor(rstd[:], rstd[:], half_neg[:], ALU.pow).then_inc(rstd_ready, 1)
                if g.exists:
                    wait_apart(pool, res_loaded[g.par], (g.pair + 1) * 16, passed)
                    r = res_t[g.par]
                    nc.gpsimd.tensor_tensor(r[:], r[:], bo_bc[:].unsqueeze(1).to_broadcast([S, GB, D]),
                                            ALU.add).then_inc(res_ready, 1)
                if g1.exists:
                    if first:
                        wait_apart(pool, pv_done, (g1.n - 1) * UPS, passed)
                        wait_apart(pool, ctx_loaded[g1.par], (g1.pair + 1) * 16, passed)
                        nc.gpsimd.tensor_copy(
                            v_t[1][g1.par][:, :, :, 0:DH],
                            ctx_t[g1.par][:].rearrange("s b (h d) -> s b h d", d=DH)).then_inc(v_ctx_ready, 1)
                if g2.exists:
                    split_count[0] = g2.n * 6
                    wait_apart(pool, q_written, g2.n * 16, passed)
                    wait_apart(pool, k_split, g2.n, passed)
                    wait_apart(pool, misc_emptied, job_done(g2, "QP"), passed)
                    split(qf[:], q_parts, q_split)
                    wait_apart(pool, k_written, g2.n * 16, passed)
                    wait_apart(pool, misc_emptied, job_done(g2, "CX" if first else "KP"), passed)
                    wait_apart(pool, q_split, g2.n + 1, passed)
                    split(kf[:], k_parts, k_split)
            run_steps(pool, step)

        @block.scalar
        def _(act):
            def evac(g, k, job):
                u, name, b = job
                gj = g + job_group(*job)
                act.wait_ge(misc_filled, job_no(g, k) + 1)
                if name == "XT":
                    ins = nc.scalar.copy(xnT[:], misc[:])
                elif name == "QP":
                    wait(act, q_split, gj.n)
                    ins = nc.scalar.activation(qf[:], misc[:], ACT.Identity, bias=bq[:], scale=float(DH) ** -0.5)
                elif name == "FT":
                    ins = nc.scalar.copy(srcT[gj.par][:], misc[:, 0:GB * KEYS[0]])
                elif name == "KP":
                    wait(act, k_split, gj.n)
                    ins = nc.scalar.activation(kf[:, :, 0:KEYS[0]], misc[:, 0:GB * KEYS[0]].rearrange("r (b s) -> r b s", b=GB),
                                               ACT.Identity, bias=bk[:], scale=1.0)
                elif name == "CX":
                    ins = nc.scalar.copy(kf[:, :, S:], misc[:, 0:GB * SC].rearrange("r (b s) -> r b s", b=GB))
                elif name == "MT":
                    q = b % 2
                    gw, bw = (gj, b - 2) if b >= 2 else (gj + -1, b + 2)
                    if gw.exists:
                        act.wait_ge(shift_loaded[gw.par][bw], (gw.pair + 1) * 32)
                    ins = nc.scalar.copy(mT[q][:], misc_bf)
                ins.then_inc(misc_emptied, 1)
                if name == "MT":
                    act.wait_ge(misc_emptied, job_no(g, k) + 1)
                    for r in range(2):
                        act.dma_start(q_st[gj.par][SHIFT_ROW + r:SHIFT_ROW + r + 1, b],
                                      mT[b % 2][r * H:(r + 1) * H, :]).then_inc(shift_loaded[gj.par][b], 16)

            def step(g):
                for u in range(UPS):
                    uj = [(k, j) for k, j in unit_jobs(u) if job_runs(g, j) and j[1] in ON_ACT]
                    if g.exists:
                        for t in range(NT):
                            i = sc_no(g, u, t)
                            act.wait_ge(sc_filled, i + 1)
                            wait(act, pv_done, g.n * UPS + u - 1)
                            nc.scalar.activation(p_t[t][u % 2][:], ps_sc[(u * NT + t) % 2][0:KEYS[t], :],
                                                 ACT.Exp).then_inc(sc_read, 1)
                    gp, up = prev_unit(g, u)
                    if u % 2 == 0 and gp.exists:
                        act.wait_ge(pv_done, gp.n * UPS + up + 1)
                        wait(act, recip_ready, gp.n * GB + up // 2)
                        nc.scalar.copy(o_sb[:], ps_o[:]).then_inc(o_read, 1)
                    if first and u == 1 and (g + 2).exists:
                        g2 = g + 2
                        act.wait_ge(ctx_loaded[g2.par], (g2.pair + 1) * 16)
                        wait(act, misc_filled, job_done(g + 1, "CX"))
                        for b in range(GB):
                            last = nc.scalar.copy(ctx_o[:, b].rearrange("s (d h) -> s d h", d=DH),
                                                  ctx_t[g2.par][:, b].rearrange("s (h d) -> s d h", d=DH))
                        last.then_inc(ctx_ordered, 1)
                    for k, j in uj:
                        evac(g, k, j)
            run_steps(act, step)

        @block.vector
        def _(dve):
            for p in range(2):
                nc.vector.memset(q_st[p][64:SHIFT_ROW].rearrange("r b h s -> r (b h s)").bitcast(I32), 0).then_inc(q_cleared, 1)
                for t in range(NT):
                    nc.vector.memset(v_t[t][p][:, :, :, DH:DH + 1], 1.0)
            nc.vector.memset(ps_o[:], 0.0).then_inc(o_read, 1)

            def evac(g, k, job):
                u, name, b = job
                gj = g + job_group(*job)
                dve.wait_ge(misc_filled, job_no(g, k) + 1)
                if name == "XT":
                    nc.vector.tensor_copy(xnT[:], misc[:]).then_inc(misc_emptied, 1)
                elif name == "VP":
                    n = KEYS[0]
                    wait(dve, pv_done, (gj.n - 1) * UPS)
                    nc.vector.tensor_tensor(
                        v_t[0][gj.par][:, :, :, 0:DH],
                        misc[0:n, :].rearrange("s (b h d) -> s b h d", b=GB, d=DH),
                        bv_bc[0:n].rearrange("s (h d) -> s h d", d=DH).unsqueeze(1).to_broadcast([n, GB, H, DH]),
                        ALU.add).then_inc(misc_emptied, 1)
                elif name == "OB":
                    o_v = misc[:].rearrange("q (h c) -> q h c", c=32)
                    nc.vector.reciprocal(rden[:], o_v[:, :, DH]).then_inc(recip_ready, 1)
                    dve.wait_ge(recip_ready, gj.n * GB + b + 1)
                    nc.vector.tensor_tensor(att[:], o_v[:, :, 0:DH], rden[:].unsqueeze(2).to_broadcast([S, H, DH]),
                                            ALU.mult).then_inc(misc_emptied, 1)
                elif name == "AT":
                    nc.vector.tensor_copy(attT[:], misc[:, 0:S]).then_inc(misc_emptied, 1)
                elif name == "OP":
                    if b == 0:
                        dve.wait_ge(res_ready, gj.n + 1)
                        wait(dve, stored[gj.par], gj.pair * 16)
                    nc.vector.tensor_tensor(out_t[gj.par][:, b], misc[:, 0:D], res_t[gj.par][:, b],
                                            ALU.add).then_inc(misc_emptied, 1)

            def step(g):
                g1, g2 = g + 1, g + 2
                if g2.exists:
                    dve.wait_ge(x_loaded[g2.par], (g2.pair + 1) * 16)
                    for b in range(GB):
                        nc.vector.bn_stats(stats[:, b], x_t[g2.par][:, b]).then_inc(stats_ready, 1)
                    wait_apart(dve, stats_ready, (g2.n + 1) * GB, passed)
                    for b in range(GB):
                        last = nc.vector.bn_aggr(mv[:, b], stats[:, b])
                    last.then_inc(aggregated, 1)
                    dve.wait_ge(rstd_ready, g2.n + 1)
                    wait(dve, misc_filled, job_done(g1, "XT"))
                    for b in range(GB):
                        last = nc.vector.tensor_scalar(xn[:, b], x_t[g2.par][:, b], mv[:, b, 0:1], rstd[:, b:b + 1],
                                                       ALU.subtract, ALU.mult)
                    last.then_inc(normed, 1)
                for u in range(UPS):
                    uj = [(k, j) for k, j in unit_jobs(u) if job_runs(g, j) and j[1] not in ON_ACT]
                    for k, j in uj:
                        if j[1] == "AT":
                            evac(g, k, j)
                    if g1.exists:
                        b = u // 2
                        for k in range(MT_PER_U):
                            kk = (u % 2) * MT_PER_U + k
                            i = mx_no(g1, b, kk)
                            dve.wait_ge(max_filled, i + 1)
                            v = ps_mx[kk % 2][:, 0:HPB * NK].rearrange("q (h s) -> q h s", h=HPB)
                            nc.vector.tensor_reduce(neg_max[b % 2][:, kk * HPB:(kk + 1) * HPB], v, AX.X, ALU.max,
                                                    negate=True).then_inc(max_read, 1)
                        if u % 2 == 1:
                            dve.wait_ge(max_read, mx_no(g1, b, MT_PER_B - 1) + 1)
                            wait(dve, misc_filled, job_done(g1, "MT", b - 2) if b >= 2 else job_done(g, "MT", b + 2))
                            mp = m_parts[b % 2]
                            i = g1.n * GB + b + 1
                            nc.vector.tensor_copy(mp[:, 0:H], neg_max[b % 2][:]).then_inc(m_first, 1)
                            dve.wait_ge(m_first, i)
                            nc.vector.tensor_tensor(mp[:, H:2 * H], neg_max[b % 2][:], mp[:, 0:H],
                                                    ALU.subtract).then_inc(m_ready, 1)
                    for k, j in uj:
                        if j[1] != "AT":
                            evac(g, k, j)
            run_steps(dve, step)

        @block.tensor
        def _(pe):
            mm = nc.tensor.matmul

            def fill(g, k, job):
                u, name, b = job
                gj = g + job_group(*job)
                wait(pe, misc_emptied, job_no(g, k))
                if name == "XT":
                    pe.wait_ge(normed, gj.n + 1)
                    for j in range(GB):
                        last = nc.tensor.transpose(misc[:, j * S:(j + 1) * S], xn[:, j], ident[:])
                elif name == "QP":
                    last = mm(misc[:], wq[:], xnT[:], start=True, stop=True)
                elif name == "FT":
                    n = KEYS[0]
                    if first:
                        pe.wait_ge(side_loaded[gj.par], (gj.pair + 1) * 16)
                    else:
                        pe.wait_ge(ctx_loaded[gj.par], (gj.pair + 1) * 16)
                    src = side_t if first else ctx_t
                    for j in range(GB):
                        last = nc.tensor.transpose(misc[:, j * n:(j + 1) * n], src[gj.par][:, j], ident[0:n, 0:n])
                elif name == "KP":
                    n = GB * KEYS[0]
                    last = mm(misc[:, 0:n], wk[:], srcT[gj.par][:].rearrange("d b s -> d (b s)"), start=True, stop=True)
                elif name == "CX":
                    pe.wait_ge(ctx_ordered, gj.n + 1)
                    for j in range(GB):
                        last = nc.tensor.transpose(misc[:, j * SC:(j + 1) * SC], ctx_o[:, j], ident[0:SC, 0:SC])
                elif name == "VP":
                    n = KEYS[0]
                    for j in range(GB):
                        last = mm(misc[0:n, j * D:(j + 1) * D], srcT[gj.par][:, j], wv[:], start=True, stop=True)
                elif name == "MT":
                    pe.wait_ge(m_ready, gj.n * GB + b + 1)
                    last = nc.tensor.transpose(misc_bf, m_parts[b % 2][:], ident_bf[:])
                elif name == "OB":
                    pe.wait_ge(o_read, gj.n * GB + b + 2)
                    for j in range(4):
                        last = nc.tensor.transpose(misc[:, j * S:(j + 1) * S], o_sb[:, j * S:(j + 1) * S], ident[:])
                elif name == "AT":
                    last = nc.tensor.transpose(misc[:, 0:S], att[:].rearrange("q h d -> q (h d)"), ident[:])
                elif name == "OP":
                    last = mm(misc[:, 0:D], attT[:], wo[:], start=True, stop=True)
                last.then_inc(misc_filled, 1)

            def scores(g, u, t):
                b, hf, p = u // 2, u % 2, g.par
                i = sc_no(g, u, t)
                if t == 0 and hf == 0:
                    pe.wait_ge(shift_loaded[p][b], (g.pair + 1) * 32)
                wait(pe, sc_read, i - 1)
                k0 = sum(KEYS[:t])
                out = ps_sc[(u * NT + t) % 2]
                for j in range(HALF):
                    h = hf * HALF + j
                    last = mm(out[0:KEYS[t], j * S:(j + 1) * S], k_st[p][:, b, h, k0:k0 + KEYS[t]], q_st[p][:, b, h, :],
                              start=True, stop=True)
                last.then_inc(sc_filled, 1)

            def max_tile(g, b, k):
                p = g.par
                i = mx_no(g, b, k)
                if k == 0:
                    pe.wait_ge(st_loaded[p][b], (g.pair + 1) * 16 * (NPART + 1))
                wait(pe, max_read, i - 1)
                for j in range(HPB):
                    h = k * HPB + j
                    last = mm(ps_mx[k % 2][:, j * NK:(j + 1) * NK], q_st[p][0:SHIFT_ROW, b, h, :],
                              k_st[p][0:SHIFT_ROW, b, h, :], start=True, stop=True)
                last.then_inc(max_filled, 1)

            def weighted_values(g, u):
                b, hf, p = u // 2, u % 2, g.par
                if u == 0:
                    pe.wait_ge(misc_emptied, job_done(g, "VP"))
                    if first:
                        pe.wait_ge(v_ctx_ready, g.n + 1)
                pe.wait_ge(sc_read, sc_no(g, u, NT - 1) + 1)
                if hf == 0:
                    pe.wait_ge(o_read, g.n * GB + b + 1)
                for q0 in range(0, HALF, 4):
                    for t in range(NT):
                        for j in range(q0, q0 + 4):
                            h = hf * HALF + j
                            r, col = 32 * (h % 4), (h // 4) * S
                            last = mm(ps_o[r:r + DH + 1, col:col + S], v_t[t][p][:, b, h, :],
                                      p_t[t][u % 2][:, j * S:(j + 1) * S], start=(t == 0), stop=(t == NT - 1))
                last.then_inc(pv_done, 1)

            def step(g):
                g1 = g + 1
                for u in range(UPS):
                    uj = [(k, j) for k, j in unit_jobs(u) if job_runs(g, j)]
                    tiles = list(range((u % 2) * MT_PER_U, (u % 2 + 1) * MT_PER_U))
                    if uj and uj[0][1][1] == "AT":
                        fill(g, *uj.pop(0))
                    for t in range(NT):
                        if g.exists:
                            scores(g, u, t)
                        if g1.exists:
                            for k in tiles[t * MT_PER_U // NT:(t + 1) * MT_PER_U // NT]:
                                max_tile(g1, u // 2, k)
                    gp, up = prev_unit(g, u)
                    if gp.exists:
                        weighted_values(gp, up)
                    for k, j in uj:
                        fill(g, k, j)
            run_steps(pe, step)


def diagonal(nc, pool, t, cleared, done):
    nc.gpsimd.memset(t[:], 0.0).then_inc(cleared, 1)
    pool.wait_ge(cleared, 1)
    nc.gpsimd.affine_select(out=t[:], in_=t[:], compare_op=ALU.not_equal, fill=1.0, base=0,
                            pattern=[[-1, t.shape[-1]]], channel_multiplier=1).then_inc(done, 1)


def attention_consts(nc, c, weights, layer):
    Wq, bq_d, Wk, bk_d, Wv, bv_d, Wo, bo_d = weights
    first = layer == 0
    tag = f"C{layer}_"
    sb = lambda name, shape, dt=F32: c.enter_context(nc.sbuf_tensor(tag + name, shape, dt))
    ident, ident_bf = sb("ident", [128, 128]), sb("ident_bf", [128, 128], BF16)
    ready = [sb(n, [D, D]) for n in ("wq", "wk", "wv", "wo")]
    bq, bk = sb("bq", [D, 1]), sb("bk", [D, 1])
    bv_bc, bo_bc, half_neg = sb("bv_bc", [S, D]), sb("bo_bc", [S, D]), sb("half_neg", [S, GB])
    with ExitStack() as p:
        raw = [p.enter_context(nc.sbuf_tensor(tag + "raw_" + n, [D, D], F32)) for n in "qkvo"]
        bq_raw = p.enter_context(nc.sbuf_tensor(tag + "bq_raw", [D, 1], F32))
        ps = p.enter_context(nc.psum_tensor(tag + "ps", [D, 4, D], F32))
        sem = p.enter_context(phase_semaphores(nc, tag))
        loaded, cleared, made, turned, done = (sem(n) for n in
                                               ("loaded", "cleared", "made", "turned", "done"))
        block = p.enter_context(nc.Block())

        @block.sync
        def _(sp):
            for t, w in zip(raw, (Wq, Wk, Wv, Wo)):
                sp.dma_start(t[:], w).then_inc(loaded, 16)
            for t, w in ((bq_raw, bq_d), (bk, bk_d)):
                for d in range(DH):
                    sp.dma_start(t[d * H:(d + 1) * H, :], w.rearrange("(h d one) -> d h one", d=DH, one=1)[d],
                                 allow_slow_non_contiguous=True).then_inc(loaded, 16)
            for t, w in ((bv_bc, bv_d), (bo_bc, bo_d)):
                sp.dma_start(t[:], w.unsqueeze(0).to_broadcast([S, D])).then_inc(loaded, 16)

        @block.gpsimd
        def _(pool):
            nc.gpsimd.memset(half_neg[:], -0.5)
            diagonal(nc, pool, ident, cleared, made)

        @block.tensor
        def _(pe):
            pe.wait_ge(loaded, 16 * 22)
            pe.wait_ge(made, 1)
            if not first:
                for i in range(4):
                    last = nc.tensor.transpose(ps[:, i], raw[i][:], ident[:])
                last.then_inc(turned, 1)

        @block.vector
        def _(dve):
            dve.wait_ge(loaded, 16 * 22)
            dve.wait_ge(made, 1)
            nc.vector.tensor_copy(ident_bf[:], ident[:])
            nc.vector.tensor_scalar(bq[:], bq_raw[:], float(DH) ** -0.5, None, ALU.mult)
            if not first:
                dve.wait_ge(turned, 1)
            for i in range(4):
                src = raw[i][:] if first else ps[:, i]
                if i < 2:
                    src = src.rearrange("r (h d) -> r d h", d=DH)
                    last = nc.vector.tensor_copy(ready[i][:].rearrange("r (d h) -> r d h", d=DH), src)
                else:
                    last = nc.vector.tensor_copy(ready[i][:], src)
            last.then_inc(done, 1)
            dve.wait_ge(done, 1)
    return (ident, ident_bf, *ready, bq, bk, bv_bc, bo_bc, half_neg)


TOKENS = B * S
F = 352
TOP = 2
REGION = TOKENS + S
TILES = (TOKENS * TOP // S + E) // 2 * 2
SPARE = E * REGION
ROUTED_ROWS = SPARE + E * S
FCHUNKS = [(0, 128), (128, 128), (256, F - 256)]
G_STEPS = 2 * NPART


def loop_groups(eng, step, lead):
    for n in range(-2, 2):
        step(Group(n // 2, n % 2))
    with eng.Fori(1, NG // 2 - 1) as pair:
        step(Group(pair, 0))
        step(Group(pair, 1))
    for n in range(NG - 2, NG + 2):
        step(Group(n // 2, n % 2))


def route_tokens(nc, x1, xs, wqkv, keep):
    slots_all, gates_all, tile_row, tile_expert = keep
    x_v = x1.rearrange("(n b) s d -> n s b d", b=GB)
    with ExitStack() as c:
        sb = lambda name, shape, dt=F32: c.enter_context(nc.sbuf_tensor("R_" + name, shape, dt))
        pb = lambda name, shape, dt=F32: c.enter_context(nc.psum_tensor("R_" + name, shape, dt))
        sem = c.enter_context(phase_semaphores(nc, "R_"))
        two = lambda f: [f(0), f(1)]
        ident = sb("ident", [128, 128])
        before, ones = sb("before", [128, 128], BF16), sb("ones", [128, 128], BF16)
        zeros = sb("zeros", [128, D])
        half_neg = sb("half_neg", [S, GB])
        iota_e, iota_ei = sb("iota_e", [S, E]), sb("iota_ei", [S, E], I32)
        iota_t, iota_ti = sb("iota_t", [1, TILES]), sb("iota_ti", [1, TILES], I32)
        w_raw, wT = sb("w_raw", [3 * E, D]), sb("wT", [D, 3 * E])
        x_t = two(lambda p: sb(f"x{p}", [S, GB, D]))
        xn = two(lambda p: sb(f"xn{p}", [S, GB, D]))
        stats, mv, rstd = sb("stats", [S, GB, 6]), sb("mv", [S, GB, 2]), sb("rstd", [S, GB])
        xnT = sb("xnT", [D, GB, S])
        qkv = sb("qkv", [S, GB, 3 * E])
        pr, prv, pe_ = (sb(n, [S, GB, E, E]) for n in ("pr", "prv", "pexp"))
        mx, sm, lv, lg = (sb(n, [S, GB, E]) for n in ("mx", "sm", "lv", "lg"))
        top, top_i = sb("top", [S, GB, 8]), sb("top_i", [S, GB, 8], mybir.dt.uint32)
        idx_f, diff, e2, den = sb("idx_f", [S, GB, TOP]), sb("diff", [S, GB]), sb("e2", [S, GB]), sb("den", [S, GB])
        g0 = sb("g0", [S, GB])
        oh, ohp = sb("oh", [S, GB, TOP, E]), sb("ohp", [S, GB, TOP, E])
        hits = sb("hits", [S, GB, E], BF16)
        base, pos = sb("base", [S, GB, E]), sb("pos", [S, GB, E])
        count, region0 = sb("count", [S, E]), sb("region0", [S, E])
        slot_f = sb("slot_f", [S, GB, TOP])
        slots_f, crossed = sb("slots_f", [S, NG * GB * TOP]), sb("crossed", [S, NG * GB * TOP, E - 1])
        moved = sb("moved", [S, NG * GB * TOP])
        slot = two(lambda p: sb(f"slot{p}", [S, GB, TOP], mybir.dt.uint32))
        nf, ni, nt_i, ntf, te, delta = (sb(n, [S, E], dt) for n, dt in
            (("nf", F32), ("ni", I32), ("nt_i", I32), ("ntf", F32), ("te", F32), ("delta", F32)))
        end_row = sb("end_row", [1, E], I32)
        tmask, tm2 = sb("tmask", [1, TILES, E]), sb("tm2", [1, TILES, E])
        tef, trf = sb("tef", [1, TILES]), sb("trf", [1, TILES])
        ps_x, ps_q, ps_r = pb("ps_x", [D, GB, S]), pb("ps_q", [S, GB, 3 * E]), pb("ps_r", [S, 2, GB, E])

        w_loaded, made, cleared, consts_ready = sem("w_loaded"), sem("made"), sem("cleared"), sem("consts_ready")
        x_loaded = two(lambda p: sem(f"x_loaded{p}"))
        stats_ready, aggregated, rstd_ready, eps_added, normed = (sem(n) for n in
            ("stats_ready", "aggregated", "rstd_ready", "eps_added", "normed"))
        w_turned, wT_ready = sem("w_turned"), sem("wT_ready")
        x_turned, xT_ready, projected, qkv_ready = sem("x_turned"), sem("xT_ready"), sem("projected"), sem("qkv_ready")
        shifted, exp_ready, gap_ready, e2_ready = sem("shifted"), sem("exp_ready"), sem("gap_ready"), sem("e2_ready")
        hits_ready, counted, order = sem("hits_ready"), sem("counted"), sem("order")
        slot_ready = sem("slot_ready")
        scattered = two(lambda p: sem(f"scattered{p}"))
        table_ready, zeroed, passed = sem("table_ready"), sem("zeroed"), sem("passed")
        ORDER = 21

        block = c.enter_context(nc.Block())

        @block.sync
        def _(sp):
            sp.dma_start(w_raw[:], wqkv).then_inc(w_loaded, 16)

            def step(g):
                gl = g + 2
                if gl.exists:
                    wait_apart(sp, normed, gl.n - 1, passed)
                    sp.dma_start(x_t[gl.par][:], x_v[gl.n]).then_inc(x_loaded[gl.par], 16)
            loop_groups(sp, step, 2)
            sp.wait_ge(made, 3)
            for k in range(E):
                sp.dma_start(xs[SPARE + k * S:SPARE + (k + 1) * S], zeros[:]).then_inc(zeroed, 16)
            sp.wait_ge(table_ready, 1)
            for e in range(E):
                row = sp.value_load(end_row[0:1, e:e + 1], min_val=e * REGION, max_val=e * REGION + TOKENS)
                sp.dma_start(xs[bass.ds(row, S)], zeros[:]).then_inc(zeroed, 16)
            sp.wait_ge(zeroed, 2 * E * 16)

        @block.gpsimd
        def _(pool):
            n = [0]

            def done(ins):
                n[0] += 1
                ins.then_inc(cleared, 1)
                pool.wait_ge(cleared, n[0])
            done(nc.gpsimd.memset(half_neg[:], -0.5))
            done(nc.gpsimd.memset(ident[:], 0.0))
            nc.gpsimd.affine_select(out=ident[:], in_=ident[:], compare_op=ALU.not_equal, fill=1.0, base=0,
                                    pattern=[[-1, 128]], channel_multiplier=1).then_inc(made, 1)
            done(nc.gpsimd.memset(ones[:], 1.0))
            nc.gpsimd.affine_select(out=before[:], in_=ones[:], compare_op=ALU.is_gt, fill=0.0, base=0,
                                    pattern=[[1, 128]], channel_multiplier=-1).then_inc(made, 1)
            nc.gpsimd.memset(zeros[:], 0.0).then_inc(made, 1)
            done(nc.gpsimd.iota(iota_ei[:], pattern=[[1, E]], base=0, channel_multiplier=0))
            done(nc.gpsimd.iota(iota_ti[:], pattern=[[1, TILES]], base=0, channel_multiplier=0))
            done(nc.gpsimd.tensor_copy(iota_e[:], iota_ei[:]))
            done(nc.gpsimd.tensor_copy(iota_t[:], iota_ti[:]))
            done(nc.gpsimd.tensor_scalar(region0[:], iota_e[:], float(REGION), None, ALU.mult))
            nc.gpsimd.tensor_copy(count[:], region0[:]).then_inc(consts_ready, 1)

            def step(g):
                g1 = g + 1
                if g1.exists:
                    wait_apart(pool, aggregated, g1.n + 1, passed)
                    nc.gpsimd.tensor_scalar(rstd[:], mv[:, :, 1], EPS, None, ALU.add).then_inc(eps_added, 1)
                    wait_apart(pool, eps_added, g1.n + 1, passed)
                    nc.gpsimd.tensor_tensor(rstd[:], rstd[:], half_neg[:], ALU.pow).then_inc(rstd_ready, 1)
                if g.exists:
                    wait_apart(pool, slot_ready, g.n + 1, passed)
                    for b in range(GB):
                        for k in range(TOP):
                            nc.gpsimd.indirect_dma_start(
                                out=xs, out_offset=bass.IndirectOffsetOnAxis(ap=slot[g.par][:, b, k:k + 1], axis=0),
                                in_=xn[g.par][:, b], in_offset=None).then_inc(scattered[g.par], 16)
            loop_groups(pool, step, 1)
            for p in range(2):
                pool.wait_ge(scattered[p], NG // 2 * GB * TOP * 16)

        @block.tensor
        def _(pe):
            pe.wait_ge(w_loaded, 16)
            pe.wait_ge(made, 3)
            nc.tensor.transpose(ps_x[:, 0, 0:3 * E], w_raw[:], ident[0:3 * E, 0:3 * E]).then_inc(w_turned, 1)
            pe.wait_ge(wT_ready, 1)

            def step(g):
                g1 = g + 1
                if g1.exists:
                    wait(pe, normed, g1.n + 1)
                    wait(pe, xT_ready, g1.n)
                    for b in range(GB):
                        last = nc.tensor.transpose(ps_x[:, b], xn[g1.par][:, b], ident[:])
                    last.then_inc(x_turned, 1)
                    pe.wait_ge(xT_ready, g1.n + 1)
                    wait(pe, qkv_ready, g1.n)
                    for b in range(GB):
                        last = nc.tensor.matmul(ps_q[:, b], xnT[:, b], wT[:], start=True, stop=True)
                    last.then_inc(projected, 1)
                if g.exists:
                    pe.wait_ge(hits_ready, g.n + 1)
                    h = hits[:].rearrange("s b e -> s (b e)")
                    nc.tensor.matmul(ps_r[:, 0].rearrange("s b e -> s (b e)"), before[:], h, start=True, stop=True)
                    nc.tensor.matmul(ps_r[:, 1].rearrange("s b e -> s (b e)"), ones[:], h,
                                     start=True, stop=True).then_inc(counted, 1)
            loop_groups(pe, step, 1)

        @block.scalar
        def _(act):
            act.wait_ge(w_turned, 1)
            nc.scalar.copy(wT[:], ps_x[:, 0, 0:3 * E]).then_inc(wT_ready, 1)

            def ordered(g):
                g1 = g + 1
                if g.exists:
                    act.wait_ge(shifted, g.n + 1)
                    nc.scalar.activation(pe_[:], pr[:], ACT.Exp).then_inc(exp_ready, 1)
                    act.wait_ge(gap_ready, g.n + 1)
                    nc.scalar.activation(e2[:], diff[:], ACT.Exp).then_inc(e2_ready, 1)
                if g1.exists:
                    act.wait_ge(x_turned, g1.n + 1)
                    wait(act, projected, g1.n)
                    nc.scalar.copy(xnT[:], ps_x[:]).then_inc(xT_ready, 1)
                    act.wait_ge(projected, g1.n + 1)
                    nc.scalar.copy(qkv[:], ps_q[:]).then_inc(qkv_ready, 1)
            loop_groups(act, ordered, 1)

        @block.vector
        def _(dve):
            v = nc.vector
            dve.wait_ge(consts_ready, 1)

            def step(g):
                g1 = g + 1
                if g1.exists:
                    wait_apart(dve, x_loaded[g1.par], (g1.pair + 1) * 16, passed)
                    for b in range(GB):
                        v.bn_stats(stats[:, b], x_t[g1.par][:, b]).then_inc(stats_ready, 1)
                    wait_apart(dve, stats_ready, (g1.n + 1) * GB, passed)
                    for b in range(GB):
                        last = v.bn_aggr(mv[:, b], stats[:, b])
                    last.then_inc(aggregated, 1)
                    wait_apart(dve, rstd_ready, g1.n + 1, passed)
                    wait_apart(dve, scattered[g1.par], g1.pair * GB * TOP * 16, passed)
                    for b in range(GB):
                        last = v.tensor_scalar(xn[g1.par][:, b], x_t[g1.par][:, b], mv[:, b, 0:1], rstd[:, b:b + 1],
                                               ALU.subtract, ALU.mult)
                    last.then_inc(normed, 1)
                if not g.exists:
                    return
                links = [0]

                def link(ins):
                    links[0] += 1
                    ins.then_inc(order, 1)
                    wait_apart(dve, order, g.n * ORDER + links[0], passed)
                full = [S, GB, E, E]
                q, k, val = (qkv[:, :, i * E:(i + 1) * E] for i in range(3))
                wait_apart(dve, qkv_ready, g.n + 1, passed)
                link(v.tensor_tensor(pr[:], q.unsqueeze(3).to_broadcast(full), k.unsqueeze(2).to_broadcast(full), ALU.mult))
                link(v.tensor_reduce(mx[:], pr[:], AX.X, ALU.max))
                v.tensor_tensor(pr[:], pr[:], mx[:].unsqueeze(3).to_broadcast(full), ALU.subtract).then_inc(shifted, 1)
                wait_apart(dve, exp_ready, g.n + 1, passed)
                v.tensor_reduce(sm[:], pe_[:], AX.X, ALU.add)
                link(v.tensor_tensor(prv[:], pe_[:], val.unsqueeze(2).to_broadcast(full), ALU.mult))
                link(v.tensor_reduce(lv[:], prv[:], AX.X, ALU.add))
                link(v.reciprocal(sm[:], sm[:]))
                link(v.tensor_tensor(lg[:], lv[:], sm[:], ALU.mult))
                for b in range(GB):
                    last = v.max(top[:, b], lg[:, b])
                link(last)
                for b in range(GB):
                    last = v.max_index(top_i[:, b], top[:, b], lg[:, b])
                link(last)
                v.tensor_tensor(diff[:], top[:, :, 1], top[:, :, 0], ALU.subtract).then_inc(gap_ready, 1)
                link(v.tensor_copy(idx_f[:], top_i[:, :, 0:TOP]))
                picks = [S, GB, TOP, E]
                link(v.tensor_tensor(oh[:], iota_e[:].unsqueeze(1).unsqueeze(1).to_broadcast(picks),
                                     idx_f[:].unsqueeze(3).to_broadcast(picks), ALU.is_equal))
                v.tensor_tensor(hits[:], oh[:, :, 0], oh[:, :, 1], ALU.add).then_inc(hits_ready, 1)
                wait_apart(dve, e2_ready, g.n + 1, passed)
                link(v.tensor_scalar(den[:], e2[:], 1.0, None, ALU.add))
                link(v.reciprocal(g0[:], den[:]))
                ga = gates_all[:, bass.ds(g.n, 1)] if not isinstance(g.pair, int) else gates_all[:, g.n:g.n + 1]
                sa = slots_f[:, bass.ds(g.n * (GB * TOP), GB * TOP)]
                v.tensor_copy(ga[:, 0, :, 0], g0[:])
                v.tensor_tensor(ga[:, 0, :, 1], e2[:], g0[:], ALU.mult)
                wait_apart(dve, counted, g.n + 1, passed)
                link(v.tensor_copy(base[:, 0], count[:]))
                for b in range(GB - 1):
                    link(v.tensor_tensor(base[:, b + 1], base[:, b], ps_r[:, 1, b], ALU.add))
                v.tensor_tensor(count[:], base[:, GB - 1], ps_r[:, 1, GB - 1], ALU.add)
                link(v.tensor_tensor(pos[:], base[:], ps_r[:, 0], ALU.add))
                link(v.tensor_tensor(ohp[:], oh[:], pos[:].unsqueeze(2).to_broadcast(picks), ALU.mult))
                link(v.tensor_reduce(slot_f[:], ohp[:], AX.X, ALU.add))
                link(v.tensor_copy(sa, slot_f[:].rearrange("s b k -> s (b k)")))
                v.tensor_copy(slot[g.par][:], slot_f[:]).then_inc(slot_ready, 1)
                assert links[0] == ORDER - 2 + 1, links[0]
                link(v.tensor_copy(idx_f[:, 0, 0:1], slot_f[:, 0, 0:1]))
            loop_groups(dve, step, 1)

            at = [NG * ORDER]

            def link(ins):
                at[0] += 1
                ins.then_inc(order, 1)
                dve.wait_ge(order, at[0])
            link(v.tensor_copy(end_row[:], count[0:1]))
            link(v.tensor_tensor(nf[:], count[:], region0[:], ALU.subtract))
            link(v.tensor_scalar(ni[:], nf[:], float(S - 1), None, ALU.add))
            link(v.tensor_scalar(nt_i[:], ni[:], S.bit_length() - 1, None, ALU.logical_shift_right))
            link(v.tensor_copy(ntf[:], nt_i[:]))
            link(v.tensor_copy(te[:], ntf[:]))
            for e in range(1, E):
                link(v.tensor_tensor(te[:, e:e + 1], te[:, e - 1:e], ntf[:, e:e + 1], ALU.add))
            table = [1, TILES, E]
            link(v.tensor_tensor(tmask[:], iota_t[:].unsqueeze(2).to_broadcast(table), te[0:1].unsqueeze(1).to_broadcast(table), ALU.is_ge))
            link(v.tensor_reduce(tef[:], tmask[:], AX.X, ALU.add))
            link(v.tensor_scalar(tile_expert[:], tef[:], float(E - 1), None, ALU.min))
            link(v.tensor_scalar(delta[:], ntf[:], -float(S), float(REGION), ALU.mult, ALU.add))
            link(v.tensor_tensor(tm2[:], tmask[:], delta[0:1].unsqueeze(1).to_broadcast(table), ALU.mult))
            link(v.tensor_reduce(trf[:], tm2[:], AX.X, ALU.add))
            link(v.scalar_tensor_tensor(trf[:], iota_t[:], float(S), trf[:], ALU.mult, ALU.add))
            v.tensor_copy(tile_row[:], trf[:]).then_inc(table_ready, 1)
            each = [S, NG * GB * TOP, E - 1]
            link(v.tensor_tensor(crossed[:], slots_f[:].unsqueeze(2).to_broadcast(each),
                                 region0[:, 1:E].unsqueeze(1).to_broadcast(each), ALU.is_ge))
            link(v.tensor_tensor(crossed[:], crossed[:], delta[:, 0:E - 1].unsqueeze(1).to_broadcast(each), ALU.mult))
            link(v.tensor_reduce(moved[:], crossed[:], AX.X, ALU.add))
            link(v.tensor_tensor(slots_all[:].rearrange("s n b k -> s (n b k)"), slots_f[:], moved[:], ALU.subtract))


def expert_tiles(nc, xs, ys, w1, w2, keep):
    _, _, tile_row, tile_expert = keep
    NB1 = E * 2 * F // 128
    with ExitStack() as c:
        sb = lambda name, shape, dt=F32: c.enter_context(nc.sbuf_tensor("M_" + name, shape, dt))
        pb = lambda name, shape, dt=F32: c.enter_context(nc.psum_tensor("M_" + name, shape, dt))
        sem = c.enter_context(phase_semaphores(nc, "M_"))
        two = lambda f: [f(0), f(1)]
        ident = sb("ident", [128, 128])
        w1T, w2T = sb("w1T", [D, E * 2 * F]), sb("w2T", [128, len(FCHUNKS), E * D])
        w1_raw, w2_raw = sb("w1_raw", [128, NB1, D]), sb("w2_raw", [D, E, F])
        NX = 4
        x_t = [sb(f"x{i}", [S, D]) for i in range(NX)]
        xT = two(lambda p: sb(f"xT{p}", [D, S]))
        act_a = two(lambda p: sb(f"act_a{p}", [S, F]))
        h_t = two(lambda p: sb(f"h{p}", [S, F]))
        hT = two(lambda p: sb(f"hT{p}", [128, len(FCHUNKS), S]))
        y_t = [sb(f"y{i}", [S, D]) for i in range(NX)]
        ps_x, ps_y, ps_t = pb("ps_x", [D, 512]), pb("ps_y", [S, 512]), pb("ps_t", [128, 512])
        ps_a, ps_g = two(lambda p: pb(f"ps_a{p}", [S, 512])), two(lambda p: pb(f"ps_g{p}", [S, 512]))

        loaded, cleared, made = sem("loaded"), sem("cleared"), sem("made")
        w_turned, w_copied = sem("w_turned"), sem("w_copied")
        x_loaded = [sem(f"x_loaded{i}") for i in range(NX)]
        x_turned, xT_ready, hidden, silu_ready, h_ready, h_turned, hT_ready, y_done, y_ready = (sem(n) for n in
            ("x_turned", "xT_ready", "hidden", "silu_ready", "h_ready", "h_turned", "hT_ready", "y_done", "y_ready"))
        y_stored = [sem(f"y_stored{i}") for i in range(NX)]
        passed = sem("passed")
        block = c.enter_context(nc.Block())
        U = NX

        def run(eng, step):
            for t in range(-U, U):
                step(t, t % U, 0)
            with eng.Fori(1, TILES // U - 1) as turn:
                for i in range(U):
                    step(turn * U + i, i, turn)
            for t in range(TILES - U, TILES + U):
                step(t, t % U, 0)

        def has(t):
            return not isinstance(t, int) or 0 <= t < TILES

        def row_of(eng, t):
            cell = tile_row[0:1, t:t + 1] if isinstance(t, int) else tile_row[0:1, bass.ds(t, 1)]
            return eng.value_load(cell, min_val=0, max_val=ROUTED_ROWS - S)

        def expert_of(eng, t):
            cell = tile_expert[0:1, t:t + 1] if isinstance(t, int) else tile_expert[0:1, bass.ds(t, 1)]
            return eng.value_load(cell, min_val=0, max_val=E - 1)

        def nth(t, i):
            return (t // U + 1) * 16 if isinstance(t, int) else (t - i + U) * (16 // U)

        @block.sync
        def _(sp):
            for k in range(4):
                n = NB1 // 4
                sp.dma_start(w1_raw[:, k * n:(k + 1) * n],
                             w1.rearrange("e f d -> (e f) d").rearrange("(j p) d -> p j d", p=128)[:, k * n:(k + 1) * n]).then_inc(loaded, 16)
            sp.dma_start(w2_raw[:], w2.rearrange("e d f -> d e f")).then_inc(loaded, 16)

            def step(t, i, turn):
                tl, tll = t + 3, (i + 3) % U
                if has(tl):
                    wait_apart(sp, x_turned, tl - U + 1, passed)
                    r = row_of(sp, tl)
                    sp.dma_start(x_t[tll][:], xs[bass.ds(r, S)]).then_inc(x_loaded[tll], 16)
            run(sp, step)

        @block.gpsimd
        def _(pool):
            diagonal(nc, pool, ident, cleared, made)

            def step(t, i, turn):
                ts, si = t - 3, (i - 3) % U
                if has(ts):
                    wait_apart(pool, y_ready, ts + 1, passed)
                    pool.dma_start(ys[ts * S:(ts + 1) * S] if isinstance(ts, int) else ys[bass.ds(ts * S, S)], y_t[si][:]).then_inc(y_stored[si], 16)
            run(pool, step)
            for i in range(NX):
                pool.wait_ge(y_stored[i], TILES // NX * 16)

        @block.tensor
        def _(pe):
            pe.wait_ge(loaded, 16 * 5)
            pe.wait_ge(made, 1)
            for j in range(NB1 // 4):
                wait(pe, w_copied, j - 1)
                for k in range(4):
                    last = nc.tensor.transpose(ps_a[j % 2][:, k * 128:(k + 1) * 128], w1_raw[:, 4 * j + k], ident[:])
                last.then_inc(w_turned, 1)
            for e in range(E):
                n = NB1 // 4 + e
                wait(pe, w_copied, n - 1)
                for k, (f0, fn) in enumerate(FCHUNKS):
                    last = nc.tensor.transpose(ps_a[n % 2][0:fn, k * 128:(k + 1) * 128], w2_raw[:, e, f0:f0 + fn], ident[:])
                last.then_inc(w_turned, 1)
            pe.wait_ge(w_copied, NB1 // 4 + E)

            def step(t, i, turn):
                tx, th, tt, ty = t + 2, t + 1, t, t - 1
                if has(th):
                    e_h = expert_of(pe, th)
                if has(ty):
                    e_y = expert_of(pe, ty)
                if has(tx):
                    pe.wait_ge(x_loaded[(i + 2) % U], nth(tx, (i + 2) % U))
                    wait(pe, xT_ready, tx)
                    nc.tensor.transpose(ps_x[:, 0:S], x_t[(i + 2) % U][:], ident[:]).then_inc(x_turned, 1)
                if has(th):
                    p = (i + 1) % 2
                    pe.wait_ge(xT_ready, th + 1)
                    wait(pe, h_ready, th - 1)
                    nc.tensor.matmul(ps_a[p][:, 0:F], xT[p][:], w1T[:, bass.ds(e_h * (2 * F), F)], start=True, stop=True)
                    nc.tensor.matmul(ps_g[p][:, 0:F], xT[p][:], w1T[:, bass.ds(e_h * (2 * F) + F, F)],
                                     start=True, stop=True).then_inc(hidden, 1)
                if has(tt):
                    p = i % 2
                    pe.wait_ge(h_ready, tt + 1)
                    wait(pe, hT_ready, tt)
                    for k, (f0, fn) in enumerate(FCHUNKS):
                        last = nc.tensor.transpose(ps_t[0:fn, k * S:(k + 1) * S], h_t[p][:, f0:f0 + fn], ident[:])
                    last.then_inc(h_turned, 1)
                if has(ty):
                    p = (i - 1) % 2
                    pe.wait_ge(hT_ready, ty + 1)
                    wait(pe, y_ready, ty)
                    for k, (f0, fn) in enumerate(FCHUNKS):
                        last = nc.tensor.matmul(ps_y[:, 0:D], hT[p][0:fn, k], w2T[0:fn, k, bass.ds(e_y * D, D)],
                                                start=(k == 0), stop=(k == len(FCHUNKS) - 1))
                    last.then_inc(y_done, 1)
            run(pe, step)

        @block.scalar
        def _(act):
            def step(t, i, turn):
                th, tt = t + 1, t
                if has(th):
                    p = (i + 1) % 2
                    act.wait_ge(hidden, th + 1)
                    nc.scalar.activation(act_a[p][:], ps_a[p][:, 0:F], ACT.Silu).then_inc(silu_ready, 1)
                if has(tt):
                    p = i % 2
                    act.wait_ge(h_turned, tt + 1)
                    wait(act, y_done, tt - 1)
                    nc.scalar.copy(hT[p][:, 0:2], ps_t[:, 0:2 * S].rearrange("f (k s) -> f k s", s=S))
                    nc.scalar.copy(hT[p][0:F - 256, 2], ps_t[0:F - 256, 2 * S:3 * S]).then_inc(hT_ready, 1)
            run(act, step)

        @block.vector
        def _(dve):
            for j in range(NB1 // 4):
                dve.wait_ge(w_turned, j + 1)
                nc.vector.tensor_copy(w1T[:, j * 512:(j + 1) * 512], ps_a[j % 2][:]).then_inc(w_copied, 1)
            for e in range(E):
                n = NB1 // 4 + e
                dve.wait_ge(w_turned, n + 1)
                nc.vector.tensor_copy(w2T[:, 0:2, e * D:(e + 1) * D],
                                      ps_a[n % 2][:, 0:256].rearrange("f (k d) -> f k d", d=D))
                nc.vector.tensor_copy(w2T[0:F - 256, 2, e * D:(e + 1) * D], ps_a[n % 2][0:F - 256, 256:384]).then_inc(w_copied, 1)

            def step(t, i, turn):
                tx, th, ty = t + 2, t + 1, t - 1
                if has(tx):
                    dve.wait_ge(x_turned, tx + 1)
                    wait(dve, hidden, tx - 1)
                    nc.vector.tensor_copy(xT[i % 2][:], ps_x[:, 0:S]).then_inc(xT_ready, 1)
                if has(th):
                    p = (i + 1) % 2
                    dve.wait_ge(silu_ready, th + 1)
                    wait(dve, h_turned, th - 1)
                    nc.vector.tensor_tensor(h_t[p][:], act_a[p][:], ps_g[p][:, 0:F], ALU.mult).then_inc(h_ready, 1)
                if has(ty):
                    j = (i - 1) % U
                    dve.wait_ge(y_done, ty + 1)
                    wait(dve, y_stored[j], nth(ty, j) - 16)
                    nc.vector.tensor_copy(y_t[j][:], ps_y[:, 0:D]).then_inc(y_ready, 1)
            run(dve, step)


def combine(nc, x1, x2, ys, keep):
    slots_all, gates_all, _, _ = keep
    x_v, o_v = (t.rearrange("(n b) s d -> n s b d", b=GB) for t in (x1, x2))
    with ExitStack() as c:
        sb = lambda name, shape, dt=F32: c.enter_context(nc.sbuf_tensor("K_" + name, shape, dt))
        sem = c.enter_context(phase_semaphores(nc, "K_"))
        two = lambda f: [f(0), f(1)]
        x_t = two(lambda p: sb(f"x{p}", [S, GB, D]))
        y_t = two(lambda p: sb(f"y{p}", [S, GB, TOP, D]))
        acc, out = sb("acc", [S, GB, D]), two(lambda p: sb(f"out{p}", [S, GB, D]))
        slot = two(lambda p: sb(f"slot{p}", [S, GB, TOP], mybir.dt.uint32))
        gate = two(lambda p: sb(f"gate{p}", [S, GB, TOP]))
        x_loaded, gathered, stored = (two(lambda p: sem(f"{n}{p}")) for n in ("x_loaded", "gathered", "stored"))
        slot_ready, gate_ready, added, summed, passed = (sem(n) for n in ("slot_ready", "gate_ready", "added", "summed", "passed"))
        block = c.enter_context(nc.Block())
        cell = lambda t, g: t[:, g.n] if isinstance(g.pair, int) else t[:, bass.ds(g.n, 1)][:, 0]

        @block.sync
        def _(sp):
            def step(g):
                g1, gm = g + 1, g + -1
                if g1.exists:
                    wait_apart(sp, summed, g1.n - 1, passed)
                    sp.dma_start(x_t[g1.par][:], x_v[g1.n]).then_inc(x_loaded[g1.par], 16)
                if gm.exists:
                    wait_apart(sp, summed, gm.n + 1, passed)
                    sp.dma_start(o_v[gm.n], out[gm.par][:]).then_inc(stored[gm.par], 16)
            loop_groups(sp, step, 1)
            for p in range(2):
                sp.wait_ge(stored[p], NG // 2 * 16)

        @block.scalar
        def _(act):
            def step(g):
                g1 = g + 1
                if g1.exists:
                    wait_apart(act, gathered[g1.par], g1.pair * GB * TOP * 16, passed)
                    nc.scalar.copy(slot[g1.par][:].bitcast(F32), cell(slots_all, g1).bitcast(F32)).then_inc(slot_ready, 1)
                    wait_apart(act, summed, g1.n - 1, passed)
                    nc.scalar.copy(gate[g1.par][:], cell(gates_all, g1)).then_inc(gate_ready, 1)
            loop_groups(act, step, 1)

        @block.gpsimd
        def _(pool):
            def step(g):
                g1 = g + 1
                if g1.exists:
                    wait_apart(pool, slot_ready, g1.n + 1, passed)
                    wait_apart(pool, summed, g1.n - 1, passed)
                    for b in range(GB):
                        for k in range(TOP):
                            nc.gpsimd.indirect_dma_start(
                                out=y_t[g1.par][:, b, k], out_offset=None, in_=ys,
                                in_offset=bass.IndirectOffsetOnAxis(ap=slot[g1.par][:, b, k:k + 1], axis=0),
                            ).then_inc(gathered[g1.par], 16)
            loop_groups(pool, step, 1)

        @block.vector
        def _(dve):
            def step(g):
                if not g.exists:
                    return
                p = g.par
                wait_apart(dve, x_loaded[p], (g.pair + 1) * 16, passed)
                wait_apart(dve, gathered[p], (g.pair + 1) * GB * TOP * 16, passed)
                wait_apart(dve, gate_ready, g.n + 1, passed)
                wait_apart(dve, stored[p], g.pair * 16, passed)
                wait_apart(dve, summed, g.n, passed)
                for b in range(GB):
                    last = nc.vector.scalar_tensor_tensor(acc[:, b], y_t[p][:, b, 0], gate[p][:, b, 0:1], x_t[p][:, b], ALU.mult, ALU.add)
                last.then_inc(added, 1)
                wait_apart(dve, added, g.n + 1, passed)
                for b in range(GB):
                    last = nc.vector.scalar_tensor_tensor(out[p][:, b], y_t[p][:, b, 1], gate[p][:, b, 1:2], acc[:, b], ALU.mult, ALU.add)
                last.then_inc(summed, 1)
            loop_groups(dve, step, 1)


R = 64
ER = E * R
SCALING = 2.0


def adapter_layer(nc, x3, out, Wg, bg, W1, W2):
    x_v, o_v = (t.rearrange("(n b) s d -> n s b d", b=GB) for t in (x3, out))
    with ExitStack() as c:
        sb = lambda name, shape, dt=F32: c.enter_context(nc.sbuf_tensor("F_" + name, shape, dt))
        pb = lambda name, shape, dt=F32: c.enter_context(nc.psum_tensor("F_" + name, shape, dt))
        sem = c.enter_context(phase_semaphores(nc, "F_"))
        two = lambda f: [f(0), f(1)]
        ident, half_neg = sb("ident", [128, 128]), sb("half_neg", [S, GB])
        iota_e, iota_ei = sb("iota_e", [S, E]), sb("iota_ei", [S, E], I32)
        wg_raw, bg_bc = sb("wg_raw", [E, D]), sb("bg_bc", [S, E])
        w1_raw, w2_raw = sb("w1_raw", [128, ER // 128, D]), sb("w2_raw", [D, E, R])
        wgT, w1T, w2T = sb("wgT", [D, E]), sb("w1T", [D, ER]), sb("w2T", [128, ER // 128, D])
        NX = 4
        x_t = two(lambda p: sb(f"x{p}", [S, GB, D]))
        res_t = two(lambda p: sb(f"res{p}", [S, GB, D]))
        stats, mv, rstd, xn = sb("stats", [S, GB, 6]), sb("mv", [S, GB, 2]), sb("rstd", [S, GB]), sb("xn", [S, GB, D])
        xnT = two(lambda p: sb(f"xnT{p}", [D, GB, S]))
        lg, top = sb("lg", [S, GB, E]), sb("top", [S, GB, 8])
        top_i, idx_f = sb("top_i", [S, GB, 8], mybir.dt.uint32), sb("idx_f", [S, GB, TOP])
        diff, e2, den, gates = sb("diff", [S, GB]), sb("e2", [S, GB]), sb("den", [S, GB]), sb("gates", [S, GB, TOP])
        oh = sb("oh", [S, GB, TOP, E])
        gate_e = two(lambda p: sb(f"gate_e{p}", [S, GB, E]))
        h_t, hg = two(lambda p: sb(f"h{p}", [S, ER])), two(lambda p: sb(f"hg{p}", [S, ER]))
        hgT = two(lambda p: sb(f"hgT{p}", [128, ER]))
        out_t = two(lambda p: sb(f"out{p}", [S, GB, D]))
        ps_x, ps_l, ps_y = pb("ps_x", [D, GB, S]), pb("ps_l", [S, GB, E]), pb("ps_y", [S, 512])
        ps_h, ps_t = two(lambda p: pb(f"ps_h{p}", [S, 512])), two(lambda p: pb(f"ps_t{p}", [128, 512]))

        loaded, cleared, made = sem("loaded"), sem("cleared"), sem("made")
        w_turned, w_copied, passed, order = sem("w_turned"), sem("w_copied"), sem("passed"), sem("order")
        x_loaded, res_loaded, stored = (two(lambda p: sem(f"{n}{p}")) for n in ("x_loaded", "res_loaded", "stored"))
        (stats_ready, aggregated, eps_added, rstd_ready, normed, x_turned, xT_ready, logits_done, gap_ready, e2_ready,
         gates_ready, hidden, gelu_ready, gated, h_turned, hT_ready, y_done, summed) = (sem(n) for n in (
            "stats_ready", "aggregated", "eps_added", "rstd_ready", "normed", "x_turned", "xT_ready", "logits_done",
            "gap_ready", "e2_ready", "gates_ready", "hidden", "gelu_ready", "gated", "h_turned", "hT_ready", "y_done", "summed"))
        ORDER = 10
        block = c.enter_context(nc.Block())

        def at(g, b):
            gg, bb = (g + 1, b - GB) if b >= GB else (g + -1, b + GB) if b < 0 else (g, b)
            return gg, bb, gg.n * GB + bb

        @block.sync
        def _(sp):
            sp.dma_start(w1_raw[:], W1.rearrange("e r d -> (e r) d").rearrange("(j p) d -> p j d", p=128)).then_inc(loaded, 16)
            sp.dma_start(w2_raw[:], W2.rearrange("e d r -> d e r")).then_inc(loaded, 16)
            sp.dma_start(wg_raw[:], Wg).then_inc(loaded, 16)
            sp.dma_start(bg_bc[:], bg.unsqueeze(0).to_broadcast([S, E])).then_inc(loaded, 16)

            def step(g):
                g2, gm = g + 2, g + -1
                if g2.exists:
                    wait_apart(sp, normed, g2.n - 1, passed)
                    sp.dma_start(x_t[g2.par][:], x_v[g2.n]).then_inc(x_loaded[g2.par], 16)
                if g.exists:
                    wait_apart(sp, summed, (g.n - 1) * GB, passed)
                    sp.dma_start(res_t[g.par][:], x_v[g.n]).then_inc(res_loaded[g.par], 16)
                if gm.exists:
                    wait_apart(sp, summed, (gm.n + 1) * GB, passed)
                    sp.dma_start(o_v[gm.n], out_t[gm.par][:]).then_inc(stored[gm.par], 16)
            loop_groups(sp, step, 2)
            for p in range(2):
                sp.wait_ge(stored[p], NG // 2 * 16)

        @block.gpsimd
        def _(pool):
            nc.gpsimd.memset(half_neg[:], -0.5).then_inc(cleared, 1)
            pool.wait_ge(cleared, 1)
            nc.gpsimd.memset(ident[:], 0.0).then_inc(cleared, 1)
            pool.wait_ge(cleared, 2)
            nc.gpsimd.affine_select(out=ident[:], in_=ident[:], compare_op=ALU.not_equal, fill=1.0, base=0,
                                    pattern=[[-1, 128]], channel_multiplier=1).then_inc(made, 1)
            nc.gpsimd.iota(iota_ei[:], pattern=[[1, E]], base=0, channel_multiplier=0).then_inc(cleared, 1)
            pool.wait_ge(cleared, 3)
            nc.gpsimd.tensor_copy(iota_e[:], iota_ei[:]).then_inc(made, 1)

            def step(g):
                g1 = g + 1
                if g1.exists:
                    wait_apart(pool, aggregated, g1.n + 1, passed)
                    nc.gpsimd.tensor_scalar(rstd[:], mv[:, :, 1], EPS, None, ALU.add).then_inc(eps_added, 1)
                    wait_apart(pool, eps_added, g1.n + 1, passed)
                    nc.gpsimd.tensor_tensor(rstd[:], rstd[:], half_neg[:], ALU.pow).then_inc(rstd_ready, 1)
            loop_groups(pool, step, 1)

        @block.tensor
        def _(pe):
            pe.wait_ge(loaded, 16 * 4)
            pe.wait_ge(made, 1)
            for j in range(ER // 128):
                last = nc.tensor.transpose(ps_h[0][:, j * 128:(j + 1) * 128], w1_raw[:, j], ident[:])
            last.then_inc(w_turned, 1)
            w2_rows = w2_raw[:].rearrange("d e r -> d (e r)")
            for j in range(ER // 128):
                last = nc.tensor.transpose(ps_h[1][:, j * 128:(j + 1) * 128], w2_rows[:, j * 128:(j + 1) * 128], ident[:])
            last.then_inc(w_turned, 1)
            nc.tensor.transpose(ps_y[:, 0:E], wg_raw[:], ident[0:E, 0:E]).then_inc(w_turned, 1)
            pe.wait_ge(w_copied, 3)

            def step(g):
                g1 = g + 1
                for b in range(GB):
                    if b == 0 and g1.exists:
                        pe.wait_ge(normed, g1.n + 1)
                        wait(pe, xT_ready, g1.n)
                        for j in range(GB):
                            last = nc.tensor.transpose(ps_x[:, j], xn[:, j], ident[:])
                        last.then_inc(x_turned, 1)
                    if b == 1 and g1.exists:
                        pe.wait_ge(xT_ready, g1.n + 1)
                        wait(pe, gap_ready, g1.n)
                        for j in range(GB):
                            last = nc.tensor.matmul(ps_l[:, j], xnT[g1.par][:, j], wgT[:], start=True, stop=True)
                        last.then_inc(logits_done, 1)
                    gh, bh, vh = at(g, b + 1)
                    if gh.exists:
                        if bh == 0:
                            pe.wait_ge(xT_ready, gh.n + 1)
                        wait(pe, gelu_ready, vh - 1)
                        nc.tensor.matmul(ps_h[bh % 2][:], xnT[gh.par][:, bh], w1T[:], start=True, stop=True).then_inc(hidden, 1)
                    if g.exists:
                        v = g.n * GB + b
                        pe.wait_ge(gated, v + 1)
                        wait(pe, hT_ready, v - 1)
                        for j in range(ER // 128):
                            last = nc.tensor.transpose(ps_t[b % 2][:, j * 128:(j + 1) * 128], hg[b % 2][:, j * 128:(j + 1) * 128], ident[:])
                        last.then_inc(h_turned, 1)
                    gy, by, vy = at(g, b - 1)
                    if gy.exists:
                        pe.wait_ge(hT_ready, vy + 1)
                        wait(pe, summed, vy)
                        for j in range(ER // 128):
                            last = nc.tensor.matmul(ps_y[:, 0:D], hgT[by % 2][:, j * 128:(j + 1) * 128], w2T[:, j],
                                                    start=(j == 0), stop=(j == ER // 128 - 1))
                        last.then_inc(y_done, 1)
            loop_groups(pe, step, 1)

        @block.scalar
        def _(act):
            def step(g):
                g1 = g + 1
                for b in range(GB):
                    if b == 0 and g1.exists:
                        act.wait_ge(x_turned, g1.n + 1)
                        wait(act, hidden, (g1.n - 1) * GB)
                        nc.scalar.copy(xnT[g1.par][:], ps_x[:]).then_inc(xT_ready, 1)
                    gh, bh, vh = at(g, b + 1)
                    if gh.exists:
                        act.wait_ge(hidden, vh + 1)
                        wait(act, gated, vh - 1)
                        nc.scalar.activation(h_t[bh % 2][:], ps_h[bh % 2][:], ACT.Gelu).then_inc(gelu_ready, 1)
                    if g.exists:
                        v = g.n * GB + b
                        act.wait_ge(h_turned, v + 1)
                        wait(act, y_done, v - 1)
                        nc.scalar.copy(hgT[b % 2][:], ps_t[b % 2][:]).then_inc(hT_ready, 1)
                    if b == 1 and g1.exists:
                        act.wait_ge(gap_ready, g1.n + 1)
                        nc.scalar.activation(e2[:], diff[:], ACT.Exp).then_inc(e2_ready, 1)
            loop_groups(act, step, 1)

        @block.vector
        def _(dve):
            v_ = nc.vector
            dve.wait_ge(w_turned, 3)
            dve.wait_ge(made, 2)
            v_.tensor_copy(w1T[:], ps_h[0][:]).then_inc(w_copied, 1)
            v_.tensor_copy(w2T[:].rearrange("p j d -> p (j d)"), ps_h[1][:]).then_inc(w_copied, 1)
            v_.tensor_copy(wgT[:], ps_y[:, 0:E]).then_inc(w_copied, 1)

            def step(g):
                g1 = g + 1
                links = [0]

                def link(ins):
                    links[0] += 1
                    ins.then_inc(order, 1)
                    wait_apart(dve, order, g1.n * ORDER + links[0], passed)
                for b in range(GB):
                    if b == 0 and g1.exists:
                        wait_apart(dve, x_loaded[g1.par], (g1.pair + 1) * 16, passed)
                        for j in range(GB):
                            v_.bn_stats(stats[:, j], x_t[g1.par][:, j]).then_inc(stats_ready, 1)
                        wait_apart(dve, stats_ready, (g1.n + 1) * GB, passed)
                        for j in range(GB):
                            last = v_.bn_aggr(mv[:, j], stats[:, j])
                        last.then_inc(aggregated, 1)
                        wait_apart(dve, rstd_ready, g1.n + 1, passed)
                        wait_apart(dve, x_turned, g1.n, passed)
                        for j in range(GB):
                            last = v_.tensor_scalar(xn[:, j], x_t[g1.par][:, j], mv[:, j, 0:1], rstd[:, j:j + 1],
                                                    ALU.subtract, ALU.mult)
                        last.then_inc(normed, 1)
                    if b == 1 and g1.exists:
                        wait_apart(dve, logits_done, g1.n + 1, passed)
                        link(v_.tensor_tensor(lg[:], ps_l[:], bg_bc[:].unsqueeze(1).to_broadcast([S, GB, E]), ALU.add))
                        for j in range(GB):
                            last = v_.max(top[:, j], lg[:, j])
                        link(last)
                        for j in range(GB):
                            last = v_.max_index(top_i[:, j], top[:, j], lg[:, j])
                        link(last)
                        v_.tensor_tensor(diff[:], top[:, :, 1], top[:, :, 0], ALU.subtract).then_inc(gap_ready, 1)
                        link(v_.tensor_copy(idx_f[:], top_i[:, :, 0:TOP]))
                        picks = [S, GB, TOP, E]
                        link(v_.tensor_tensor(oh[:], iota_e[:].unsqueeze(1).unsqueeze(1).to_broadcast(picks),
                                              idx_f[:].unsqueeze(3).to_broadcast(picks), ALU.is_equal))
                    if b == 2 and g1.exists:
                        wait_apart(dve, e2_ready, g1.n + 1, passed)
                        link(v_.tensor_scalar(den[:], e2[:], 1.0, None, ALU.add))
                        link(v_.reciprocal(gates[:, :, 0], den[:]))
                        link(v_.tensor_tensor(gates[:, :, 1], e2[:], gates[:, :, 0], ALU.mult))
                        link(v_.tensor_tensor(oh[:], oh[:], gates[:].unsqueeze(3).to_broadcast(picks), ALU.mult))
                        link(v_.tensor_tensor(gate_e[g1.par][:], oh[:, :, 0], oh[:, :, 1], ALU.add))
                        assert links[0] == ORDER
                    gh, bh, vh = at(g, b + 1)
                    if gh.exists:
                        dve.wait_ge(gelu_ready, vh + 1)
                        wait(dve, h_turned, vh - 1)
                        v_.tensor_tensor(hg[bh % 2][:].rearrange("s (e r) -> s e r", r=R),
                                         h_t[bh % 2][:].rearrange("s (e r) -> s e r", r=R),
                                         gate_e[gh.par][:, bh].unsqueeze(2).to_broadcast([S, E, R]), ALU.mult).then_inc(gated, 1)
                    gy, by, vy = at(g, b - 1)
                    if gy.exists:
                        dve.wait_ge(y_done, vy + 1)
                        if by == 0:
                            wait_apart(dve, res_loaded[gy.par], (gy.pair + 1) * 16, passed)
                            wait_apart(dve, stored[gy.par], gy.pair * 16, passed)
                        v_.scalar_tensor_tensor(out_t[gy.par][:, by], ps_y[:, 0:D], SCALING, res_t[gy.par][:, by],
                                                ALU.mult, ALU.add).then_inc(summed, 1)
            loop_groups(dve, step, 1)


def encoder(nc, a, out):
    x1, x2, x3 = (nc.dram_tensor(n, (B, S, D), F32, kind="Internal").ap() for n in ("x1", "x2", "x3"))
    xs = nc.dram_tensor("routed_in", (ROUTED_ROWS, D), F32, kind="Internal").ap()
    ys = nc.dram_tensor("routed_out", (TILES * S, D), F32, kind="Internal").ap()
    with ExitStack() as c:
        w = [a["L0_xattn_" + n] for n in ("Wq", "bq", "Wk", "bk", "Wv", "bv", "Wp", "bp")]
        attention_layer(nc, a["x"], x1, a["fside_BxSxS_0"], a["ctx_1024"], 0, attention_consts(nc, c, w, 0))
    with ExitStack() as c:
        sb = lambda name, shape, dt: c.enter_context(nc.sbuf_tensor(name, shape, dt))
        keep = (sb("slots_all", [S, NG, GB, TOP], mybir.dt.uint32), sb("gates_all", [S, NG, GB, TOP], F32),
                sb("tile_row", [1, TILES], I32), sb("tile_expert", [1, TILES], I32))
        route_tokens(nc, x1, xs, a["L0_ffn_wqkv"], keep)
        expert_tiles(nc, xs, ys, a["L0_ffn_w1"], a["L0_ffn_w2"], keep)
        combine(nc, x1, x2, ys, keep)
    with ExitStack() as c:
        w = [a["L1_xattn_" + n] for n in ("W_q", "b_q", "W_k", "b_k", "W_v", "b_v", "W_o", "b_o")]
        attention_layer(nc, x2, x3, a["fside_BxSxS_0"], a["ctx_1024"], 1, attention_consts(nc, c, w, 1))
    adapter_layer(nc, x3, out, a["L1_ffn_Wg"], a["L1_ffn_bg"], a["L1_ffn_W1"], a["L1_ffn_W2"])


INPUTS = ["x", "fside_BxSxS_0", "ctx_1024"] + ["L0_xattn_" + n for n in ("Wq", "bq", "Wk", "bk", "Wv", "bv", "Wp", "bp")] \
    + ["L0_ffn_" + n for n in ("wqkv", "w1", "w2")] \
    + ["L1_xattn_" + n for n in ("W_q", "b_q", "W_k", "b_k", "W_v", "b_v", "W_o", "b_o")] \
    + ["L1_ffn_" + n for n in ("Wg", "bg", "W1", "W2")]


def kernel(**inputs):
    import concourse.bacc as bacc
    from concourse.bass_utils import run_bass_kernel_spmd as run

    nc = bacc.Bacc("TRN2", target_bir_lowering=False, num_devices=1)
    arrays, tensors = {}, {}
    for name in INPUTS:
        array = np.ascontiguousarray(inputs[name])
        arrays["in_" + name] = array
        tensors[name] = nc.dram_tensor("in_" + name, array.shape, mybir.dt.from_np(array.dtype), kind="ExternalInput").ap()
    out = nc.dram_tensor("out_0", (B, S, D), F32, kind="ExternalOutput").ap()
    encoder(nc, tensors, out)
    return run(nc, [arrays], core_ids=[0]).results[0]["out_0"]
```

```python
import concourse.bass as bass
from concourse import mybir
from contextlib import ExitStack, contextmanager
import numpy as np

F32 = mybir.dt.float32
BF16 = mybir.dt.bfloat16
I32 = mybir.dt.int32
ACT = mybir.ActivationFunctionType
ALU = mybir.AluOpType
AX = mybir.AxisListType

B, S, D = 64, 128, 128
H, DH = 16, 8
SC = 120
E = 8
GB = 4
NG = B // GB
EPS = 1e-5
FIRST_STEP = -3
ONE_ONE = 0x3F803F80
NPART = 3
TERM_ROWS = NPART * NPART * DH
SHIFT_ROW = 96
STACK_ROWS = SHIFT_ROW + 2
HALF = H // 2


@contextmanager
def phase_semaphores(nc, tag):
    held = []

    def sem(name):
        held.append(nc.alloc_semaphore(tag + name))
        return held[-1]
    yield sem
    nc.clear_and_free_semaphores(held)
    nc.all_engine_barrier()


class Group:

    def __init__(self, pair, par):
        self.pair, self.par = pair, par

    def __add__(self, k):
        t = self.par + k
        return Group(self.pair + t // 2 if t // 2 else self.pair, t % 2)

    @property
    def n(self):
        return self.pair * 2 + self.par

    @property
    def exists(self):
        return not isinstance(self.pair, int) or 0 <= self.n < NG


def wait(eng, sem, value):
    if isinstance(value, int) and value <= 0:
        return
    eng.wait_ge(sem, value)


def wait_apart(eng, sem, value, passed):
    if isinstance(value, int):
        return wait(eng, sem, value)
    eng.wait_ge(sem, value)
    eng.sem_inc(passed, 1)


def run_steps(eng, step):
    for n in range(FIRST_STEP, 2):
        step(Group(n // 2, n % 2))
    with eng.Fori(1, NG // 2 - 2) as pair:
        step(Group(pair, 0))
        step(Group(pair, 1))
    for n in range(NG - 4, NG + 1):
        step(Group(n // 2, n % 2))


def attention_layer(nc, x_in, x_out, side, ctx_in, layer, consts):
    first = layer == 0
    KEYS = [S, SC] if first else [SC]
    NT = len(KEYS)
    NK = sum(KEYS)
    HPB = 2 if first else 4
    MT_PER_B = H // HPB
    MT_PER_U = MT_PER_B // 2
    tag = f"L{layer}_"
    ident, ident_bf, wq, wk, wv, wo, bq, bk, bv_bc, bo_bc, half_neg = consts

    q_scr = nc.dram_tensor(tag + "q_parts", (2, GB, NPART, D, S), BF16, kind="Internal").ap()
    k_scr = nc.dram_tensor(tag + "k_parts", (2, GB, NPART, D, NK), BF16, kind="Internal").ap()
    x_v = x_in.rearrange("(n b) s d -> n s b d", b=GB)
    xo_v = x_out.rearrange("(n b) s d -> n s b d", b=GB)
    side_v = side.rearrange("(n b) s d -> n s b d", b=GB)
    ctx_v = ctx_in.rearrange("(n b) s d -> n s b d", b=GB)

    if first:
        jobs = [(0, 0, "FT", 0), (0, 2, "MT", 2), (1, 0, "KP", 0), (1, 1, "OB", 3), (1, 2, "CX", 0), (2, 0, "XT", 0),
                (2, 1, "AT", 0), (2, 2, "QP", 0), (3, 0, "OP", 0), (3, 2, "VP", 0), (4, 0, "OB", 0), (4, 2, "MT", 0),
                (5, 2, "OB", 1), (7, 2, "OB", 2)]
    else:
        jobs = [(0, 0, "FT", 0), (0, 1, "MT", 2), (1, 0, "KP", 0), (1, 1, "OB", 3), (2, 0, "XT", 0), (2, 1, "AT", 0),
                (3, 0, "QP", 0), (3, 1, "OP", 0), (4, 0, "OB", 0), (4, 1, "MT", 0), (5, 0, "VP", 0), (5, 1, "OB", 1),
                (7, 1, "OB", 2)]
    if first:
        UNIT = [("job", 0), ("scores", 0), ("max", 0), ("job", 1), ("max", 1), ("scores", 1), ("max", 2), ("job", 2),
                ("values", 0), ("max", 3), ("values", 1)]
    else:
        UNIT = [("job", 0), ("scores", 0), ("max", 0), ("job", 1), ("values", 0), ("max", 1), ("values", 1)]
    def job_group(u, place, name, b):
        if name in ("XT", "QP", "FT", "KP", "CX"):
            return 2
        if name == "VP":
            return 1
        if name in ("AT", "OP"):
            return -1
        if name == "OB":
            return -1 if u < 3 else 0
        return 1 if u >= 2 else 0
    def job_runs(g, job):
        return (g + job_group(*job)).exists

    NJ = len(jobs)
    peeled = {}
    total = 0
    for n in range(FIRST_STEP, NG + 1):
        peeled[n] = total
        total += sum(job_runs(Group(n // 2, n % 2), j) for j in jobs)
    LOOP0 = 2
    def job_no(g, k):
        if isinstance(g.pair, int):
            return peeled[g.n] + sum(job_runs(g, j) for j in jobs[:k])
        return g.n * NJ + (peeled[LOOP0] - LOOP0 * NJ + k)
    def job_done(gj, name, b=0):
        k = [j[2:] for j in jobs].index((name, b))
        return job_no(gj + -job_group(*jobs[k]), k) + 1 if gj.exists else 0

    with ExitStack() as c:
        sb = lambda name, shape, dt=F32: c.enter_context(nc.sbuf_tensor(tag + name, shape, dt))
        pb = lambda name, shape, dt=F32: c.enter_context(nc.psum_tensor(tag + name, shape, dt))
        sem = c.enter_context(phase_semaphores(nc, tag))
        two = lambda f: [f(0), f(1)]

        x_t = two(lambda p: sb(f"x{p}", [S, GB, D]))
        res_t = two(lambda p: sb(f"res{p}", [S, GB, D]))
        side_t = two(lambda p: sb(f"side{p}", [S, GB, D])) if first else None
        ctx_t = two(lambda p: sb(f"ctx{p}", [SC, GB, D]))
        stats = sb("stats", [S, GB, 6])
        mv = sb("mv", [S, GB, 2])
        rstd = sb("rstd", [S, GB])
        xn = sb("xn", [S, GB, D])
        ctx_o = sb("ctx_o", [SC, GB, D]) if first else None
        xnT = sb("xnT", [D, GB * S])
        srcT = two(lambda p: sb(f"srcT{p}", [D, GB, KEYS[0]]))
        qf = sb("qf", [D, GB, S])
        kf = sb("kf", [D, GB, NK])
        rem = sb("rem", [D, GB, max(NK, S)])
        q_parts = sb("q_parts_sb", [D, GB, NPART, S], BF16)
        k_parts = sb("k_parts_sb", [D, GB, NPART, NK], BF16)
        q_st = two(lambda p: sb(f"q_stack{p}", [STACK_ROWS, GB, H, S], BF16))
        k_st = two(lambda p: sb(f"k_stack{p}", [STACK_ROWS, GB, H, NK], BF16))
        v_t = [two(lambda p: sb(f"v{t}_{p}", [KEYS[t], GB, H, DH + 1])) for t in range(NT)]
        p_t = [two(lambda p: sb(f"p{t}_{p}", [KEYS[t], HALF * S])) for t in range(NT)]
        neg_max = sb("neg_max", [S, GB, H])
        m_parts = two(lambda p: sb(f"m_parts{p}", [S, 2, 2, H], BF16))
        mT = two(lambda p: sb(f"mT{p}", [4 * H, S], BF16))
        o_sb = sb("o_sb", [D, 4 * S])
        rden = sb("rden", [S, H])
        att = sb("att", [S, GB, H, DH])
        attT = sb("attT", [D, GB * S])
        out_t = two(lambda p: sb(f"out{p}", [S, GB, D]))

        ps_sc = two(lambda p: pb(f"ps_sc{p}", [S, HALF * S]))
        ps_mx = two(lambda p: pb(f"ps_mx{p}", [S, 512]))
        ps_o = pb("ps_o", [D, 512])
        misc = pb("misc", [D, 512])
        misc_bf = misc[0:4 * H, 0:S // 2].bitcast(BF16)

        x_loaded = two(lambda p: sem(f"x_loaded{p}"))
        res_loaded = two(lambda p: sem(f"res_loaded{p}"))
        side_loaded = two(lambda p: sem(f"side_loaded{p}")) if first else None
        ctx_loaded = two(lambda p: sem(f"ctx_loaded{p}"))
        stored = two(lambda p: sem(f"stored{p}"))
        q_written, k_written = sem("q_written"), sem("k_written")
        st_loaded = [[sem(f"st_loaded{p}{b}") for b in range(GB)] for p in range(2)]
        shift_loaded = [[sem(f"shift_loaded{p}{k}") for k in range(2)] for p in range(2)]
        aggregated, rstd_ready, normed = sem("aggregated"), sem("rstd_ready"), sem("normed")
        stats_ready, eps_added = sem("stats_ready"), sem("eps_added")
        misc_filled, misc_emptied = sem("misc_filled"), sem("misc_emptied")
        q_split, k_split, v_ctx_ready = sem("q_split"), sem("k_split"), sem("v_ctx_ready")
        res_ready, split_step = sem("res_ready"), sem("split_step")
        q_cleared = sem("q_cleared")
        passed = sem("passed")
        stack_cleared, ctx_ordered = sem("stack_cleared"), sem("ctx_ordered")
        max_filled, max_read = sem("max_filled"), sem("max_read")
        sc_filled, sc_read = sem("sc_filled"), sem("sc_read")
        pv_done, o_read = sem("pv_done"), sem("o_read")
        m_first, m_ready = sem("m_first"), sem("m_ready")
        recip_ready = sem("recip_ready")

        UPS = 8
        sc_no = lambda g, u, t: (g.n * UPS + u) * NT + t
        mx_no = lambda g, b, k: (g.n * GB + b) * MT_PER_B + k
        def prev_unit(g, u):
            return (g, u - 1) if u else (g + -1, UPS - 1)

        def jobs_at(g, u, place, engines_jobs=None):
            return [(k, j) for k, j in enumerate(jobs) if j[:2] == (u, place) and job_runs(g, j)
                    and (engines_jobs is None or j[2] in engines_jobs)]

        ON_ACT = ("QP", "KP", "CX", "MT", "FT")
        ON_DVE = ("XT", "VP", "OB", "AT", "OP")

        block = c.enter_context(nc.Block())

        @block.sync
        def _(sp):
            def step(g):
                p, g1, g2, g3, gm = g.par, g + 1, g + 2, g + 3, g + -1
                if g.exists:
                    wait_apart(sp, misc_emptied, job_done(g + -2, "OP"), passed)
                    sp.dma_start(res_t[p][:], x_v[g.n]).then_inc(res_loaded[p], 16)
                for gl in [g3]:
                    if gl.exists:
                        q = gl.par
                        wait_apart(sp, normed, gl.n - 1, passed)
                        sp.dma_start(x_t[q][:], x_v[gl.n]).then_inc(x_loaded[q], 16)
                        if first:
                            wait_apart(sp, misc_filled, job_done(gl + -2, "FT"), passed)
                            sp.dma_start(side_t[q][:], side_v[gl.n]).then_inc(side_loaded[q], 16)
                            wait_apart(sp, v_ctx_ready, gl.n - 1, passed)
                            wait_apart(sp, ctx_ordered, gl.n - 1, passed)
                        else:
                            wait_apart(sp, misc_filled, job_done(gl + -2, "FT"), passed)
                        sp.dma_start(ctx_t[q][:], ctx_v[gl.n]).then_inc(ctx_loaded[q], 16)
                if g2.exists:
                    if g.exists:
                        for b in range(GB):
                            wait_apart(sp, st_loaded[p][b], (g.pair + 1) * 16 * (NPART + 1), passed)
                    wait_apart(sp, k_split, g2.n + 1, passed)
                    sp.dma_start(k_scr[p].rearrange("b a r s -> r (b a) s"),
                                 k_parts[:].rearrange("r b a s -> r (b a) s")).then_inc(k_written, 16)
                if gm.exists:
                    wait_apart(sp, misc_emptied, job_done(gm, "OP"), passed)
                    sp.dma_start(xo_v[gm.n], out_t[gm.par][:]).then_inc(stored[gm.par], 16)
                if g2.exists:
                    if isinstance(g.pair, int) and g.n == -2:
                        sp.wait_ge(stack_cleared, 4)
                        sp.wait_ge(q_cleared, 2)

                    def slot_free(b):
                        if g.exists:
                            wait_apart(sp, sc_filled, sc_no(g, 2 * b + 1, NT - 1) + 1, passed)

                    def load_k(b):
                        sp.dma_start(
                            k_st[p][0:TERM_ROWS, b].rearrange("r h s -> r (h s)"),
                            k_scr[p, b].rearrange("a (d h) s -> (a d) (h s)", d=DH).unsqueeze(0)
                            .to_broadcast([NPART, NPART * DH, H * NK])).then_inc(st_loaded[p][b], 16)
                    wait_apart(sp, k_written, (g2.n + 1) * 16, passed)
                    for b in range(2):
                        slot_free(b)
                        load_k(b)
                    wait_apart(sp, q_split, g2.n + 1, passed)
                    sp.dma_start(q_scr[p].rearrange("b a r s -> r (b a) s"),
                                 q_parts[:].rearrange("r b a s -> r (b a) s")).then_inc(q_written, 16)
                    wait_apart(sp, q_written, (g2.n + 1) * 16, passed)
                    for b in range(GB):
                        if b >= 2:
                            slot_free(b)
                            load_k(b)
                        for a in range(NPART):
                            rows = slice(a * NPART * DH, (a + 1) * NPART * DH)
                            sp.dma_start(
                                q_st[p][rows, b].rearrange("r h s -> r (h s)"),
                                q_scr[p, b, a].rearrange("(d h) s -> d (h s)", d=DH).unsqueeze(0)
                                .to_broadcast([NPART, DH, H * S])).then_inc(st_loaded[p][b], 16)
            run_steps(sp, step)
            sp.wait_ge(stored[0], NG // 2 * 16)
            sp.wait_ge(stored[1], NG // 2 * 16)

        @block.gpsimd
        def _(pool):
            def split(src, parts, done, links):
                r = rem[:, :, 0:src.shape[-1]]
                nc.gpsimd.tensor_tensor(r, src, parts[:, :, 0], ALU.subtract).then_inc(split_step, 1)
                wait_apart(pool, split_step, links + 1, passed)
                nc.gpsimd.tensor_copy(parts[:, :, 1], r).then_inc(split_step, 1)
                wait_apart(pool, split_step, links + 2, passed)
                nc.gpsimd.tensor_tensor(parts[:, :, 2], r, parts[:, :, 1], ALU.subtract).then_inc(done, 1)
            for p in range(2):
                for i, (r0, r1, v) in enumerate(((64, SHIFT_ROW, 0), (SHIFT_ROW, STACK_ROWS, ONE_ONE))):
                    nc.gpsimd.memset(k_st[p][r0:r1].rearrange("r b h s -> r (b h s)").bitcast(I32), v).then_inc(stack_cleared, 1)
                    pool.wait_ge(stack_cleared, 2 * p + i + 1)

            def step(g):
                g1, g2, g3 = g + 1, g + 2, g + 3
                if g1.exists and first:
                    wait_apart(pool, pv_done, (g1.n - 1) * UPS, passed)
                    wait_apart(pool, ctx_loaded[g1.par], (g1.pair + 1) * 16, passed)
                    nc.gpsimd.tensor_copy(
                        v_t[1][g1.par][:, :, :, 0:DH],
                        ctx_t[g1.par][:].rearrange("s b (h d) -> s b h d", d=DH)).then_inc(v_ctx_ready, 1)
                if g2.exists:
                    wait_apart(pool, q_split, g2.n, passed)
                    wait_apart(pool, misc_emptied, job_done(g2, "CX" if first else "KP"), passed)
                    split(kf[:], k_parts, k_split, g2.n * 4)
                if g3.exists:
                    wait_apart(pool, aggregated, g3.n + 1, passed)
                    nc.gpsimd.tensor_scalar(rstd[:], mv[:, :, 1], EPS, None, ALU.add).then_inc(eps_added, 1)
                    wait_apart(pool, eps_added, g3.n + 1, passed)
                    nc.gpsimd.tensor_tensor(rstd[:], rstd[:], half_neg[:], ALU.pow).then_inc(rstd_ready, 1)
                if g2.exists:
                    wait_apart(pool, misc_emptied, job_done(g2, "QP"), passed)
                    wait_apart(pool, k_split, g2.n + 1, passed)
                    split(qf[:], q_parts, q_split, g2.n * 4 + 2)
                if g.exists:
                    wait_apart(pool, res_loaded[g.par], (g.pair + 1) * 16, passed)
                    r = res_t[g.par]
                    nc.gpsimd.tensor_tensor(r[:], r[:], bo_bc[:].unsqueeze(1).to_broadcast([S, GB, D]),
                                            ALU.add).then_inc(res_ready, 1)
            run_steps(pool, step)

        @block.scalar
        def _(act):
            def evac(g, k, job):
                _, _, name, b = job
                gj = g + job_group(*job)
                act.wait_ge(misc_filled, job_no(g, k) + 1)
                n0 = KEYS[0]
                by_batch = lambda n: misc[:, 0:GB * n].rearrange("r (b s) -> r b s", b=GB)
                if name == "FT":
                    ins = nc.scalar.copy(srcT[gj.par][:], by_batch(n0))
                elif name == "QP":
                    wait(act, q_split, gj.n)
                    wait(act, q_written, gj.n * 16)
                    for dst in (qf[:], q_parts[:, :, 0]):
                        ins = nc.scalar.activation(dst, by_batch(S), ACT.Identity, bias=bq[:], scale=float(DH) ** -0.5)
                elif name == "KP":
                    wait(act, k_split, gj.n)
                    wait(act, k_written, gj.n * 16)
                    for dst in (kf[:, :, 0:n0], k_parts[:, :, 0, 0:n0]):
                        ins = nc.scalar.activation(dst, by_batch(n0), ACT.Identity, bias=bk[:], scale=1.0)
                elif name == "CX":
                    wait(act, k_split, gj.n)
                    wait(act, k_written, gj.n * 16)
                    for dst in (kf[:, :, S:], k_parts[:, :, 0, S:]):
                        ins = nc.scalar.copy(dst, by_batch(SC))
                elif name == "MT":
                    pr = b // 2
                    if (gj + -1).exists:
                        act.wait_ge(shift_loaded[(gj + -1).par][pr], ((gj + -1).pair + 1) * 32)
                    ins = nc.scalar.copy(mT[pr][:], misc_bf)
                ins.then_inc(misc_emptied, 1)

            def send_shifts(gj, pr):
                act.wait_ge(misc_emptied, job_done(gj, "MT", 2 * pr))
                for r in range(2):
                    act.dma_start(q_st[gj.par][SHIFT_ROW + r:SHIFT_ROW + r + 1, 2 * pr:2 * pr + 2],
                                  mT[pr][r * 2 * H:(r + 1) * 2 * H, :]).then_inc(shift_loaded[gj.par][pr], 16)

            def order_context(g2):
                act.wait_ge(ctx_loaded[g2.par], (g2.pair + 1) * 16)
                wait(act, misc_filled, job_done(g2 + -1, "CX"))
                for b in range(GB):
                    last = nc.scalar.copy(ctx_o[:, b].rearrange("s (d h) -> s d h", d=DH),
                                          ctx_t[g2.par][:, b].rearrange("s (h d) -> s d h", d=DH))
                last.then_inc(ctx_ordered, 1)

            def exponent(g, u, t):
                act.wait_ge(sc_filled, sc_no(g, u, t) + 1)
                wait(act, pv_done, g.n * UPS + u - 1)
                nc.scalar.activation(p_t[t][u % 2][:], ps_sc[(u * NT + t) % 2][0:KEYS[t], :],
                                     ACT.Exp).then_inc(sc_read, 1)

            def step(g):
                for u in range(UPS):
                    for place in range(3):
                        for k, j in jobs_at(g, u, place, ON_ACT):
                            evac(g, k, j)
                        if place < NT and g.exists:
                            exponent(g, u, place)
                        if first and (u, place) == (0, 1) and (g + 2).exists:
                            order_context(g + 2)
                        if (u, place) == (1, 0) and g.exists:
                            send_shifts(g, 1)
                        if (u, place) == (5, 0) and (g + 1).exists:
                            send_shifts(g + 1, 0)
                    gp, up = prev_unit(g, u)
                    if u % 2 == 0 and gp.exists:
                        act.wait_ge(pv_done, gp.n * UPS + up + 1)
                        wait(act, recip_ready, gp.n * GB + up // 2)
                        nc.scalar.copy(o_sb[:], ps_o[:]).then_inc(o_read, 1)
            run_steps(act, step)

        @block.vector
        def _(dve):
            for p in range(2):
                nc.vector.memset(q_st[p][64:SHIFT_ROW].rearrange("r b h s -> r (b h s)").bitcast(I32), 0).then_inc(q_cleared, 1)
                for t in range(NT):
                    nc.vector.memset(v_t[t][p][:, :, :, DH:DH + 1], 1.0)
            nc.vector.memset(ps_o[:], 0.0).then_inc(o_read, 1)

            def evac(g, k, job):
                _, _, name, b = job
                gj = g + job_group(*job)
                dve.wait_ge(misc_filled, job_no(g, k) + 1)
                if name == "XT":
                    nc.vector.tensor_copy(xnT[:], misc[:]).then_inc(misc_emptied, 1)
                elif name == "VP":
                    n = KEYS[0]
                    wait(dve, pv_done, (gj.n - 1) * UPS)
                    nc.vector.tensor_tensor(
                        v_t[0][gj.par][:, :, :, 0:DH],
                        misc[0:n, :].rearrange("s (b h d) -> s b h d", b=GB, d=DH),
                        bv_bc[0:n].rearrange("s (h d) -> s h d", d=DH).unsqueeze(1).to_broadcast([n, GB, H, DH]),
                        ALU.add).then_inc(misc_emptied, 1)
                elif name == "OB":
                    o_v = misc[:].rearrange("q (h c) -> q h c", c=32)
                    nc.vector.reciprocal(rden[:], o_v[:, :, DH]).then_inc(recip_ready, 1)
                    dve.wait_ge(recip_ready, gj.n * GB + b + 1)
                    nc.vector.tensor_tensor(att[:, b], o_v[:, :, 0:DH], rden[:].unsqueeze(2).to_broadcast([S, H, DH]),
                                            ALU.mult).then_inc(misc_emptied, 1)
                elif name == "AT":
                    nc.vector.tensor_copy(attT[:], misc[:]).then_inc(misc_emptied, 1)
                elif name == "OP":
                    dve.wait_ge(res_ready, gj.n + 1)
                    wait(dve, stored[gj.par], gj.pair * 16)
                    nc.vector.tensor_tensor(out_t[gj.par][:].rearrange("s b d -> s (b d)"), misc[:],
                                            res_t[gj.par][:].rearrange("s b d -> s (b d)"), ALU.add).then_inc(misc_emptied, 1)

            def statistics(g3):
                dve.wait_ge(x_loaded[g3.par], (g3.pair + 1) * 16)
                for b in range(GB):
                    nc.vector.bn_stats(stats[:, b], x_t[g3.par][:, b]).then_inc(stats_ready, 1)
                wait_apart(dve, stats_ready, (g3.n + 1) * GB, passed)
                for b in range(GB):
                    last = nc.vector.bn_aggr(mv[:, b], stats[:, b])
                last.then_inc(aggregated, 1)

            def normalise(g3):
                dve.wait_ge(rstd_ready, g3.n + 1)
                wait(dve, misc_filled, job_done(g3 + -1, "XT"))
                for b in range(GB):
                    last = nc.vector.tensor_scalar(xn[:, b], x_t[g3.par][:, b], mv[:, b, 0:1], rstd[:, b:b + 1],
                                                   ALU.subtract, ALU.mult)
                last.then_inc(normed, 1)

            def row_maxima(g1, b, kk):
                dve.wait_ge(max_filled, mx_no(g1, b, kk) + 1)
                v = ps_mx[kk % 2][:, 0:HPB * NK].rearrange("q (h s) -> q h s", h=HPB)
                nc.vector.tensor_reduce(neg_max[:, b, kk * HPB:(kk + 1) * HPB], v, AX.X, ALU.max,
                                        negate=True).then_inc(max_read, 1)

            def shift_parts(g1, pr):
                dve.wait_ge(max_read, mx_no(g1, 2 * pr + 1, MT_PER_B - 1) + 1)
                wait(dve, misc_filled, job_done(g1 + -1, "MT", 2 * pr))
                mp, m = m_parts[pr], neg_max[:, 2 * pr:2 * pr + 2]
                nc.vector.tensor_copy(mp[:, 0], m).then_inc(m_first, 1)
                dve.wait_ge(m_first, g1.n * 2 + pr + 1)
                nc.vector.tensor_tensor(mp[:, 1], m, mp[:, 0], ALU.subtract).then_inc(m_ready, 1)

            def step(g):
                g1, g3 = g + 1, g + 3
                for u in range(UPS):
                    if u == 7 and g3.exists:
                        normalise(g3)
                    for what, i in UNIT:
                        if what == "job":
                            for k, j in jobs_at(g, u, i, ON_DVE):
                                evac(g, k, j)
                        elif what == "max" and g1.exists:
                            row_maxima(g1, u // 2, (u % 2) * MT_PER_U + i)
                    if u % 4 == 3 and g1.exists:
                        shift_parts(g1, u // 4)
                    if u == 2 and g3.exists:
                        statistics(g3)
            run_steps(dve, step)

        @block.tensor
        def _(pe):
            mm = nc.tensor.matmul

            def fill(g, k, job):
                _, _, name, b = job
                gj = g + job_group(*job)
                if name == "MT":
                    wait_apart(pe, m_ready, gj.n * 2 + b // 2 + 1, passed)
                    wait_apart(pe, misc_emptied, job_no(g, k), passed)
                else:
                    wait(pe, misc_emptied, job_no(g, k))
                if name == "XT":
                    pe.wait_ge(normed, gj.n + 1)
                    for j in range(GB):
                        last = nc.tensor.transpose(misc[:, j * S:(j + 1) * S], xn[:, j], ident[:])
                elif name == "QP":
                    last = mm(misc[:], wq[:], xnT[:], start=True, stop=True)
                elif name == "FT":
                    n = KEYS[0]
                    if first:
                        pe.wait_ge(side_loaded[gj.par], (gj.pair + 1) * 16)
                    else:
                        pe.wait_ge(ctx_loaded[gj.par], (gj.pair + 1) * 16)
                    src = side_t if first else ctx_t
                    for j in range(GB):
                        last = nc.tensor.transpose(misc[:, j * n:(j + 1) * n], src[gj.par][:, j], ident[0:n, 0:n])
                elif name == "KP":
                    n = GB * KEYS[0]
                    last = mm(misc[:, 0:n], wk[:], srcT[gj.par][:].rearrange("d b s -> d (b s)"), start=True, stop=True)
                elif name == "CX":
                    pe.wait_ge(ctx_ordered, gj.n + 1)
                    for j in range(GB):
                        last = nc.tensor.transpose(misc[:, j * SC:(j + 1) * SC], ctx_o[:, j], ident[0:SC, 0:SC])
                elif name == "VP":
                    n = KEYS[0]
                    for j in range(GB):
                        last = mm(misc[0:n, j * D:(j + 1) * D], srcT[gj.par][:, j], wv[:], start=True, stop=True)
                elif name == "MT":
                    last = nc.tensor.transpose(misc_bf, m_parts[b // 2][:].rearrange("q r i h -> q (r i h)"), ident_bf[:])
                elif name == "OB":
                    pe.wait_ge(o_read, gj.n * GB + b + 2)
                    for j in range(4):
                        last = nc.tensor.transpose(misc[:, j * S:(j + 1) * S], o_sb[:, j * S:(j + 1) * S], ident[:])
                elif name == "AT":
                    for j in range(GB):
                        last = nc.tensor.transpose(misc[:, j * S:(j + 1) * S], att[:, j].rearrange("q h d -> q (h d)"), ident[:])
                elif name == "OP":
                    for j in range(GB):
                        last = mm(misc[:, j * D:(j + 1) * D], attT[:, j * S:(j + 1) * S], wo[:], start=True, stop=True)
                last.then_inc(misc_filled, 1)

            def scores(g, u, t):
                b, hf, p = u // 2, u % 2, g.par
                i = sc_no(g, u, t)
                if t == 0 and hf == 0 and b % 2 == 0:
                    pe.wait_ge(shift_loaded[p][b // 2], (g.pair + 1) * 32)
                wait(pe, sc_read, i - 1)
                k0 = sum(KEYS[:t])
                out = ps_sc[(u * NT + t) % 2]
                for j in range(HALF):
                    h = hf * HALF + j
                    last = mm(out[0:KEYS[t], j * S:(j + 1) * S], k_st[p][:, b, h, k0:k0 + KEYS[t]], q_st[p][:, b, h, :],
                              start=True, stop=True)
                last.then_inc(sc_filled, 1)

            def max_tile(g, b, k):
                p = g.par
                i = mx_no(g, b, k)
                if k == 0:
                    pe.wait_ge(st_loaded[p][b], (g.pair + 1) * 16 * (NPART + 1))
                wait(pe, max_read, i - 1)
                for j in range(HPB):
                    h = k * HPB + j
                    last = mm(ps_mx[k % 2][:, j * NK:(j + 1) * NK], q_st[p][0:SHIFT_ROW, b, h, :],
                              k_st[p][0:SHIFT_ROW, b, h, :], start=True, stop=True)
                last.then_inc(max_filled, 1)

            def weighted_values(g, u, quarter):
                b, hf, p = u // 2, u % 2, g.par
                if u == 0 and quarter == 0:
                    pe.wait_ge(misc_emptied, job_done(g, "VP"))
                    if first:
                        pe.wait_ge(v_ctx_ready, g.n + 1)
                pe.wait_ge(sc_read, sc_no(g, u, NT - 1) + 1)
                if hf == 0 and quarter == 0:
                    pe.wait_ge(o_read, g.n * GB + b + 1)
                for t in range(NT):
                    for j in range(quarter * 4, quarter * 4 + 4):
                        h = hf * HALF + j
                        r, col = 32 * (h % 4), (h // 4) * S
                        last = mm(ps_o[r:r + DH + 1, col:col + S], v_t[t][p][:, b, h, :],
                                  p_t[t][u % 2][:, j * S:(j + 1) * S], start=(t == 0), stop=(t == NT - 1))
                if quarter == 1:
                    last.then_inc(pv_done, 1)

            def step(g):
                g1 = g + 1
                for u in range(UPS):
                    gp, up = prev_unit(g, u)
                    for what, i in UNIT:
                        if what == "job":
                            for k, j in jobs_at(g, u, i):
                                fill(g, k, j)
                        elif what == "scores" and g.exists:
                            scores(g, u, i)
                        elif what == "max" and g1.exists:
                            max_tile(g1, u // 2, (u % 2) * MT_PER_U + i)
                        elif what == "values" and gp.exists:
                            weighted_values(gp, up, i)
            run_steps(pe, step)


def diagonal(nc, pool, t, cleared, done):
    nc.gpsimd.memset(t[:], 0.0).then_inc(cleared, 1)
    pool.wait_ge(cleared, 1)
    nc.gpsimd.affine_select(out=t[:], in_=t[:], compare_op=ALU.not_equal, fill=1.0, base=0,
                            pattern=[[-1, t.shape[-1]]], channel_multiplier=1).then_inc(done, 1)


def attention_consts(nc, c, weights, layer):
    Wq, bq_d, Wk, bk_d, Wv, bv_d, Wo, bo_d = weights
    first = layer == 0
    tag = f"C{layer}_"
    sb = lambda name, shape, dt=F32: c.enter_context(nc.sbuf_tensor(tag + name, shape, dt))
    ident, ident_bf = sb("ident", [128, 128]), sb("ident_bf", [128, 128], BF16)
    ready = [sb(n, [D, D]) for n in ("wq", "wk", "wv", "wo")]
    bq, bk = sb("bq", [D, 1]), sb("bk", [D, 1])
    bv_bc, bo_bc, half_neg = sb("bv_bc", [S, D]), sb("bo_bc", [S, D]), sb("half_neg", [S, GB])
    with ExitStack() as p:
        raw = [p.enter_context(nc.sbuf_tensor(tag + "raw_" + n, [D, D], F32)) for n in "qkvo"]
        bq_raw = p.enter_context(nc.sbuf_tensor(tag + "bq_raw", [D, 1], F32))
        ps = p.enter_context(nc.psum_tensor(tag + "ps", [D, 4, D], F32))
        sem = p.enter_context(phase_semaphores(nc, tag))
        loaded, cleared, made, turned, done = (sem(n) for n in
                                               ("loaded", "cleared", "made", "turned", "done"))
        block = p.enter_context(nc.Block())

        @block.sync
        def _(sp):
            for t, w in zip(raw, (Wq, Wk, Wv, Wo)):
                sp.dma_start(t[:], w).then_inc(loaded, 16)
            for t, w in ((bq_raw, bq_d), (bk, bk_d)):
                for d in range(DH):
                    sp.dma_start(t[d * H:(d + 1) * H, :], w.rearrange("(h d one) -> d h one", d=DH, one=1)[d],
                                 allow_slow_non_contiguous=True).then_inc(loaded, 16)
            for t, w in ((bv_bc, bv_d), (bo_bc, bo_d)):
                sp.dma_start(t[:], w.unsqueeze(0).to_broadcast([S, D])).then_inc(loaded, 16)

        @block.gpsimd
        def _(pool):
            nc.gpsimd.memset(half_neg[:], -0.5)
            diagonal(nc, pool, ident, cleared, made)

        @block.tensor
        def _(pe):
            pe.wait_ge(loaded, 16 * 22)
            pe.wait_ge(made, 1)
            if not first:
                for i in range(4):
                    last = nc.tensor.transpose(ps[:, i], raw[i][:], ident[:])
                last.then_inc(turned, 1)

        @block.vector
        def _(dve):
            dve.wait_ge(loaded, 16 * 22)
            dve.wait_ge(made, 1)
            nc.vector.tensor_copy(ident_bf[:], ident[:])
            nc.vector.tensor_scalar(bq[:], bq_raw[:], float(DH) ** -0.5, None, ALU.mult)
            if not first:
                dve.wait_ge(turned, 1)
            for i in range(4):
                src = raw[i][:] if first else ps[:, i]
                if i < 2:
                    src = src.rearrange("r (h d) -> r d h", d=DH)
                    last = nc.vector.tensor_copy(ready[i][:].rearrange("r (d h) -> r d h", d=DH), src)
                else:
                    last = nc.vector.tensor_copy(ready[i][:], src)
            last.then_inc(done, 1)
            dve.wait_ge(done, 1)
    return (ident, ident_bf, *ready, bq, bk, bv_bc, bo_bc, half_neg)


TOKENS = B * S
F = 352
TOP = 2
REGION = TOKENS + S
TILES = (TOKENS * TOP // S + E) // 2 * 2
SPARE = E * REGION
ROUTED_ROWS = SPARE + E * S
FCHUNKS = [(0, 128), (128, 128), (256, F - 256)]
G_STEPS = 2 * NPART


def loop_groups(eng, step, lead):
    for n in range(-2, 2):
        step(Group(n // 2, n % 2))
    with eng.Fori(1, NG // 2 - 1) as pair:
        step(Group(pair, 0))
        step(Group(pair, 1))
    for n in range(NG - 2, NG + 2):
        step(Group(n // 2, n % 2))


def route_tokens(nc, x1, xs, wqkv, keep):
    slots_all, gates_all, tile_row, tile_expert = keep
    x_v = x1.rearrange("(n b) s d -> n s b d", b=GB)
    with ExitStack() as c:
        sb = lambda name, shape, dt=F32: c.enter_context(nc.sbuf_tensor("R_" + name, shape, dt))
        pb = lambda name, shape, dt=F32: c.enter_context(nc.psum_tensor("R_" + name, shape, dt))
        sem = c.enter_context(phase_semaphores(nc, "R_"))
        two = lambda f: [f(0), f(1)]
        ident = sb("ident", [128, 128])
        before, ones = sb("before", [128, 128], BF16), sb("ones", [128, 128], BF16)
        zeros = sb("zeros", [128, D])
        half_neg = sb("half_neg", [S, GB])
        iota_e, iota_ei = sb("iota_e", [S, E]), sb("iota_ei", [S, E], I32)
        iota_t, iota_ti = sb("iota_t", [1, TILES]), sb("iota_ti", [1, TILES], I32)
        w_raw, wT = sb("w_raw", [3 * E, D]), sb("wT", [D, 3 * E])
        x_t = two(lambda p: sb(f"x{p}", [S, GB, D]))
        xn = two(lambda p: sb(f"xn{p}", [S, GB, D]))
        stats, mv, rstd = sb("stats", [S, GB, 6]), sb("mv", [S, GB, 2]), sb("rstd", [S, GB])
        xnT = sb("xnT", [D, GB, S])
        qkv = sb("qkv", [S, GB, 3 * E])
        pr, prv, pe_ = (sb(n, [S, GB, E, E]) for n in ("pr", "prv", "pexp"))
        mx, sm, lv, lg = (sb(n, [S, GB, E]) for n in ("mx", "sm", "lv", "lg"))
        top, top_i = sb("top", [S, GB, 8]), sb("top_i", [S, GB, 8], mybir.dt.uint32)
        idx_f, diff, e2, den = sb("idx_f", [S, GB, TOP]), sb("diff", [S, GB]), sb("e2", [S, GB]), sb("den", [S, GB])
        g0 = sb("g0", [S, GB])
        oh, ohp = sb("oh", [S, GB, TOP, E]), sb("ohp", [S, GB, TOP, E])
        hits = sb("hits", [S, GB, E], BF16)
        base, pos = sb("base", [S, GB, E]), sb("pos", [S, GB, E])
        count, region0 = sb("count", [S, E]), sb("region0", [S, E])
        slot_f = sb("slot_f", [S, GB, TOP])
        slots_f, crossed = sb("slots_f", [S, NG * GB * TOP]), sb("crossed", [S, NG * GB * TOP, E - 1])
        moved = sb("moved", [S, NG * GB * TOP])
        slot = two(lambda p: sb(f"slot{p}", [S, GB, TOP], mybir.dt.uint32))
        nf, ni, nt_i, ntf, te, delta = (sb(n, [S, E], dt) for n, dt in
            (("nf", F32), ("ni", I32), ("nt_i", I32), ("ntf", F32), ("te", F32), ("delta", F32)))
        end_row = sb("end_row", [1, E], I32)
        tmask, tm2 = sb("tmask", [1, TILES, E]), sb("tm2", [1, TILES, E])
        tef, trf = sb("tef", [1, TILES]), sb("trf", [1, TILES])
        ps_x, ps_q, ps_r = pb("ps_x", [D, GB, S]), pb("ps_q", [S, GB, 3 * E]), pb("ps_r", [S, 2, GB, E])

        w_loaded, made, cleared, consts_ready = sem("w_loaded"), sem("made"), sem("cleared"), sem("consts_ready")
        x_loaded = two(lambda p: sem(f"x_loaded{p}"))
        stats_ready, aggregated, rstd_ready, eps_added, normed = (sem(n) for n in
            ("stats_ready", "aggregated", "rstd_ready", "eps_added", "normed"))
        w_turned, wT_ready = sem("w_turned"), sem("wT_ready")
        x_turned, xT_ready, projected, qkv_ready = sem("x_turned"), sem("xT_ready"), sem("projected"), sem("qkv_ready")
        shifted, exp_ready, gap_ready, e2_ready = sem("shifted"), sem("exp_ready"), sem("gap_ready"), sem("e2_ready")
        hits_ready, counted, order = sem("hits_ready"), sem("counted"), sem("order")
        slot_ready = sem("slot_ready")
        scattered = two(lambda p: sem(f"scattered{p}"))
        table_ready, zeroed, passed = sem("table_ready"), sem("zeroed"), sem("passed")
        ORDER = 21

        block = c.enter_context(nc.Block())

        @block.sync
        def _(sp):
            sp.dma_start(w_raw[:], wqkv).then_inc(w_loaded, 16)

            def step(g):
                gl = g + 2
                if gl.exists:
                    wait_apart(sp, normed, gl.n - 1, passed)
                    sp.dma_start(x_t[gl.par][:], x_v[gl.n]).then_inc(x_loaded[gl.par], 16)
            loop_groups(sp, step, 2)
            sp.wait_ge(made, 3)
            for k in range(E):
                sp.dma_start(xs[SPARE + k * S:SPARE + (k + 1) * S], zeros[:]).then_inc(zeroed, 16)
            sp.wait_ge(table_ready, 1)
            for e in range(E):
                row = sp.value_load(end_row[0:1, e:e + 1], min_val=e * REGION, max_val=e * REGION + TOKENS)
                sp.dma_start(xs[bass.ds(row, S)], zeros[:]).then_inc(zeroed, 16)
            sp.wait_ge(zeroed, 2 * E * 16)

        @block.gpsimd
        def _(pool):
            n = [0]

            def done(ins):
                n[0] += 1
                ins.then_inc(cleared, 1)
                pool.wait_ge(cleared, n[0])
            done(nc.gpsimd.memset(half_neg[:], -0.5))
            done(nc.gpsimd.memset(ident[:], 0.0))
            nc.gpsimd.affine_select(out=ident[:], in_=ident[:], compare_op=ALU.not_equal, fill=1.0, base=0,
                                    pattern=[[-1, 128]], channel_multiplier=1).then_inc(made, 1)
            done(nc.gpsimd.memset(ones[:], 1.0))
            nc.gpsimd.affine_select(out=before[:], in_=ones[:], compare_op=ALU.is_gt, fill=0.0, base=0,
                                    pattern=[[1, 128]], channel_multiplier=-1).then_inc(made, 1)
            nc.gpsimd.memset(zeros[:], 0.0).then_inc(made, 1)
            done(nc.gpsimd.iota(iota_ei[:], pattern=[[1, E]], base=0, channel_multiplier=0))
            done(nc.gpsimd.iota(iota_ti[:], pattern=[[1, TILES]], base=0, channel_multiplier=0))
            done(nc.gpsimd.tensor_copy(iota_e[:], iota_ei[:]))
            done(nc.gpsimd.tensor_copy(iota_t[:], iota_ti[:]))
            done(nc.gpsimd.tensor_scalar(region0[:], iota_e[:], float(REGION), None, ALU.mult))
            nc.gpsimd.tensor_copy(count[:], region0[:]).then_inc(consts_ready, 1)

            def step(g):
                g1 = g + 1
                if g1.exists:
                    wait_apart(pool, aggregated, g1.n + 1, passed)
                    nc.gpsimd.tensor_scalar(rstd[:], mv[:, :, 1], EPS, None, ALU.add).then_inc(eps_added, 1)
                    wait_apart(pool, eps_added, g1.n + 1, passed)
                    nc.gpsimd.tensor_tensor(rstd[:], rstd[:], half_neg[:], ALU.pow).then_inc(rstd_ready, 1)
                if g.exists:
                    wait_apart(pool, slot_ready, g.n + 1, passed)
                    for b in range(GB):
                        for k in range(TOP):
                            nc.gpsimd.indirect_dma_start(
                                out=xs, out_offset=bass.IndirectOffsetOnAxis(ap=slot[g.par][:, b, k:k + 1], axis=0),
                                in_=xn[g.par][:, b], in_offset=None).then_inc(scattered[g.par], 16)
            loop_groups(pool, step, 1)
            for p in range(2):
                pool.wait_ge(scattered[p], NG // 2 * GB * TOP * 16)

        @block.tensor
        def _(pe):
            pe.wait_ge(w_loaded, 16)
            pe.wait_ge(made, 3)
            nc.tensor.transpose(ps_x[:, 0, 0:3 * E], w_raw[:], ident[0:3 * E, 0:3 * E]).then_inc(w_turned, 1)
            pe.wait_ge(wT_ready, 1)

            def step(g):
                g1 = g + 1
                if g1.exists:
                    wait(pe, normed, g1.n + 1)
                    wait(pe, xT_ready, g1.n)
                    for b in range(GB):
                        last = nc.tensor.transpose(ps_x[:, b], xn[g1.par][:, b], ident[:])
                    last.then_inc(x_turned, 1)
                    pe.wait_ge(xT_ready, g1.n + 1)
                    wait(pe, qkv_ready, g1.n)
                    for b in range(GB):
                        last = nc.tensor.matmul(ps_q[:, b], xnT[:, b], wT[:], start=True, stop=True)
                    last.then_inc(projected, 1)
                if g.exists:
                    pe.wait_ge(hits_ready, g.n + 1)
                    h = hits[:].rearrange("s b e -> s (b e)")
                    nc.tensor.matmul(ps_r[:, 0].rearrange("s b e -> s (b e)"), before[:], h, start=True, stop=True)
                    nc.tensor.matmul(ps_r[:, 1].rearrange("s b e -> s (b e)"), ones[:], h,
                                     start=True, stop=True).then_inc(counted, 1)
            loop_groups(pe, step, 1)

        @block.scalar
        def _(act):
            act.wait_ge(w_turned, 1)
            nc.scalar.copy(wT[:], ps_x[:, 0, 0:3 * E]).then_inc(wT_ready, 1)

            def ordered(g):
                g1 = g + 1
                if g.exists:
                    act.wait_ge(shifted, g.n + 1)
                    nc.scalar.activation(pe_[:], pr[:], ACT.Exp).then_inc(exp_ready, 1)
                    act.wait_ge(gap_ready, g.n + 1)
                    nc.scalar.activation(e2[:], diff[:], ACT.Exp).then_inc(e2_ready, 1)
                if g1.exists:
                    act.wait_ge(x_turned, g1.n + 1)
                    wait(act, projected, g1.n)
                    nc.scalar.copy(xnT[:], ps_x[:]).then_inc(xT_ready, 1)
                    act.wait_ge(projected, g1.n + 1)
                    nc.scalar.copy(qkv[:], ps_q[:]).then_inc(qkv_ready, 1)
            loop_groups(act, ordered, 1)

        @block.vector
        def _(dve):
            v = nc.vector
            dve.wait_ge(consts_ready, 1)

            def step(g):
                g1 = g + 1
                if g1.exists:
                    wait_apart(dve, x_loaded[g1.par], (g1.pair + 1) * 16, passed)
                    for b in range(GB):
                        v.bn_stats(stats[:, b], x_t[g1.par][:, b]).then_inc(stats_ready, 1)
                    wait_apart(dve, stats_ready, (g1.n + 1) * GB, passed)
                    for b in range(GB):
                        last = v.bn_aggr(mv[:, b], stats[:, b])
                    last.then_inc(aggregated, 1)
                    wait_apart(dve, rstd_ready, g1.n + 1, passed)
                    wait_apart(dve, scattered[g1.par], g1.pair * GB * TOP * 16, passed)
                    for b in range(GB):
                        last = v.tensor_scalar(xn[g1.par][:, b], x_t[g1.par][:, b], mv[:, b, 0:1], rstd[:, b:b + 1],
                                               ALU.subtract, ALU.mult)
                    last.then_inc(normed, 1)
                if not g.exists:
                    return
                links = [0]

                def link(ins):
                    links[0] += 1
                    ins.then_inc(order, 1)
                    wait_apart(dve, order, g.n * ORDER + links[0], passed)
                full = [S, GB, E, E]
                q, k, val = (qkv[:, :, i * E:(i + 1) * E] for i in range(3))
                wait_apart(dve, qkv_ready, g.n + 1, passed)
                link(v.tensor_tensor(pr[:], q.unsqueeze(3).to_broadcast(full), k.unsqueeze(2).to_broadcast(full), ALU.mult))
                link(v.tensor_reduce(mx[:], pr[:], AX.X, ALU.max))
                v.tensor_tensor(pr[:], pr[:], mx[:].unsqueeze(3).to_broadcast(full), ALU.subtract).then_inc(shifted, 1)
                wait_apart(dve, exp_ready, g.n + 1, passed)
                v.tensor_reduce(sm[:], pe_[:], AX.X, ALU.add)
                link(v.tensor_tensor(prv[:], pe_[:], val.unsqueeze(2).to_broadcast(full), ALU.mult))
                link(v.tensor_reduce(lv[:], prv[:], AX.X, ALU.add))
                link(v.reciprocal(sm[:], sm[:]))
                link(v.tensor_tensor(lg[:], lv[:], sm[:], ALU.mult))
                for b in range(GB):
                    last = v.max(top[:, b], lg[:, b])
                link(last)
                for b in range(GB):
                    last = v.max_index(top_i[:, b], top[:, b], lg[:, b])
                link(last)
                v.tensor_tensor(diff[:], top[:, :, 1], top[:, :, 0], ALU.subtract).then_inc(gap_ready, 1)
                link(v.tensor_copy(idx_f[:], top_i[:, :, 0:TOP]))
                picks = [S, GB, TOP, E]
                link(v.tensor_tensor(oh[:], iota_e[:].unsqueeze(1).unsqueeze(1).to_broadcast(picks),
                                     idx_f[:].unsqueeze(3).to_broadcast(picks), ALU.is_equal))
                v.tensor_tensor(hits[:], oh[:, :, 0], oh[:, :, 1], ALU.add).then_inc(hits_ready, 1)
                wait_apart(dve, e2_ready, g.n + 1, passed)
                link(v.tensor_scalar(den[:], e2[:], 1.0, None, ALU.add))
                link(v.reciprocal(g0[:], den[:]))
                ga = gates_all[:, bass.ds(g.n, 1)] if not isinstance(g.pair, int) else gates_all[:, g.n:g.n + 1]
                sa = slots_f[:, bass.ds(g.n * (GB * TOP), GB * TOP)]
                v.tensor_copy(ga[:, 0, :, 0], g0[:])
                v.tensor_tensor(ga[:, 0, :, 1], e2[:], g0[:], ALU.mult)
                wait_apart(dve, counted, g.n + 1, passed)
                link(v.tensor_copy(base[:, 0], count[:]))
                for b in range(GB - 1):
                    link(v.tensor_tensor(base[:, b + 1], base[:, b], ps_r[:, 1, b], ALU.add))
                v.tensor_tensor(count[:], base[:, GB - 1], ps_r[:, 1, GB - 1], ALU.add)
                link(v.tensor_tensor(pos[:], base[:], ps_r[:, 0], ALU.add))
                link(v.tensor_tensor(ohp[:], oh[:], pos[:].unsqueeze(2).to_broadcast(picks), ALU.mult))
                link(v.tensor_reduce(slot_f[:], ohp[:], AX.X, ALU.add))
                link(v.tensor_copy(sa, slot_f[:].rearrange("s b k -> s (b k)")))
                v.tensor_copy(slot[g.par][:], slot_f[:]).then_inc(slot_ready, 1)
                assert links[0] == ORDER - 2 + 1, links[0]
                link(v.tensor_copy(idx_f[:, 0, 0:1], slot_f[:, 0, 0:1]))
            loop_groups(dve, step, 1)

            at = [NG * ORDER]

            def link(ins):
                at[0] += 1
                ins.then_inc(order, 1)
                dve.wait_ge(order, at[0])
            link(v.tensor_copy(end_row[:], count[0:1]))
            link(v.tensor_tensor(nf[:], count[:], region0[:], ALU.subtract))
            link(v.tensor_scalar(ni[:], nf[:], float(S - 1), None, ALU.add))
            link(v.tensor_scalar(nt_i[:], ni[:], S.bit_length() - 1, None, ALU.logical_shift_right))
            link(v.tensor_copy(ntf[:], nt_i[:]))
            link(v.tensor_copy(te[:], ntf[:]))
            for e in range(1, E):
                link(v.tensor_tensor(te[:, e:e + 1], te[:, e - 1:e], ntf[:, e:e + 1], ALU.add))
            table = [1, TILES, E]
            link(v.tensor_tensor(tmask[:], iota_t[:].unsqueeze(2).to_broadcast(table), te[0:1].unsqueeze(1).to_broadcast(table), ALU.is_ge))
            link(v.tensor_reduce(tef[:], tmask[:], AX.X, ALU.add))
            link(v.tensor_scalar(tile_expert[:], tef[:], float(E - 1), None, ALU.min))
            link(v.tensor_scalar(delta[:], ntf[:], -float(S), float(REGION), ALU.mult, ALU.add))
            link(v.tensor_tensor(tm2[:], tmask[:], delta[0:1].unsqueeze(1).to_broadcast(table), ALU.mult))
            link(v.tensor_reduce(trf[:], tm2[:], AX.X, ALU.add))
            link(v.scalar_tensor_tensor(trf[:], iota_t[:], float(S), trf[:], ALU.mult, ALU.add))
            v.tensor_copy(tile_row[:], trf[:]).then_inc(table_ready, 1)
            each = [S, NG * GB * TOP, E - 1]
            link(v.tensor_tensor(crossed[:], slots_f[:].unsqueeze(2).to_broadcast(each),
                                 region0[:, 1:E].unsqueeze(1).to_broadcast(each), ALU.is_ge))
            link(v.tensor_tensor(crossed[:], crossed[:], delta[:, 0:E - 1].unsqueeze(1).to_broadcast(each), ALU.mult))
            link(v.tensor_reduce(moved[:], crossed[:], AX.X, ALU.add))
            link(v.tensor_tensor(slots_all[:].rearrange("s n b k -> s (n b k)"), slots_f[:], moved[:], ALU.subtract))


def expert_tiles(nc, xs, ys, w1, w2, keep):
    _, _, tile_row, tile_expert = keep
    NB1 = E * 2 * F // 128
    with ExitStack() as c:
        sb = lambda name, shape, dt=F32: c.enter_context(nc.sbuf_tensor("M_" + name, shape, dt))
        pb = lambda name, shape, dt=F32: c.enter_context(nc.psum_tensor("M_" + name, shape, dt))
        sem = c.enter_context(phase_semaphores(nc, "M_"))
        two = lambda f: [f(0), f(1)]
        ident = sb("ident", [128, 128])
        w1T, w2T = sb("w1T", [D, E * 2 * F]), sb("w2T", [128, len(FCHUNKS), E * D])
        w1_raw, w2_raw = sb("w1_raw", [128, NB1, D]), sb("w2_raw", [D, E, F])
        NX = 4
        x_t = [sb(f"x{i}", [S, D]) for i in range(NX)]
        xT = two(lambda p: sb(f"xT{p}", [D, S]))
        act_a = two(lambda p: sb(f"act_a{p}", [S, F]))
        h_t = two(lambda p: sb(f"h{p}", [S, F]))
        hT = two(lambda p: sb(f"hT{p}", [128, len(FCHUNKS), S]))
        y_t = [sb(f"y{i}", [S, D]) for i in range(NX)]
        ps_x, ps_y, ps_t = pb("ps_x", [D, 512]), pb("ps_y", [S, 512]), pb("ps_t", [128, 512])
        ps_a, ps_g = two(lambda p: pb(f"ps_a{p}", [S, 512])), two(lambda p: pb(f"ps_g{p}", [S, 512]))

        loaded, cleared, made = sem("loaded"), sem("cleared"), sem("made")
        w_turned, w_copied = sem("w_turned"), sem("w_copied")
        x_loaded = [sem(f"x_loaded{i}") for i in range(NX)]
        x_turned, xT_ready, hidden, silu_ready, h_ready, h_turned, hT_ready, y_done, y_ready = (sem(n) for n in
            ("x_turned", "xT_ready", "hidden", "silu_ready", "h_ready", "h_turned", "hT_ready", "y_done", "y_ready"))
        y_stored = [sem(f"y_stored{i}") for i in range(NX)]
        passed = sem("passed")
        block = c.enter_context(nc.Block())
        U = NX

        def run(eng, step):
            for t in range(-U, U):
                step(t, t % U, 0)
            with eng.Fori(1, TILES // U - 1) as turn:
                for i in range(U):
                    step(turn * U + i, i, turn)
            for t in range(TILES - U, TILES + U):
                step(t, t % U, 0)

        def has(t):
            return not isinstance(t, int) or 0 <= t < TILES

        def row_of(eng, t):
            cell = tile_row[0:1, t:t + 1] if isinstance(t, int) else tile_row[0:1, bass.ds(t, 1)]
            return eng.value_load(cell, min_val=0, max_val=ROUTED_ROWS - S)

        def expert_of(eng, t):
            cell = tile_expert[0:1, t:t + 1] if isinstance(t, int) else tile_expert[0:1, bass.ds(t, 1)]
            return eng.value_load(cell, min_val=0, max_val=E - 1)

        def nth(t, i):
            return (t // U + 1) * 16 if isinstance(t, int) else (t - i + U) * (16 // U)

        @block.sync
        def _(sp):
            for k in range(4):
                n = NB1 // 4
                sp.dma_start(w1_raw[:, k * n:(k + 1) * n],
                             w1.rearrange("e f d -> (e f) d").rearrange("(j p) d -> p j d", p=128)[:, k * n:(k + 1) * n]).then_inc(loaded, 16)
            sp.dma_start(w2_raw[:], w2.rearrange("e d f -> d e f")).then_inc(loaded, 16)

            def step(t, i, turn):
                tl, tll = t + 3, (i + 3) % U
                if has(tl):
                    wait_apart(sp, x_turned, tl - U + 1, passed)
                    r = row_of(sp, tl)
                    sp.dma_start(x_t[tll][:], xs[bass.ds(r, S)]).then_inc(x_loaded[tll], 16)
            run(sp, step)

        @block.gpsimd
        def _(pool):
            diagonal(nc, pool, ident, cleared, made)

            def step(t, i, turn):
                ts, si = t - 3, (i - 3) % U
                if has(ts):
                    wait_apart(pool, y_ready, ts + 1, passed)
                    pool.dma_start(ys[ts * S:(ts + 1) * S] if isinstance(ts, int) else ys[bass.ds(ts * S, S)], y_t[si][:]).then_inc(y_stored[si], 16)
            run(pool, step)
            for i in range(NX):
                pool.wait_ge(y_stored[i], TILES // NX * 16)

        @block.tensor
        def _(pe):
            pe.wait_ge(loaded, 16 * 5)
            pe.wait_ge(made, 1)
            for j in range(NB1 // 4):
                wait(pe, w_copied, j - 1)
                for k in range(4):
                    last = nc.tensor.transpose(ps_a[j % 2][:, k * 128:(k + 1) * 128], w1_raw[:, 4 * j + k], ident[:])
                last.then_inc(w_turned, 1)
            for e in range(E):
                n = NB1 // 4 + e
                wait(pe, w_copied, n - 1)
                for k, (f0, fn) in enumerate(FCHUNKS):
                    last = nc.tensor.transpose(ps_a[n % 2][0:fn, k * 128:(k + 1) * 128], w2_raw[:, e, f0:f0 + fn], ident[:])
                last.then_inc(w_turned, 1)
            pe.wait_ge(w_copied, NB1 // 4 + E)

            def step(t, i, turn):
                tx, th, tt, ty = t + 2, t + 1, t, t - 1
                if has(th):
                    e_h = expert_of(pe, th)
                if has(ty):
                    e_y = expert_of(pe, ty)
                if has(tx):
                    pe.wait_ge(x_loaded[(i + 2) % U], nth(tx, (i + 2) % U))
                    wait(pe, xT_ready, tx)
                    nc.tensor.transpose(ps_x[:, 0:S], x_t[(i + 2) % U][:], ident[:]).then_inc(x_turned, 1)
                if has(th):
                    p = (i + 1) % 2
                    pe.wait_ge(xT_ready, th + 1)
                    wait(pe, h_ready, th - 1)
                    nc.tensor.matmul(ps_a[p][:, 0:F], xT[p][:], w1T[:, bass.ds(e_h * (2 * F), F)], start=True, stop=True)
                    nc.tensor.matmul(ps_g[p][:, 0:F], xT[p][:], w1T[:, bass.ds(e_h * (2 * F) + F, F)],
                                     start=True, stop=True).then_inc(hidden, 1)
                if has(tt):
                    p = i % 2
                    pe.wait_ge(h_ready, tt + 1)
                    wait(pe, hT_ready, tt)
                    for k, (f0, fn) in enumerate(FCHUNKS):
                        last = nc.tensor.transpose(ps_t[0:fn, k * S:(k + 1) * S], h_t[p][:, f0:f0 + fn], ident[:])
                    last.then_inc(h_turned, 1)
                if has(ty):
                    p = (i - 1) % 2
                    pe.wait_ge(hT_ready, ty + 1)
                    wait(pe, y_ready, ty)
                    for k, (f0, fn) in enumerate(FCHUNKS):
                        last = nc.tensor.matmul(ps_y[:, 0:D], hT[p][0:fn, k], w2T[0:fn, k, bass.ds(e_y * D, D)],
                                                start=(k == 0), stop=(k == len(FCHUNKS) - 1))
                    last.then_inc(y_done, 1)
            run(pe, step)

        @block.scalar
        def _(act):
            def step(t, i, turn):
                th, tt = t + 1, t
                if has(th):
                    p = (i + 1) % 2
                    act.wait_ge(hidden, th + 1)
                    nc.scalar.activation(act_a[p][:], ps_a[p][:, 0:F], ACT.Silu).then_inc(silu_ready, 1)
                if has(tt):
                    p = i % 2
                    act.wait_ge(h_turned, tt + 1)
                    wait(act, y_done, tt - 1)
                    nc.scalar.copy(hT[p][:, 0:2], ps_t[:, 0:2 * S].rearrange("f (k s) -> f k s", s=S))
                    nc.scalar.copy(hT[p][0:F - 256, 2], ps_t[0:F - 256, 2 * S:3 * S]).then_inc(hT_ready, 1)
            run(act, step)

        @block.vector
        def _(dve):
            for j in range(NB1 // 4):
                dve.wait_ge(w_turned, j + 1)
                nc.vector.tensor_copy(w1T[:, j * 512:(j + 1) * 512], ps_a[j % 2][:]).then_inc(w_copied, 1)
            for e in range(E):
                n = NB1 // 4 + e
                dve.wait_ge(w_turned, n + 1)
                nc.vector.tensor_copy(w2T[:, 0:2, e * D:(e + 1) * D],
                                      ps_a[n % 2][:, 0:256].rearrange("f (k d) -> f k d", d=D))
                nc.vector.tensor_copy(w2T[0:F - 256, 2, e * D:(e + 1) * D], ps_a[n % 2][0:F - 256, 256:384]).then_inc(w_copied, 1)

            def step(t, i, turn):
                tx, th, ty = t + 2, t + 1, t - 1
                if has(tx):
                    dve.wait_ge(x_turned, tx + 1)
                    wait(dve, hidden, tx - 1)
                    nc.vector.tensor_copy(xT[i % 2][:], ps_x[:, 0:S]).then_inc(xT_ready, 1)
                if has(th):
                    p = (i + 1) % 2
                    dve.wait_ge(silu_ready, th + 1)
                    wait(dve, h_turned, th - 1)
                    nc.vector.tensor_tensor(h_t[p][:], act_a[p][:], ps_g[p][:, 0:F], ALU.mult).then_inc(h_ready, 1)
                if has(ty):
                    j = (i - 1) % U
                    dve.wait_ge(y_done, ty + 1)
                    wait(dve, y_stored[j], nth(ty, j) - 16)
                    nc.vector.tensor_copy(y_t[j][:], ps_y[:, 0:D]).then_inc(y_ready, 1)
            run(dve, step)


def combine(nc, x1, x2, ys, keep):
    slots_all, gates_all, _, _ = keep
    x_v, o_v = (t.rearrange("(n b) s d -> n s b d", b=GB) for t in (x1, x2))
    with ExitStack() as c:
        sb = lambda name, shape, dt=F32: c.enter_context(nc.sbuf_tensor("K_" + name, shape, dt))
        sem = c.enter_context(phase_semaphores(nc, "K_"))
        two = lambda f: [f(0), f(1)]
        x_t = two(lambda p: sb(f"x{p}", [S, GB, D]))
        y_t = two(lambda p: sb(f"y{p}", [S, GB, TOP, D]))
        acc, out = sb("acc", [S, GB, D]), two(lambda p: sb(f"out{p}", [S, GB, D]))
        slot = two(lambda p: sb(f"slot{p}", [S, GB, TOP], mybir.dt.uint32))
        gate = two(lambda p: sb(f"gate{p}", [S, GB, TOP]))
        x_loaded, gathered, stored = (two(lambda p: sem(f"{n}{p}")) for n in ("x_loaded", "gathered", "stored"))
        slot_ready, gate_ready, added, summed, passed = (sem(n) for n in ("slot_ready", "gate_ready", "added", "summed", "passed"))
        block = c.enter_context(nc.Block())
        cell = lambda t, g: t[:, g.n] if isinstance(g.pair, int) else t[:, bass.ds(g.n, 1)][:, 0]

        @block.sync
        def _(sp):
            def step(g):
                g1, gm = g + 1, g + -1
                if g1.exists:
                    wait_apart(sp, summed, g1.n - 1, passed)
                    sp.dma_start(x_t[g1.par][:], x_v[g1.n]).then_inc(x_loaded[g1.par], 16)
                if gm.exists:
                    wait_apart(sp, summed, gm.n + 1, passed)
                    sp.dma_start(o_v[gm.n], out[gm.par][:]).then_inc(stored[gm.par], 16)
            loop_groups(sp, step, 1)
            for p in range(2):
                sp.wait_ge(stored[p], NG // 2 * 16)

        @block.scalar
        def _(act):
            def step(g):
                g1 = g + 1
                if g1.exists:
                    wait_apart(act, gathered[g1.par], g1.pair * GB * TOP * 16, passed)
                    nc.scalar.copy(slot[g1.par][:].bitcast(F32), cell(slots_all, g1).bitcast(F32)).then_inc(slot_ready, 1)
                    wait_apart(act, summed, g1.n - 1, passed)
                    nc.scalar.copy(gate[g1.par][:], cell(gates_all, g1)).then_inc(gate_ready, 1)
            loop_groups(act, step, 1)

        @block.gpsimd
        def _(pool):
            def step(g):
                g1 = g + 1
                if g1.exists:
                    wait_apart(pool, slot_ready, g1.n + 1, passed)
                    wait_apart(pool, summed, g1.n - 1, passed)
                    for b in range(GB):
                        for k in range(TOP):
                            nc.gpsimd.indirect_dma_start(
                                out=y_t[g1.par][:, b, k], out_offset=None, in_=ys,
                                in_offset=bass.IndirectOffsetOnAxis(ap=slot[g1.par][:, b, k:k + 1], axis=0),
                            ).then_inc(gathered[g1.par], 16)
            loop_groups(pool, step, 1)

        @block.vector
        def _(dve):
            def step(g):
                if not g.exists:
                    return
                p = g.par
                wait_apart(dve, x_loaded[p], (g.pair + 1) * 16, passed)
                wait_apart(dve, gathered[p], (g.pair + 1) * GB * TOP * 16, passed)
                wait_apart(dve, gate_ready, g.n + 1, passed)
                wait_apart(dve, stored[p], g.pair * 16, passed)
                wait_apart(dve, summed, g.n, passed)
                for b in range(GB):
                    last = nc.vector.scalar_tensor_tensor(acc[:, b], y_t[p][:, b, 0], gate[p][:, b, 0:1], x_t[p][:, b], ALU.mult, ALU.add)
                last.then_inc(added, 1)
                wait_apart(dve, added, g.n + 1, passed)
                for b in range(GB):
                    last = nc.vector.scalar_tensor_tensor(out[p][:, b], y_t[p][:, b, 1], gate[p][:, b, 1:2], acc[:, b], ALU.mult, ALU.add)
                last.then_inc(summed, 1)
            loop_groups(dve, step, 1)


R = 64
ER = E * R
SCALING = 2.0


def adapter_layer(nc, x3, out, Wg, bg, W1, W2):
    x_v, o_v = (t.rearrange("(n b) s d -> n s b d", b=GB) for t in (x3, out))
    with ExitStack() as c:
        sb = lambda name, shape, dt=F32: c.enter_context(nc.sbuf_tensor("F_" + name, shape, dt))
        pb = lambda name, shape, dt=F32: c.enter_context(nc.psum_tensor("F_" + name, shape, dt))
        sem = c.enter_context(phase_semaphores(nc, "F_"))
        two = lambda f: [f(0), f(1)]
        ident, half_neg = sb("ident", [128, 128]), sb("half_neg", [S, GB])
        iota_e, iota_ei = sb("iota_e", [S, E]), sb("iota_ei", [S, E], I32)
        wg_raw, bg_bc = sb("wg_raw", [E, D]), sb("bg_bc", [S, E])
        w1_raw, w2_raw = sb("w1_raw", [128, ER // 128, D]), sb("w2_raw", [D, E, R])
        wgT, w1T, w2T = sb("wgT", [D, E]), sb("w1T", [D, ER]), sb("w2T", [128, ER // 128, D])
        NX = 4
        x_t = two(lambda p: sb(f"x{p}", [S, GB, D]))
        res_t = two(lambda p: sb(f"res{p}", [S, GB, D]))
        stats, mv, rstd, xn = sb("stats", [S, GB, 6]), sb("mv", [S, GB, 2]), sb("rstd", [S, GB]), sb("xn", [S, GB, D])
        xnT = two(lambda p: sb(f"xnT{p}", [D, GB, S]))
        lg, top = sb("lg", [S, GB, E]), sb("top", [S, GB, 8])
        top_i, idx_f = sb("top_i", [S, GB, 8], mybir.dt.uint32), sb("idx_f", [S, GB, TOP])
        diff, e2, den, gates = sb("diff", [S, GB]), sb("e2", [S, GB]), sb("den", [S, GB]), sb("gates", [S, GB, TOP])
        oh = sb("oh", [S, GB, TOP, E])
        gate_e = two(lambda p: sb(f"gate_e{p}", [S, GB, E]))
        h_t, hg = two(lambda p: sb(f"h{p}", [S, ER])), two(lambda p: sb(f"hg{p}", [S, ER]))
        hgT = two(lambda p: sb(f"hgT{p}", [128, ER]))
        out_t = two(lambda p: sb(f"out{p}", [S, GB, D]))
        ps_x, ps_l, ps_y = pb("ps_x", [D, GB, S]), pb("ps_l", [S, GB, E]), pb("ps_y", [S, 512])
        ps_h, ps_t = two(lambda p: pb(f"ps_h{p}", [S, 512])), two(lambda p: pb(f"ps_t{p}", [128, 512]))

        loaded, cleared, made = sem("loaded"), sem("cleared"), sem("made")
        w_turned, w_copied, passed, order = sem("w_turned"), sem("w_copied"), sem("passed"), sem("order")
        x_loaded, res_loaded, stored = (two(lambda p: sem(f"{n}{p}")) for n in ("x_loaded", "res_loaded", "stored"))
        (stats_ready, aggregated, eps_added, rstd_ready, normed, x_turned, xT_ready, logits_done, gap_ready, e2_ready,
         gates_ready, hidden, gelu_ready, gated, h_turned, hT_ready, y_done, summed) = (sem(n) for n in (
            "stats_ready", "aggregated", "eps_added", "rstd_ready", "normed", "x_turned", "xT_ready", "logits_done",
            "gap_ready", "e2_ready", "gates_ready", "hidden", "gelu_ready", "gated", "h_turned", "hT_ready", "y_done", "summed"))
        ORDER = 10
        block = c.enter_context(nc.Block())

        def at(g, b):
            gg, bb = (g + 1, b - GB) if b >= GB else (g + -1, b + GB) if b < 0 else (g, b)
            return gg, bb, gg.n * GB + bb

        @block.sync
        def _(sp):
            sp.dma_start(w1_raw[:], W1.rearrange("e r d -> (e r) d").rearrange("(j p) d -> p j d", p=128)).then_inc(loaded, 16)
            sp.dma_start(w2_raw[:], W2.rearrange("e d r -> d e r")).then_inc(loaded, 16)
            sp.dma_start(wg_raw[:], Wg).then_inc(loaded, 16)
            sp.dma_start(bg_bc[:], bg.unsqueeze(0).to_broadcast([S, E])).then_inc(loaded, 16)

            def step(g):
                g2, gm = g + 2, g + -1
                if g2.exists:
                    wait_apart(sp, normed, g2.n - 1, passed)
                    sp.dma_start(x_t[g2.par][:], x_v[g2.n]).then_inc(x_loaded[g2.par], 16)
                if g.exists:
                    wait_apart(sp, summed, (g.n - 1) * GB, passed)
                    sp.dma_start(res_t[g.par][:], x_v[g.n]).then_inc(res_loaded[g.par], 16)
                if gm.exists:
                    wait_apart(sp, summed, (gm.n + 1) * GB, passed)
                    sp.dma_start(o_v[gm.n], out_t[gm.par][:]).then_inc(stored[gm.par], 16)
            loop_groups(sp, step, 2)
            for p in range(2):
                sp.wait_ge(stored[p], NG // 2 * 16)

        @block.gpsimd
        def _(pool):
            nc.gpsimd.memset(half_neg[:], -0.5).then_inc(cleared, 1)
            pool.wait_ge(cleared, 1)
            nc.gpsimd.memset(ident[:], 0.0).then_inc(cleared, 1)
            pool.wait_ge(cleared, 2)
            nc.gpsimd.affine_select(out=ident[:], in_=ident[:], compare_op=ALU.not_equal, fill=1.0, base=0,
                                    pattern=[[-1, 128]], channel_multiplier=1).then_inc(made, 1)
            nc.gpsimd.iota(iota_ei[:], pattern=[[1, E]], base=0, channel_multiplier=0).then_inc(cleared, 1)
            pool.wait_ge(cleared, 3)
            nc.gpsimd.tensor_copy(iota_e[:], iota_ei[:]).then_inc(made, 1)

            def step(g):
                g1 = g + 1
                if g1.exists:
                    wait_apart(pool, aggregated, g1.n + 1, passed)
                    nc.gpsimd.tensor_scalar(rstd[:], mv[:, :, 1], EPS, None, ALU.add).then_inc(eps_added, 1)
                    wait_apart(pool, eps_added, g1.n + 1, passed)
                    nc.gpsimd.tensor_tensor(rstd[:], rstd[:], half_neg[:], ALU.pow).then_inc(rstd_ready, 1)
            loop_groups(pool, step, 1)

        @block.tensor
        def _(pe):
            pe.wait_ge(loaded, 16 * 4)
            pe.wait_ge(made, 1)
            for j in range(ER // 128):
                last = nc.tensor.transpose(ps_h[0][:, j * 128:(j + 1) * 128], w1_raw[:, j], ident[:])
            last.then_inc(w_turned, 1)
            w2_rows = w2_raw[:].rearrange("d e r -> d (e r)")
            for j in range(ER // 128):
                last = nc.tensor.transpose(ps_h[1][:, j * 128:(j + 1) * 128], w2_rows[:, j * 128:(j + 1) * 128], ident[:])
            last.then_inc(w_turned, 1)
            nc.tensor.transpose(ps_y[:, 0:E], wg_raw[:], ident[0:E, 0:E]).then_inc(w_turned, 1)
            pe.wait_ge(w_copied, 3)

            def step(g):
                g1 = g + 1
                for b in range(GB):
                    if b == 0 and g1.exists:
                        pe.wait_ge(normed, g1.n + 1)
                        wait(pe, xT_ready, g1.n)
                        for j in range(GB):
                            last = nc.tensor.transpose(ps_x[:, j], xn[:, j], ident[:])
                        last.then_inc(x_turned, 1)
                    if b == 1 and g1.exists:
                        pe.wait_ge(xT_ready, g1.n + 1)
                        wait(pe, gap_ready, g1.n)
                        for j in range(GB):
                            last = nc.tensor.matmul(ps_l[:, j], xnT[g1.par][:, j], wgT[:], start=True, stop=True)
                        last.then_inc(logits_done, 1)
                    gh, bh, vh = at(g, b + 1)
                    if gh.exists:
                        if bh == 0:
                            pe.wait_ge(xT_ready, gh.n + 1)
                        wait(pe, gelu_ready, vh - 1)
                        nc.tensor.matmul(ps_h[bh % 2][:], xnT[gh.par][:, bh], w1T[:], start=True, stop=True).then_inc(hidden, 1)
                    if g.exists:
                        v = g.n * GB + b
                        pe.wait_ge(gated, v + 1)
                        wait(pe, hT_ready, v - 1)
                        for j in range(ER // 128):
                            last = nc.tensor.transpose(ps_t[b % 2][:, j * 128:(j + 1) * 128], hg[b % 2][:, j * 128:(j + 1) * 128], ident[:])
                        last.then_inc(h_turned, 1)
                    gy, by, vy = at(g, b - 1)
                    if gy.exists:
                        pe.wait_ge(hT_ready, vy + 1)
                        wait(pe, summed, vy)
                        for j in range(ER // 128):
                            last = nc.tensor.matmul(ps_y[:, 0:D], hgT[by % 2][:, j * 128:(j + 1) * 128], w2T[:, j],
                                                    start=(j == 0), stop=(j == ER // 128 - 1))
                        last.then_inc(y_done, 1)
            loop_groups(pe, step, 1)

        @block.scalar
        def _(act):
            def step(g):
                g1 = g + 1
                for b in range(GB):
                    if b == 0 and g1.exists:
                        act.wait_ge(x_turned, g1.n + 1)
                        wait(act, hidden, (g1.n - 1) * GB)
                        nc.scalar.copy(xnT[g1.par][:], ps_x[:]).then_inc(xT_ready, 1)
                    gh, bh, vh = at(g, b + 1)
                    if gh.exists:
                        act.wait_ge(hidden, vh + 1)
                        wait(act, gated, vh - 1)
                        nc.scalar.activation(h_t[bh % 2][:], ps_h[bh % 2][:], ACT.Gelu).then_inc(gelu_ready, 1)
                    if g.exists:
                        v = g.n * GB + b
                        act.wait_ge(h_turned, v + 1)
                        wait(act, y_done, v - 1)
                        nc.scalar.copy(hgT[b % 2][:], ps_t[b % 2][:]).then_inc(hT_ready, 1)
                    if b == 1 and g1.exists:
                        act.wait_ge(gap_ready, g1.n + 1)
                        nc.scalar.activation(e2[:], diff[:], ACT.Exp).then_inc(e2_ready, 1)
            loop_groups(act, step, 1)

        @block.vector
        def _(dve):
            v_ = nc.vector
            dve.wait_ge(w_turned, 3)
            dve.wait_ge(made, 2)
            v_.tensor_copy(w1T[:], ps_h[0][:]).then_inc(w_copied, 1)
            v_.tensor_copy(w2T[:].rearrange("p j d -> p (j d)"), ps_h[1][:]).then_inc(w_copied, 1)
            v_.tensor_copy(wgT[:], ps_y[:, 0:E]).then_inc(w_copied, 1)

            def step(g):
                g1 = g + 1
                links = [0]

                def link(ins):
                    links[0] += 1
                    ins.then_inc(order, 1)
                    wait_apart(dve, order, g1.n * ORDER + links[0], passed)
                for b in range(GB):
                    if b == 0 and g1.exists:
                        wait_apart(dve, x_loaded[g1.par], (g1.pair + 1) * 16, passed)
                        for j in range(GB):
                            v_.bn_stats(stats[:, j], x_t[g1.par][:, j]).then_inc(stats_ready, 1)
                        wait_apart(dve, stats_ready, (g1.n + 1) * GB, passed)
                        for j in range(GB):
                            last = v_.bn_aggr(mv[:, j], stats[:, j])
                        last.then_inc(aggregated, 1)
                        wait_apart(dve, rstd_ready, g1.n + 1, passed)
                        wait_apart(dve, x_turned, g1.n, passed)
                        for j in range(GB):
                            last = v_.tensor_scalar(xn[:, j], x_t[g1.par][:, j], mv[:, j, 0:1], rstd[:, j:j + 1],
                                                    ALU.subtract, ALU.mult)
                        last.then_inc(normed, 1)
                    if b == 1 and g1.exists:
                        wait_apart(dve, logits_done, g1.n + 1, passed)
                        link(v_.tensor_tensor(lg[:], ps_l[:], bg_bc[:].unsqueeze(1).to_broadcast([S, GB, E]), ALU.add))
                        for j in range(GB):
                            last = v_.max(top[:, j], lg[:, j])
                        link(last)
                        for j in range(GB):
                            last = v_.max_index(top_i[:, j], top[:, j], lg[:, j])
                        link(last)
                        v_.tensor_tensor(diff[:], top[:, :, 1], top[:, :, 0], ALU.subtract).then_inc(gap_ready, 1)
                        link(v_.tensor_copy(idx_f[:], top_i[:, :, 0:TOP]))
                        picks = [S, GB, TOP, E]
                        link(v_.tensor_tensor(oh[:], iota_e[:].unsqueeze(1).unsqueeze(1).to_broadcast(picks),
                                              idx_f[:].unsqueeze(3).to_broadcast(picks), ALU.is_equal))
                    if b == 2 and g1.exists:
                        wait_apart(dve, e2_ready, g1.n + 1, passed)
                        link(v_.tensor_scalar(den[:], e2[:], 1.0, None, ALU.add))
                        link(v_.reciprocal(gates[:, :, 0], den[:]))
                        link(v_.tensor_tensor(gates[:, :, 1], e2[:], gates[:, :, 0], ALU.mult))
                        link(v_.tensor_tensor(oh[:], oh[:], gates[:].unsqueeze(3).to_broadcast(picks), ALU.mult))
                        link(v_.tensor_tensor(gate_e[g1.par][:], oh[:, :, 0], oh[:, :, 1], ALU.add))
                        assert links[0] == ORDER
                    gh, bh, vh = at(g, b + 1)
                    if gh.exists:
                        dve.wait_ge(gelu_ready, vh + 1)
                        wait(dve, h_turned, vh - 1)
                        v_.tensor_tensor(hg[bh % 2][:].rearrange("s (e r) -> s e r", r=R),
                                         h_t[bh % 2][:].rearrange("s (e r) -> s e r", r=R),
                                         gate_e[gh.par][:, bh].unsqueeze(2).to_broadcast([S, E, R]), ALU.mult).then_inc(gated, 1)
                    gy, by, vy = at(g, b - 1)
                    if gy.exists:
                        dve.wait_ge(y_done, vy + 1)
                        if by == 0:
                            wait_apart(dve, res_loaded[gy.par], (gy.pair + 1) * 16, passed)
                            wait_apart(dve, stored[gy.par], gy.pair * 16, passed)
                        v_.scalar_tensor_tensor(out_t[gy.par][:, by], ps_y[:, 0:D], SCALING, res_t[gy.par][:, by],
                                                ALU.mult, ALU.add).then_inc(summed, 1)
            loop_groups(dve, step, 1)


def encoder(nc, a, out):
    x1, x2, x3 = (nc.dram_tensor(n, (B, S, D), F32, kind="Internal").ap() for n in ("x1", "x2", "x3"))
    xs = nc.dram_tensor("routed_in", (ROUTED_ROWS, D), F32, kind="Internal").ap()
    ys = nc.dram_tensor("routed_out", (TILES * S, D), F32, kind="Internal").ap()
    with ExitStack() as c:
        w = [a["L0_xattn_" + n] for n in ("Wq", "bq", "Wk", "bk", "Wv", "bv", "Wp", "bp")]
        attention_layer(nc, a["x"], x1, a["fside_BxSxS_0"], a["ctx_1024"], 0, attention_consts(nc, c, w, 0))
    with ExitStack() as c:
        sb = lambda name, shape, dt: c.enter_context(nc.sbuf_tensor(name, shape, dt))
        keep = (sb("slots_all", [S, NG, GB, TOP], mybir.dt.uint32), sb("gates_all", [S, NG, GB, TOP], F32),
                sb("tile_row", [1, TILES], I32), sb("tile_expert", [1, TILES], I32))
        route_tokens(nc, x1, xs, a["L0_ffn_wqkv"], keep)
        expert_tiles(nc, xs, ys, a["L0_ffn_w1"], a["L0_ffn_w2"], keep)
        combine(nc, x1, x2, ys, keep)
    with ExitStack() as c:
        w = [a["L1_xattn_" + n] for n in ("W_q", "b_q", "W_k", "b_k", "W_v", "b_v", "W_o", "b_o")]
        attention_layer(nc, x2, x3, a["fside_BxSxS_0"], a["ctx_1024"], 1, attention_consts(nc, c, w, 1))
    adapter_layer(nc, x3, out, a["L1_ffn_Wg"], a["L1_ffn_bg"], a["L1_ffn_W1"], a["L1_ffn_W2"])


INPUTS = ["x", "fside_BxSxS_0", "ctx_1024"] + ["L0_xattn_" + n for n in ("Wq", "bq", "Wk", "bk", "Wv", "bv", "Wp", "bp")] \
    + ["L0_ffn_" + n for n in ("wqkv", "w1", "w2")] \
    + ["L1_xattn_" + n for n in ("W_q", "b_q", "W_k", "b_k", "W_v", "b_v", "W_o", "b_o")] \
    + ["L1_ffn_" + n for n in ("Wg", "bg", "W1", "W2")]


def kernel(**inputs):
    import concourse.bacc as bacc
    from concourse.bass_utils import run_bass_kernel_spmd as run

    nc = bacc.Bacc("TRN2", target_bir_lowering=False, num_devices=1)
    arrays, tensors = {}, {}
    for name in INPUTS:
        array = np.ascontiguousarray(inputs[name])
        arrays["in_" + name] = array
        tensors[name] = nc.dram_tensor("in_" + name, array.shape, mybir.dt.from_np(array.dtype), kind="ExternalInput").ap()
    out = nc.dram_tensor("out_0", (B, S, D), F32, kind="ExternalOutput").ap()
    encoder(nc, tensors, out)
    return run(nc, [arrays], core_ids=[0]).results[0]["out_0"]
```

```python
import concourse.bass as bass
from concourse import mybir
from contextlib import ExitStack, contextmanager
import numpy as np

F32 = mybir.dt.float32
BF16 = mybir.dt.bfloat16
I32 = mybir.dt.int32
ACT = mybir.ActivationFunctionType
ALU = mybir.AluOpType
AX = mybir.AxisListType

B, S, D = 64, 128, 128
H, DH = 16, 8
SC = 120
E = 8
GB = 4
NG = B // GB
EPS = 1e-5
FIRST_STEP = -4
LOOP0 = 4
ONE_ONE = 0x3F803F80
NPART = 3
TERM_ROWS = NPART * NPART * DH
SHIFT_ROW = 96
STACK_ROWS = SHIFT_ROW + 2
HALF = H // 2


@contextmanager
def phase_semaphores(nc, tag):
    held = []

    def sem(name):
        held.append(nc.alloc_semaphore(tag + name))
        return held[-1]
    yield sem
    nc.clear_and_free_semaphores(held)
    nc.all_engine_barrier()


class Group:

    def __init__(self, pair, par):
        self.pair, self.par = pair, par

    def __add__(self, k):
        t = self.par + k
        return Group(self.pair + t // 2 if t // 2 else self.pair, t % 2)

    @property
    def n(self):
        return self.pair * 2 + self.par

    @property
    def exists(self):
        return not isinstance(self.pair, int) or 0 <= self.n < NG


def wait(eng, sem, value):
    if isinstance(value, int) and value <= 0:
        return
    eng.wait_ge(sem, value)


def wait_apart(eng, sem, value, passed):
    if isinstance(value, int):
        return wait(eng, sem, value)
    eng.wait_ge(sem, value)
    eng.sem_inc(passed, 1)


def run_steps(eng, step, last):
    for n in range(FIRST_STEP, LOOP0):
        step(Group(n // 2, n % 2))
    with eng.Fori(LOOP0 // 2, NG // 2 - 2) as pair:
        step(Group(pair, 0))
        step(Group(pair, 1))
    for n in range(NG - 4, last + 1):
        step(Group(n // 2, n % 2))


def attention_layer(nc, x_in, x_out, side, ctx_in, layer, consts, route, ys=None):
    first = layer == 0
    LAST_STEP = NG + 1 if first else NG
    KEYS = [S, SC] if first else [SC]
    NT = len(KEYS)
    NK = sum(KEYS)
    HPB = 2 if first else 4
    MT_PER_B = H // HPB
    MT_PER_U = MT_PER_B // 2
    tag = f"L{layer}_"
    ident, ident_bf, wq, wk, wv, wo, bq, bk, bv_bc, bo_bc, half_neg = consts

    q_scr = nc.dram_tensor(tag + "q_parts", (2, GB, NPART, D, S), BF16, kind="Internal").ap()
    k_scr = nc.dram_tensor(tag + "k_parts", (2, GB, NPART, D, NK), BF16, kind="Internal").ap()
    x_v = x_in.rearrange("(n b) s d -> n s b d", b=GB)
    if first:
        res_v = x_v
    else:
        res_v = nc.dram_tensor("x2", (B, S, D), F32, kind="Internal").ap().rearrange("(n b) s d -> n s b d", b=GB)
    xo_v = x_out.rearrange("(n b) s d -> n s b d", b=GB)
    side_v = side.rearrange("(n b) s d -> n s b d", b=GB)
    ctx_v = ctx_in.rearrange("(n b) s d -> n s b d", b=GB)

    if first:
        jobs = [(0, 0, "FT", 0), (0, 2, "MT", 2), (1, 0, "KP", 0), (1, 1, "OB", 3), (1, 2, "CX", 0), (2, 0, "XT", 0),
                (2, 1, "AT", 0), (2, 2, "QP", 0), (3, 0, "OP", 0), (3, 2, "VP", 0), (4, 0, "OB", 0), (4, 2, "MT", 0),
                (5, 2, "OB", 1), (7, 2, "OB", 2),
                (3, 1, "RC", 0), (6, 0, "RX", 0), (6, 2, "RQ", 0)]
    else:
        jobs = [(0, 0, "FT", 0), (0, 1, "MT", 2), (1, 0, "KP", 0), (1, 1, "OB", 3), (2, 0, "XT", 0), (2, 1, "AT", 0),
                (3, 0, "QP", 0), (3, 1, "OP", 0), (4, 0, "OB", 0), (4, 1, "MT", 0), (5, 0, "VP", 0), (5, 1, "OB", 1),
                (7, 1, "OB", 2)]
    jobs.sort()
    if first:
        UNIT = [("job", 0), ("scores", 0), ("max", 0), ("job", 1), ("max", 1), ("scores", 1), ("max", 2), ("job", 2),
                ("values", 0), ("max", 3), ("values", 1)]
    else:
        UNIT = [("job", 0), ("scores", 0), ("max", 0), ("job", 1), ("values", 0), ("max", 1), ("values", 1)]
    def job_group(u, place, name, b):
        if name in ("XT", "QP", "FT", "KP", "CX"):
            return 2
        if name == "VP":
            return 1
        if name == "RC":
            return -2
        if name in ("AT", "OP", "RX", "RQ"):
            return -1
        if name == "OB":
            return -1 if u < 3 else 0
        return 1 if u >= 2 else 0
    def job_runs(g, job):
        return (g + job_group(*job)).exists

    NJ = len(jobs)
    peeled = {}
    total = 0
    for n in range(FIRST_STEP, LAST_STEP + 1):
        peeled[n] = total
        total += sum(job_runs(Group(n // 2, n % 2), j) for j in jobs)
    def job_no(g, k):
        if isinstance(g.pair, int):
            return peeled[g.n] + sum(job_runs(g, j) for j in jobs[:k])
        return g.n * NJ + (peeled[LOOP0] - LOOP0 * NJ + k)
    def job_done(gj, name, b=0):
        k = [j[2:] for j in jobs].index((name, b))
        return job_no(gj + -job_group(*jobs[k]), k) + 1 if gj.exists else 0

    with ExitStack() as c:
        sb = lambda name, shape, dt=F32: c.enter_context(nc.sbuf_tensor(tag + name, shape, dt))
        pb = lambda name, shape, dt=F32: c.enter_context(nc.psum_tensor(tag + name, shape, dt))
        sem = c.enter_context(phase_semaphores(nc, tag))
        two = lambda f: [f(0), f(1)]

        x_t = two(lambda p: sb(f"x{p}", [S, GB, D]))
        res_t = two(lambda p: sb(f"res{p}", [S, GB, D]))
        side_t = two(lambda p: sb(f"side{p}", [S, GB, D])) if first else None
        ctx_t = two(lambda p: sb(f"ctx{p}", [SC, GB, D]))
        stats = sb("stats", [S, GB, 6])
        mv = sb("mv", [S, GB, 2])
        rstd = sb("rstd", [S, GB])
        xn = sb("xn", [S, GB, D])
        ctx_o = sb("ctx_o", [SC, GB, D]) if first else None
        xnT = sb("xnT", [D, GB * S])
        srcT = two(lambda p: sb(f"srcT{p}", [D, GB, KEYS[0]]))
        qf = sb("qf", [D, GB, S])
        kf = sb("kf", [D, GB, NK])
        rem = sb("rem", [D, GB, max(NK, S)])
        q_parts = sb("q_parts_sb", [D, GB, NPART, S], BF16)
        k_parts = sb("k_parts_sb", [D, GB, NPART, NK], BF16)
        q_st = two(lambda p: sb(f"q_stack{p}", [STACK_ROWS, GB, H, S], BF16))
        k_st = two(lambda p: sb(f"k_stack{p}", [STACK_ROWS, GB, H, NK], BF16))
        v_t = [two(lambda p: sb(f"v{t}_{p}", [KEYS[t], GB, H, DH + 1])) for t in range(NT)]
        p_t = [two(lambda p: sb(f"p{t}_{p}", [KEYS[t], HALF * S])) for t in range(NT)]
        neg_max = sb("neg_max", [S, GB, H])
        m_parts = two(lambda p: sb(f"m_parts{p}", [S, 2, 2, H], BF16))
        mT = two(lambda p: sb(f"mT{p}", [4 * H, S], BF16))
        o_sb = sb("o_sb", [D, 4 * S])
        rden = sb("rden", [S, H])
        att = sb("att", [S, GB, H, DH])
        attT = sb("attT", [D, GB * S])
        out_t = two(lambda p: sb(f"out{p}", [S, GB, D]))

        if not first:
            base_t = two(lambda p: sb(f"base{p}", [S, GB, D]))
            y_t = two(lambda p: sb(f"y{p}", [S, GB, TOP, D]))
            slot = two(lambda p: sb(f"slot{p}", [S, GB, TOP], mybir.dt.uint32))
            gate = two(lambda p: sb(f"gate{p}", [S, GB, TOP]))
            part_sum = sb("part_sum", [S, GB, D])

        ps_sc = two(lambda p: pb(f"ps_sc{p}", [S, HALF * S]))
        ps_mx = two(lambda p: pb(f"ps_mx{p}", [S, 512]))
        ps_o = pb("ps_o", [D, 512])
        misc = pb("misc", [D, 512])
        misc_bf = misc[0:4 * H, 0:S // 2].bitcast(BF16)

        x_loaded = two(lambda p: sem(f"x_loaded{p}"))
        res_loaded = two(lambda p: sem(f"res_loaded{p}"))
        side_loaded = two(lambda p: sem(f"side_loaded{p}")) if first else None
        ctx_loaded = two(lambda p: sem(f"ctx_loaded{p}"))
        stored = two(lambda p: sem(f"stored{p}"))
        if not first:
            gathered, x2_stored = two(lambda p: sem(f"gathered{p}")), two(lambda p: sem(f"x2_stored{p}"))
            slot_ready, gate_ready, first_added, summed = (sem(n) for n in ("slot_ready", "gate_ready", "first_added", "summed"))
        q_written, k_written = sem("q_written"), sem("k_written")
        st_loaded = [[sem(f"st_loaded{p}{b}") for b in range(GB)] for p in range(2)]
        shift_loaded = [[sem(f"shift_loaded{p}{k}") for k in range(2)] for p in range(2)]
        aggregated, rstd_ready, normed = sem("aggregated"), sem("rstd_ready"), sem("normed")
        stats_ready, eps_added = sem("stats_ready"), sem("eps_added")
        misc_filled, misc_emptied = sem("misc_filled"), sem("misc_emptied")
        q_split, k_split, v_ctx_ready = sem("q_split"), sem("k_split"), sem("v_ctx_ready")
        res_ready, split_step = sem("res_ready"), sem("split_step")
        q_cleared = sem("q_cleared")
        passed = sem("passed")
        stack_filled, ctx_ordered = sem("stack_filled"), sem("ctx_ordered")
        max_filled, max_read = sem("max_filled"), sem("max_read")
        sc_filled, sc_read = sem("sc_filled"), sem("sc_read")
        pv_done, o_read = sem("pv_done"), sem("o_read")
        m_first, m_ready = sem("m_first"), sem("m_ready")
        recip_ready = sem("recip_ready")

        UPS = 8
        sc_no = lambda g, u, t: (g.n * UPS + u) * NT + t
        mx_no = lambda g, b, k: (g.n * GB + b) * MT_PER_B + k
        def prev_unit(g, u):
            return (g, u - 1) if u else (g + -1, UPS - 1)

        def jobs_at(g, u, place, engines_jobs=None):
            return [(k, j) for k, j in enumerate(jobs) if j[:2] == (u, place) and job_runs(g, j)
                    and (engines_jobs is None or j[2] in engines_jobs)]

        if first:
            rt = Router(nc, c, route, sem, out_t, misc, passed, misc_filled, misc_emptied, job_done)
        ON_ACT = ("QP", "KP", "CX", "MT", "FT", "RX", "RQ", "RC")
        ON_DVE = ("XT", "VP", "OB", "AT", "OP")

        block = c.enter_context(nc.Block())

        @block.sync
        def _(sp):
            def step(g):
                p, g1, g2, g3, g4, gm = g.par, g + 1, g + 2, g + 3, g + 4, g + -1
                if g.exists:
                    wait_apart(sp, misc_emptied, job_done(g + -2, "OP"), passed)
                    if not first:
                        wait_apart(sp, x2_stored[p], (g.pair + 1) * 16, passed)
                    sp.dma_start(res_t[p][:], res_v[g.n]).then_inc(res_loaded[p], 16)
                if not first and g4.exists:
                    wait_apart(sp, summed, g4.n - 1, passed)
                    sp.dma_start(base_t[g4.par][:], x_v[g4.n]).then_inc(x_loaded[g4.par], 16)
                for gl in [g3]:
                    if gl.exists:
                        q = gl.par
                        if first:
                            wait_apart(sp, normed, gl.n - 1, passed)
                            sp.dma_start(x_t[q][:], x_v[gl.n]).then_inc(x_loaded[q], 16)
                            wait_apart(sp, misc_filled, job_done(gl + -2, "FT"), passed)
                            sp.dma_start(side_t[q][:], side_v[gl.n]).then_inc(side_loaded[q], 16)
                            wait_apart(sp, v_ctx_ready, gl.n - 1, passed)
                            wait_apart(sp, ctx_ordered, gl.n - 1, passed)
                        else:
                            wait_apart(sp, misc_filled, job_done(gl + -2, "FT"), passed)
                        sp.dma_start(ctx_t[q][:], ctx_v[gl.n]).then_inc(ctx_loaded[q], 16)
                if g2.exists:
                    if g.exists:
                        for b in range(GB):
                            wait_apart(sp, st_loaded[p][b], (g.pair + 1) * 16 * (NPART + 1), passed)
                    wait_apart(sp, k_split, g2.n + 1, passed)
                    sp.dma_start(k_scr[p].rearrange("b a r s -> r (b a) s"),
                                 k_parts[:].rearrange("r b a s -> r (b a) s")).then_inc(k_written, 16)
                if gm.exists:
                    wait_apart(sp, misc_emptied, job_done(gm, "OP"), passed)
                    sp.dma_start(xo_v[gm.n], out_t[gm.par][:]).then_inc(stored[gm.par], 16)
                if not first and g3.exists:
                    wait_apart(sp, summed, g3.n + 1, passed)
                    sp.dma_start(res_v[g3.n], x_t[g3.par][:]).then_inc(x2_stored[g3.par], 16)
                if g2.exists:
                    if isinstance(g.pair, int) and g.n in (-2, -1):
                        sp.wait_ge(stack_filled, g.n + 3)
                        sp.wait_ge(q_cleared, g.n + 3)

                    def slot_free(b):
                        if g.exists:
                            wait_apart(sp, sc_filled, sc_no(g, 2 * b + 1, NT - 1) + 1, passed)

                    def load_k(b):
                        sp.dma_start(
                            k_st[p][0:TERM_ROWS, b].rearrange("r h s -> r (h s)"),
                            k_scr[p, b].rearrange("a (d h) s -> (a d) (h s)", d=DH).unsqueeze(0)
                            .to_broadcast([NPART, NPART * DH, H * NK])).then_inc(st_loaded[p][b], 16)
                    wait_apart(sp, k_written, (g2.n + 1) * 16, passed)
                    for b in range(2):
                        slot_free(b)
                        load_k(b)
                    wait_apart(sp, q_split, g2.n + 1, passed)
                    sp.dma_start(q_scr[p].rearrange("b a r s -> r (b a) s"),
                                 q_parts[:].rearrange("r b a s -> r (b a) s")).then_inc(q_written, 16)
                    wait_apart(sp, q_written, (g2.n + 1) * 16, passed)
                    for b in range(GB):
                        if b >= 2:
                            slot_free(b)
                            load_k(b)
                        for a in range(NPART):
                            rows = slice(a * NPART * DH, (a + 1) * NPART * DH)
                            sp.dma_start(
                                q_st[p][rows, b].rearrange("r h s -> r (h s)"),
                                q_scr[p, b, a].rearrange("(d h) s -> d (h s)", d=DH).unsqueeze(0)
                                .to_broadcast([NPART, DH, H * S])).then_inc(st_loaded[p][b], 16)
            run_steps(sp, step, LAST_STEP)
            sp.wait_ge(stored[0], NG // 2 * 16)
            sp.wait_ge(stored[1], NG // 2 * 16)

        @block.gpsimd
        def _(pool):
            def split(src, parts, done, links):
                r = rem[:, :, 0:src.shape[-1]]
                nc.gpsimd.tensor_tensor(r, src, parts[:, :, 0], ALU.subtract).then_inc(split_step, 1)
                wait_apart(pool, split_step, links + 1, passed)
                nc.gpsimd.tensor_copy(parts[:, :, 1], r).then_inc(split_step, 1)
                wait_apart(pool, split_step, links + 2, passed)
                nc.gpsimd.tensor_tensor(parts[:, :, 2], r, parts[:, :, 1], ALU.subtract).then_inc(done, 1)
            def fill_rest(p):
                nc.gpsimd.memset(k_st[p][64:STACK_ROWS].rearrange("r b h s -> r (b h s)").bitcast(I32), ONE_ONE).then_inc(stack_filled, 1)
                pool.wait_ge(stack_filled, p + 1)

            def step(g):
                g1, g2, g3 = g + 1, g + 2, g + 3
                if isinstance(g.pair, int) and g.n in (-2, -1):
                    pool.wait_ge(rstd_ready, g.n + 3)
                    fill_rest(g.par)
                if g1.exists and first:
                    wait_apart(pool, pv_done, (g1.n - 1) * UPS, passed)
                    wait_apart(pool, ctx_loaded[g1.par], (g1.pair + 1) * 16, passed)
                    nc.gpsimd.tensor_copy(
                        v_t[1][g1.par][:, :, :, 0:DH],
                        ctx_t[g1.par][:].rearrange("s b (h d) -> s b h d", d=DH)).then_inc(v_ctx_ready, 1)
                if g2.exists:
                    wait_apart(pool, q_split, g2.n, passed)
                    wait_apart(pool, misc_emptied, job_done(g2, "CX" if first else "KP"), passed)
                    split(kf[:], k_parts, k_split, g2.n * 4)
                if g2.exists:
                    wait_apart(pool, misc_emptied, job_done(g2, "QP"), passed)
                    wait_apart(pool, k_split, g2.n + 1, passed)
                    split(qf[:], q_parts, q_split, g2.n * 4 + 2)
                if g3.exists:
                    wait_apart(pool, aggregated, g3.n + 1, passed)
                    nc.gpsimd.tensor_scalar(rstd[:], mv[:, :, 1], EPS, None, ALU.add).then_inc(eps_added, 1)
                    wait_apart(pool, eps_added, g3.n + 1, passed)
                    nc.gpsimd.tensor_tensor(rstd[:], rstd[:], half_neg[:], ALU.pow).then_inc(rstd_ready, 1)
                if g.exists:
                    wait_apart(pool, res_loaded[g.par], (g.pair + 1) * 16, passed)
                    r = res_t[g.par]
                    nc.gpsimd.tensor_tensor(r[:], r[:], bo_bc[:].unsqueeze(1).to_broadcast([S, GB, D]),
                                            ALU.add).then_inc(res_ready, 1)
                if not first and (g + 4).exists:
                    g4 = g + 4
                    wait_apart(pool, slot_ready, g4.n + 1, passed)
                    wait_apart(pool, summed, g4.n - 1, passed)
                    for b in range(GB):
                        for k in range(TOP):
                            nc.gpsimd.indirect_dma_start(
                                out=y_t[g4.par][:, b, k], out_offset=None, in_=ys,
                                in_offset=bass.IndirectOffsetOnAxis(ap=slot[g4.par][:, b, k:k + 1], axis=0),
                            ).then_inc(gathered[g4.par], 16)
                if first:
                    if (g + -1).exists:
                        rt.deviation(pool, g + -1)
                    if (g + -2).exists:
                        rt.scatter(pool, g + -2)
            run_steps(pool, step, LAST_STEP)
            if first:
                rt.scattering_done(pool)

        @block.scalar
        def _(act):
            def evac(g, k, job):
                _, _, name, b = job
                gj = g + job_group(*job)
                act.wait_ge(misc_filled, job_no(g, k) + 1)
                n0 = KEYS[0]
                by_batch = lambda n: misc[:, 0:GB * n].rearrange("r (b s) -> r b s", b=GB)
                if name == "FT":
                    ins = nc.scalar.copy(srcT[gj.par][:], by_batch(n0))
                elif name == "QP":
                    wait(act, q_split, gj.n)
                    wait(act, q_written, gj.n * 16)
                    for dst in (qf[:], q_parts[:, :, 0]):
                        ins = nc.scalar.activation(dst, by_batch(S), ACT.Identity, bias=bq, scale=float(DH) ** -0.5)
                elif name == "KP":
                    wait(act, k_split, gj.n)
                    wait(act, k_written, gj.n * 16)
                    for dst in (kf[:, :, 0:n0], k_parts[:, :, 0, 0:n0]):
                        ins = nc.scalar.activation(dst, by_batch(n0), ACT.Identity, bias=bk, scale=1.0)
                elif name == "CX":
                    wait(act, k_split, gj.n)
                    wait(act, k_written, gj.n * 16)
                    for dst in (kf[:, :, S:], k_parts[:, :, 0, S:]):
                        ins = nc.scalar.copy(dst, by_batch(SC))
                elif name == "MT":
                    pr = b // 2
                    if (gj + -1).exists:
                        act.wait_ge(shift_loaded[(gj + -1).par][pr], ((gj + -1).pair + 1) * 32)
                    ins = nc.scalar.copy(mT[pr][:], misc_bf)
                elif name in ("RX", "RQ", "RC"):
                    ins = rt.take(act, gj, name)
                ins.then_inc(misc_emptied, 1)

            def send_shifts(gj, pr):
                act.wait_ge(misc_emptied, job_done(gj, "MT", 2 * pr))
                for r in range(2):
                    act.dma_start(q_st[gj.par][SHIFT_ROW + r:SHIFT_ROW + r + 1, 2 * pr:2 * pr + 2],
                                  mT[pr][r * 2 * H:(r + 1) * 2 * H, :]).then_inc(shift_loaded[gj.par][pr], 16)

            def order_context(g2):
                act.wait_ge(ctx_loaded[g2.par], (g2.pair + 1) * 16)
                wait(act, misc_filled, job_done(g2 + -1, "CX"))
                for b in range(GB):
                    last = nc.scalar.copy(ctx_o[:, b].rearrange("s (d h) -> s d h", d=DH),
                                          ctx_t[g2.par][:, b].rearrange("s (h d) -> s d h", d=DH))
                last.then_inc(ctx_ordered, 1)

            def fetch_route(g4):
                cell = lambda t: t[:, g4.n] if isinstance(g4.pair, int) else t[:, bass.ds(g4.n, 1)][:, 0]
                wait_apart(act, gathered[g4.par], g4.pair * GB * TOP * 16, passed)
                nc.scalar.copy(slot[g4.par][:].bitcast(F32), cell(route.slots_all).bitcast(F32)).then_inc(slot_ready, 1)
                wait_apart(act, summed, g4.n - 1, passed)
                nc.scalar.copy(gate[g4.par][:], cell(route.gates_all)).then_inc(gate_ready, 1)

            def exponent(g, u, t):
                act.wait_ge(sc_filled, sc_no(g, u, t) + 1)
                wait(act, pv_done, g.n * UPS + u - 1)
                nc.scalar.activation(p_t[t][u % 2][:], ps_sc[(u * NT + t) % 2][0:KEYS[t], :],
                                     ACT.Exp).then_inc(sc_read, 1)

            def step(g):
                for u in range(UPS):
                    for place in range(3):
                        for k, j in jobs_at(g, u, place, ON_ACT):
                            evac(g, k, j)
                        if place < NT and g.exists:
                            exponent(g, u, place)
                        if first and (u, place) == (0, 1) and (g + 2).exists:
                            order_context(g + 2)
                        if first and (u, place) == (0, 0) and (g + -2).exists:
                            rt.exponents(act, g + -2)
                        if first and (u, place) == (3, 0) and (g + -2).exists:
                            rt.gap_exponent(act, g + -2)
                        if not first and (u, place) == (2, 0) and (g + 4).exists:
                            fetch_route(g + 4)
                        if (u, place) == (1, 0) and g.exists:
                            send_shifts(g, 1)
                        if (u, place) == (5, 0) and (g + 1).exists:
                            send_shifts(g + 1, 0)
                    gp, up = prev_unit(g, u)
                    if u % 2 == 0 and gp.exists:
                        act.wait_ge(pv_done, gp.n * UPS + up + 1)
                        wait(act, recip_ready, gp.n * GB + up // 2)
                        nc.scalar.copy(o_sb[:], ps_o[:]).then_inc(o_read, 1)
            run_steps(act, step, LAST_STEP)

        @block.vector
        def _(dve):
            for p in range(2):
                for t in range(NT):
                    nc.vector.memset(v_t[t][p][:, :, :, DH:DH + 1], 1.0)
            nc.vector.memset(ps_o[:], 0.0).then_inc(o_read, 1)

            def clear_rest(p):
                nc.vector.memset(q_st[p][64:SHIFT_ROW].rearrange("r b h s -> r (b h s)").bitcast(I32), 0).then_inc(q_cleared, 1)
            clear_rest(0)

            def evac(g, k, job):
                _, _, name, b = job
                gj = g + job_group(*job)
                dve.wait_ge(misc_filled, job_no(g, k) + 1)
                if name == "XT":
                    nc.vector.tensor_copy(xnT[:], misc[:]).then_inc(misc_emptied, 1)
                elif name == "VP":
                    n = KEYS[0]
                    wait(dve, pv_done, (gj.n - 1) * UPS)
                    nc.vector.tensor_tensor(
                        v_t[0][gj.par][:, :, :, 0:DH],
                        misc[0:n, :].rearrange("s (b h d) -> s b h d", b=GB, d=DH),
                        bv_bc[0:n].rearrange("s (h d) -> s h d", d=DH).unsqueeze(1).to_broadcast([n, GB, H, DH]),
                        ALU.add).then_inc(misc_emptied, 1)
                elif name == "OB":
                    o_v = misc[:].rearrange("q (h c) -> q h c", c=32)
                    nc.vector.reciprocal(rden[:], o_v[:, :, DH]).then_inc(recip_ready, 1)
                    dve.wait_ge(recip_ready, gj.n * GB + b + 1)
                    nc.vector.tensor_tensor(att[:, b], o_v[:, :, 0:DH], rden[:].unsqueeze(2).to_broadcast([S, H, DH]),
                                            ALU.mult).then_inc(misc_emptied, 1)
                elif name == "AT":
                    nc.vector.tensor_copy(attT[:], misc[:]).then_inc(misc_emptied, 1)
                elif name == "OP":
                    dve.wait_ge(res_ready, gj.n + 1)
                    wait(dve, stored[gj.par], gj.pair * 16)
                    nc.vector.tensor_tensor(out_t[gj.par][:].rearrange("s b d -> s (b d)"), misc[:],
                                            res_t[gj.par][:].rearrange("s b d -> s (b d)"), ALU.add).then_inc(misc_emptied, 1)

            def add_expert(g3, part):
                q, (k, half) = g3.par, divmod(part, 2)
                if part == 0:
                    wait_apart(dve, x_loaded[q], (g3.pair + 1) * 16, passed)
                    wait_apart(dve, gathered[q], (g3.pair + 1) * GB * TOP * 16, passed)
                    wait_apart(dve, gate_ready, g3.n + 1, passed)
                if part == 2:
                    wait_apart(dve, first_added, g3.n + 1, passed)
                    wait_apart(dve, x2_stored[q], g3.pair * 16, passed)
                for b in range(2 * half, 2 * half + 2):
                    last = nc.vector.scalar_tensor_tensor(
                        (x_t[q] if k else part_sum)[:, b], y_t[q][:, b, k], gate[q][:, b, k:k + 1],
                        (part_sum if k else base_t[q])[:, b], ALU.mult, ALU.add)
                if half == 1:
                    last.then_inc(summed if k else first_added, 1)

            def statistics(g3, part):
                if part == 0 and first:
                    dve.wait_ge(x_loaded[g3.par], (g3.pair + 1) * 16)
                elif part == 0:
                    wait_apart(dve, summed, g3.n + 1, passed)
                if part < 2:
                    for b in range(2 * part, 2 * part + 2):
                        nc.vector.bn_stats(stats[:, b], x_t[g3.par][:, b]).then_inc(stats_ready, 1)
                else:
                    wait_apart(dve, stats_ready, (g3.n + 1) * GB, passed)
                    for b in range(GB):
                        last = nc.vector.bn_aggr(mv[:, b], stats[:, b])
                    last.then_inc(aggregated, 1)

            def normalise(g3, part):
                if part == 0:
                    dve.wait_ge(rstd_ready, g3.n + 1)
                    wait(dve, misc_filled, job_done(g3 + -1, "XT"))
                for b in range(2 * part, 2 * part + 2):
                    last = nc.vector.tensor_scalar(xn[:, b], x_t[g3.par][:, b], mv[:, b, 0:1], rstd[:, b:b + 1],
                                                   ALU.subtract, ALU.mult)
                if part == 1:
                    last.then_inc(normed, 1)

            if first:
                INPUT_STAGES = {(1, 2): (statistics, 0), (1, 3): (statistics, 1), (2, 0): (statistics, 2),
                                (5, 3): (normalise, 0), (6, 0): (normalise, 1)}
            else:
                INPUT_STAGES = {(1, 0): (add_expert, 0), (1, 1): (add_expert, 1), (2, 0): (add_expert, 2),
                                (2, 1): (add_expert, 3), (3, 0): (statistics, 0), (3, 1): (statistics, 1),
                                (4, 0): (statistics, 2), (6, 0): (normalise, 0), (6, 1): (normalise, 1)}

            def row_maxima(g1, b, kk):
                dve.wait_ge(max_filled, mx_no(g1, b, kk) + 1)
                v = ps_mx[kk % 2][:, 0:HPB * NK].rearrange("q (h s) -> q h s", h=HPB)
                nc.vector.tensor_reduce(neg_max[:, b, kk * HPB:(kk + 1) * HPB], v, AX.X, ALU.max,
                                        negate=True).then_inc(max_read, 1)

            def shift_parts(g1, pr):
                dve.wait_ge(max_read, mx_no(g1, 2 * pr + 1, MT_PER_B - 1) + 1)
                wait(dve, misc_filled, job_done(g1 + -1, "MT", 2 * pr))
                mp, m = m_parts[pr], neg_max[:, 2 * pr:2 * pr + 2]
                nc.vector.tensor_copy(mp[:, 0], m).then_inc(m_first, 1)
                dve.wait_ge(m_first, g1.n * 2 + pr + 1)
                nc.vector.tensor_tensor(mp[:, 1], m, mp[:, 0], ALU.subtract).then_inc(m_ready, 1)

            def between(g, u, k):
                if (u, k) in INPUT_STAGES and (g + 3).exists:
                    stage, part = INPUT_STAGES[u, k]
                    stage(g + 3, part)
                if first and (u, k) in ROUTE_STAGES:
                    behind, stage, part = ROUTE_STAGES[u, k]
                    if (g + -behind).exists:
                        stage(rt, dve, g + -behind, part)

            def step(g):
                g1 = g + 1
                if isinstance(g.pair, int) and g.n == -1:
                    clear_rest(1)
                for u in range(UPS):
                    for what, i in UNIT:
                        if what == "job":
                            for k, j in jobs_at(g, u, i, ON_DVE):
                                evac(g, k, j)
                        elif what == "max":
                            if g1.exists:
                                row_maxima(g1, u // 2, (u % 2) * MT_PER_U + i)
                            between(g, u, i)
                    if u % 4 == 3 and g1.exists:
                        shift_parts(g1, u // 4)
            run_steps(dve, step, LAST_STEP)

        @block.tensor
        def _(pe):
            mm = nc.tensor.matmul

            def fill(g, k, job):
                _, _, name, b = job
                gj = g + job_group(*job)
                if name in ("RX", "RQ", "RC"):
                    wait(pe, misc_emptied, job_no(g, k))
                    rt.fill(pe, gj, name).then_inc(misc_filled, 1)
                    return
                if name == "MT":
                    wait_apart(pe, m_ready, gj.n * 2 + b // 2 + 1, passed)
                    wait_apart(pe, misc_emptied, job_no(g, k), passed)
                else:
                    wait(pe, misc_emptied, job_no(g, k))
                if name == "XT":
                    pe.wait_ge(normed, gj.n + 1)
                    for j in range(GB):
                        last = nc.tensor.transpose(misc[:, j * S:(j + 1) * S], xn[:, j], ident[:])
                elif name == "QP":
                    last = mm(misc[:], wq[:], xnT[:], start=True, stop=True)
                elif name == "FT":
                    n = KEYS[0]
                    if first:
                        pe.wait_ge(side_loaded[gj.par], (gj.pair + 1) * 16)
                    else:
                        pe.wait_ge(ctx_loaded[gj.par], (gj.pair + 1) * 16)
                    src = side_t if first else ctx_t
                    for j in range(GB):
                        last = nc.tensor.transpose(misc[:, j * n:(j + 1) * n], src[gj.par][:, j], ident[0:n, 0:n])
                elif name == "KP":
                    n = GB * KEYS[0]
                    last = mm(misc[:, 0:n], wk[:], srcT[gj.par][:].rearrange("d b s -> d (b s)"), start=True, stop=True)
                elif name == "CX":
                    pe.wait_ge(ctx_ordered, gj.n + 1)
                    for j in range(GB):
                        last = nc.tensor.transpose(misc[:, j * SC:(j + 1) * SC], ctx_o[:, j], ident[0:SC, 0:SC])
                elif name == "VP":
                    n = KEYS[0]
                    for j in range(GB):
                        last = mm(misc[0:n, j * D:(j + 1) * D], srcT[gj.par][:, j], wv[:], start=True, stop=True)
                elif name == "MT":
                    last = nc.tensor.transpose(misc_bf, m_parts[b // 2][:].rearrange("q r i h -> q (r i h)"), ident_bf[:])
                elif name == "OB":
                    pe.wait_ge(o_read, gj.n * GB + b + 2)
                    for j in range(4):
                        last = nc.tensor.transpose(misc[:, j * S:(j + 1) * S], o_sb[:, j * S:(j + 1) * S], ident[:])
                elif name == "AT":
                    for j in range(GB):
                        last = nc.tensor.transpose(misc[:, j * S:(j + 1) * S], att[:, j].rearrange("q h d -> q (h d)"), ident[:])
                elif name == "OP":
                    for j in range(GB):
                        last = mm(misc[:, j * D:(j + 1) * D], attT[:, j * S:(j + 1) * S], wo[:], start=True, stop=True)
                last.then_inc(misc_filled, 1)

            def scores(g, u, t):
                b, hf, p = u // 2, u % 2, g.par
                i = sc_no(g, u, t)
                if t == 0 and hf == 0 and b % 2 == 0:
                    pe.wait_ge(shift_loaded[p][b // 2], (g.pair + 1) * 32)
                wait(pe, sc_read, i - 1)
                k0 = sum(KEYS[:t])
                out = ps_sc[(u * NT + t) % 2]
                for j in range(HALF):
                    h = hf * HALF + j
                    last = mm(out[0:KEYS[t], j * S:(j + 1) * S], k_st[p][:, b, h, k0:k0 + KEYS[t]], q_st[p][:, b, h, :],
                              start=True, stop=True)
                last.then_inc(sc_filled, 1)

            def max_tile(g, b, k):
                p = g.par
                i = mx_no(g, b, k)
                if k == 0:
                    pe.wait_ge(st_loaded[p][b], (g.pair + 1) * 16 * (NPART + 1))
                wait(pe, max_read, i - 1)
                for j in range(HPB):
                    h = k * HPB + j
                    last = mm(ps_mx[k % 2][:, j * NK:(j + 1) * NK], q_st[p][0:SHIFT_ROW, b, h, :],
                              k_st[p][0:SHIFT_ROW, b, h, :], start=True, stop=True)
                last.then_inc(max_filled, 1)

            def weighted_values(g, u, quarter):
                b, hf, p = u // 2, u % 2, g.par
                if u == 0 and quarter == 0:
                    pe.wait_ge(misc_emptied, job_done(g, "VP"))
                    if first:
                        pe.wait_ge(v_ctx_ready, g.n + 1)
                pe.wait_ge(sc_read, sc_no(g, u, NT - 1) + 1)
                if hf == 0 and quarter == 0:
                    pe.wait_ge(o_read, g.n * GB + b + 1)
                for t in range(NT):
                    for j in range(quarter * 4, quarter * 4 + 4):
                        h = hf * HALF + j
                        r, col = 32 * (h % 4), (h // 4) * S
                        last = mm(ps_o[r:r + DH + 1, col:col + S], v_t[t][p][:, b, h, :],
                                  p_t[t][u % 2][:, j * S:(j + 1) * S], start=(t == 0), stop=(t == NT - 1))
                if quarter == 1:
                    last.then_inc(pv_done, 1)

            def step(g):
                g1 = g + 1
                for u in range(UPS):
                    gp, up = prev_unit(g, u)
                    for what, i in UNIT:
                        if what == "job":
                            for k, j in jobs_at(g, u, i):
                                fill(g, k, j)
                        elif what == "scores" and g.exists:
                            scores(g, u, i)
                        elif what == "max" and g1.exists:
                            max_tile(g1, u // 2, (u % 2) * MT_PER_U + i)
                        elif what == "values" and gp.exists:
                            weighted_values(gp, up, i)
            run_steps(pe, step, LAST_STEP)


def diagonal(nc, pool, t, cleared, done):
    nc.gpsimd.memset(t[:], 0.0).then_inc(cleared, 1)
    pool.wait_ge(cleared, 1)
    nc.gpsimd.affine_select(out=t[:], in_=t[:], compare_op=ALU.not_equal, fill=1.0, base=0,
                            pattern=[[-1, t.shape[-1]]], channel_multiplier=1).then_inc(done, 1)


def constants(nc, c, weights, wqkv, route):
    sb = lambda name, shape, dt=F32: c.enter_context(nc.sbuf_tensor("C_" + name, shape, dt))
    ident, ident_bf, half_neg = sb("ident", [128, 128]), sb("ident_bf", [128, 128], BF16), sb("half_neg", [S, GB])
    ready = [[sb(f"{n}{layer}", [D, D]) for n in ("wq", "wk", "wv", "wo")] for layer in range(2)]
    bias = sb("bias", [D, 4])
    bias_bc = [[sb(f"{n}{layer}", [S, D]) for n in ("bv", "bo")] for layer in range(2)]
    route.ident, route.half_neg = ident, half_neg
    route.before, route.ones, route.wT = sb("before", [128, 128], BF16), sb("ones", [128, 128], BF16), sb("wT", [D, 3 * E])
    MATRICES, COLUMNS = (0, 2, 4, 6), (1, 3)
    DMAS = 2 * (4 + 2 + 2) + 1
    with ExitStack() as p:
        raw = [[p.enter_context(nc.sbuf_tensor(f"C_raw{layer}{i}", [D, D], F32)) for i in range(4)] for layer in range(2)]
        bias_raw = p.enter_context(nc.sbuf_tensor("C_bias_raw", [D, 4], F32))
        w_raw = p.enter_context(nc.sbuf_tensor("C_wqkv_raw", [3 * E, D], F32))
        order = p.enter_context(nc.sbuf_tensor("C_order", [D, D], F32))
        ps = p.enter_context(nc.psum_tensor("C_ps", [D, 4, D], F32))
        ps_b = p.enter_context(nc.psum_tensor("C_ps_b", [D, 4], F32))
        ps_w = p.enter_context(nc.psum_tensor("C_ps_w", [D, 3 * E], F32))
        sem = p.enter_context(phase_semaphores(nc, "C_"))
        loaded, cleared, made, ordered, turned, steps = (sem(n) for n in
                                                         ("loaded", "cleared", "made", "ordered", "turned", "steps"))
        block = p.enter_context(nc.Block())

        @block.sync
        def _(sp):
            for layer in range(2):
                for t, i in zip(raw[layer], MATRICES):
                    sp.dma_start(t[:], weights[layer][i]).then_inc(loaded, 16)
                for k, i in enumerate(COLUMNS):
                    sp.dma_start(bias_raw[:, 2 * layer + k:2 * layer + k + 1],
                                 weights[layer][i].rearrange("(c one) -> c one", one=1)).then_inc(loaded, 16)
                for t, i in zip(bias_bc[layer], (5, 7)):
                    sp.dma_start(t[:], weights[layer][i].unsqueeze(0).to_broadcast([S, D])).then_inc(loaded, 16)
            sp.dma_start(w_raw[:], wqkv).then_inc(loaded, 16)

        @block.gpsimd
        def _(pool):
            nc.gpsimd.memset(half_neg[:], -0.5)
            diagonal(nc, pool, ident, cleared, made)
            n = [0]

            def done(ins):
                n[0] += 1
                ins.then_inc(steps, 1)
                pool.wait_ge(steps, n[0])
            done(nc.gpsimd.memset(route.ones[:], 1.0))
            done(nc.gpsimd.affine_select(out=route.before[:], in_=route.ones[:], compare_op=ALU.is_gt, fill=0.0, base=0,
                                         pattern=[[1, 128]], channel_multiplier=-1))
            done(nc.gpsimd.iota(route.iota_ei[:], pattern=[[1, E]], base=0, channel_multiplier=0))
            done(nc.gpsimd.tensor_copy(route.iota_e[:], route.iota_ei[:]))
            done(nc.gpsimd.tensor_scalar(route.region0[:], route.iota_e[:], float(REGION), None, ALU.mult))
            done(nc.gpsimd.tensor_copy(route.count[:], route.region0[:]))

        @block.tensor
        def _(pe):
            pe.wait_ge(loaded, 16 * DMAS)
            pe.wait_ge(made, 1)
            for i in range(4):
                nc.tensor.transpose(ps[:, i], raw[1][i][:], ident[:])
            nc.tensor.transpose(ps_w[:], w_raw[:], ident[0:3 * E, 0:3 * E])
            pe.wait_ge(ordered, 1)
            nc.tensor.matmul(ps_b[:], order[:], bias_raw[:], start=True, stop=True).then_inc(turned, 1)

        @block.vector
        def _(dve):
            v = nc.vector
            d_first = lambda t: t.rearrange("r (h d) -> r d h", d=DH)
            as_dh = lambda t: t.rearrange("r (d h) -> r d h", d=DH)
            dve.wait_ge(made, 1)
            v.tensor_copy(as_dh(order[:]), d_first(ident[:])).then_inc(ordered, 1)
            v.tensor_copy(ident_bf[:], ident[:])
            dve.wait_ge(loaded, 16 * DMAS)
            for i in range(4):
                v.tensor_copy(as_dh(ready[0][i][:]) if i < 2 else ready[0][i][:],
                              d_first(raw[0][i][:]) if i < 2 else raw[0][i][:])
            dve.wait_ge(turned, 1)
            for i in range(4):
                v.tensor_copy(as_dh(ready[1][i][:]) if i < 2 else ready[1][i][:],
                              d_first(ps[:, i]) if i < 2 else ps[:, i])
            v.tensor_copy(route.wT[:], ps_w[:])
            for layer in range(2):
                v.tensor_scalar(bias[:, 2 * layer:2 * layer + 1], ps_b[:, 2 * layer:2 * layer + 1], float(DH) ** -0.5, None, ALU.mult)
                v.tensor_copy(bias[:, 2 * layer + 1:2 * layer + 2], ps_b[:, 2 * layer + 1:2 * layer + 2])
    return [(ident, ident_bf, *ready[layer], bias[:, 2 * layer:2 * layer + 1], bias[:, 2 * layer + 1:2 * layer + 2],
             *bias_bc[layer], half_neg) for layer in range(2)]


TOKENS = B * S
F = 352
TOP = 2
REGION = TOKENS + S
TILES = (TOKENS * TOP // S + E) // 2 * 2
SPARE = E * REGION
ROUTED_ROWS = SPARE + E * S
FCHUNKS = [(0, 128), (128, 128), (256, F - 256)]


def loop_groups(eng, step):
    for n in range(-3, 2):
        step(Group(n // 2, n % 2))
    with eng.Fori(1, NG // 2 - 2) as pair:
        step(Group(pair, 0))
        step(Group(pair, 1))
    for n in range(NG - 4, NG + 2):
        step(Group(n // 2, n % 2))


class Router:

    def __init__(self, nc, c, route, sem, out_t, misc, passed, misc_filled, misc_emptied, job_done):
        self.nc, self.route = nc, route
        self.out_t, self.misc, self.passed = out_t, misc, passed
        self.misc_filled, self.misc_emptied, self.job_done = misc_filled, misc_emptied, job_done
        sb = lambda name, shape, dt=F32: c.enter_context(nc.sbuf_tensor("R_" + name, shape, dt))
        two = lambda f: [f(0), f(1)]
        self.stats, self.mv, self.rstd = sb("stats", [S, GB, 6]), sb("mv", [S, GB, 2]), sb("rstd", [S, GB])
        self.xn = two(lambda p: sb(f"xn{p}", [S, GB, D]))
        self.xnT, self.qkv = sb("xnT", [D, GB * S]), sb("qkv", [S, GB, 3 * E])
        self.products = sb("products", [S, GB, E, E])
        self.exps = sb("exps", [S, GB, E, E])
        self.max, self.sum, self.weighted, self.logits = (sb(n, [S, GB, E]) for n in ("max", "sum", "weighted", "logits"))
        self.top, self.top_i = sb("top", [S, GB, 8]), sb("top_i", [S, GB, 8], mybir.dt.uint32)
        self.idx_f, self.gap, self.e2 = sb("idx_f", [S, GB, TOP]), sb("gap", [S, GB]), sb("e2", [S, GB])
        self.den, self.g0 = sb("den", [S, GB]), sb("g0", [S, GB])
        self.picked, self.picked_pos = sb("picked", [S, GB, TOP, E]), sb("picked_pos", [S, GB, TOP, E])
        self.hits = sb("hits", [S, GB, E], BF16)
        self.ranks, self.pos = sb("ranks", [S, GB + 1, E]), sb("pos", [S, GB, E])
        self.slot_f = sb("slot_f", [S, GB, TOP])
        self.slot = two(lambda p: sb(f"slot{p}", [S, GB, TOP], mybir.dt.uint32))
        (self.stats_ready, self.aggregated, self.eps_added, self.rstd_ready, self.normed, self.shifted, self.exp_ready,
         self.gap_ready, self.e2_ready, self.hits_ready, self.slot_ready, self.order) = (sem("R_" + n) for n in (
             "stats_ready", "aggregated", "eps_added", "rstd_ready", "normed", "shifted", "exp_ready", "gap_ready",
             "e2_ready", "hits_ready", "slot_ready", "order"))
        self.scattered = two(lambda p: sem(f"R_scattered{p}"))

    CHAIN = ("products", "max", "weighted", "reciprocals", "logits", "top", "top_index", "index", "picked",
             "pos", "picked_pos", "slots")

    def made(self, ins):
        ins.then_inc(self.order, 1)

    def after(self, dve, g, result):
        wait_apart(dve, self.order, g.n * len(self.CHAIN) + self.CHAIN.index(result) + 1, self.passed)

    def statistics(self, dve, g, part):
        if part == 0:
            wait_apart(dve, self.misc_emptied, self.job_done(g, "OP"), self.passed)
        if part < 2:
            for b in range(2 * part, 2 * part + 2):
                self.nc.vector.bn_stats(self.stats[:, b], self.out_t[g.par][:, b]).then_inc(self.stats_ready, 1)
        else:
            wait_apart(dve, self.stats_ready, (g.n + 1) * GB, self.passed)
            for b in range(GB):
                last = self.nc.vector.bn_aggr(self.mv[:, b], self.stats[:, b])
            last.then_inc(self.aggregated, 1)

    def normalise(self, dve, g, part):
        if part == 0:
            wait_apart(dve, self.rstd_ready, g.n + 1, self.passed)
            wait_apart(dve, self.scattered[g.par], g.pair * GB * TOP * 16, self.passed)
        for b in range(2 * part, 2 * part + 2):
            last = self.nc.vector.tensor_scalar(self.xn[g.par][:, b], self.out_t[g.par][:, b], self.mv[:, b, 0:1],
                                                self.rstd[:, b:b + 1], ALU.subtract, ALU.mult)
        if part == 1:
            last.then_inc(self.normed, 1)

    def form_products(self, dve, g, part):
        v, full = self.nc.vector, [S, GB, E, E]
        if part == 0:
            q, k = self.qkv[:, :, 0:E], self.qkv[:, :, E:2 * E]
            wait_apart(dve, self.misc_emptied, self.job_done(g, "RQ"), self.passed)
            self.made(v.tensor_tensor(self.products[:], q.unsqueeze(3).to_broadcast(full),
                                      k.unsqueeze(2).to_broadcast(full), ALU.mult))
        elif part == 1:
            self.after(dve, g, "products")
            self.made(v.tensor_reduce(self.max[:], self.products[:], AX.X, ALU.max))
        else:
            self.after(dve, g, "max")
            v.tensor_tensor(self.products[:], self.products[:], self.max[:].unsqueeze(3).to_broadcast(full),
                            ALU.subtract).then_inc(self.shifted, 1)

    def weigh(self, dve, g, part):
        v, full = self.nc.vector, [S, GB, E, E]
        if part == 0:
            wait_apart(dve, self.exp_ready, g.n + 1, self.passed)
            v.tensor_reduce(self.sum[:], self.exps[:], AX.X, ALU.add)
        else:
            self.made(v.tensor_tensor(self.products[:], self.exps[:], self.qkv[:, :, 2 * E:].unsqueeze(2).to_broadcast(full), ALU.mult))

    def form_logits(self, dve, g, part):
        v = self.nc.vector
        if part == 0:
            self.after(dve, g, "weighted")
            v.tensor_reduce(self.weighted[:], self.products[:], AX.X, ALU.add)
            self.made(v.reciprocal(self.sum[:], self.sum[:]))
        elif part == 1:
            self.after(dve, g, "reciprocals")
            self.made(v.tensor_tensor(self.logits[:], self.weighted[:], self.sum[:], ALU.mult))
        else:
            self.after(dve, g, "logits")
            for b in range(GB):
                last = v.max(self.top[:, b], self.logits[:, b])
            self.made(last)

    def pick(self, dve, g, part):
        v, picks = self.nc.vector, [S, GB, TOP, E]
        if part == 0:
            self.after(dve, g, "top")
            v.tensor_tensor(self.gap[:], self.top[:, :, 1], self.top[:, :, 0], ALU.subtract).then_inc(self.gap_ready, 1)
            for b in range(GB):
                last = v.max_index(self.top_i[:, b], self.top[:, b], self.logits[:, b])
            self.made(last)
        elif part == 1:
            self.after(dve, g, "top_index")
            self.made(v.tensor_copy(self.idx_f[:], self.top_i[:, :, 0:TOP]))
            self.after(dve, g, "index")
            self.made(v.tensor_tensor(self.picked[:], self.route.iota_e[:].unsqueeze(1).unsqueeze(1).to_broadcast(picks),
                                      self.idx_f[:].unsqueeze(3).to_broadcast(picks), ALU.is_equal))
        else:
            self.after(dve, g, "picked")
            v.tensor_tensor(self.hits[:], self.picked[:, :, 0], self.picked[:, :, 1], ALU.add).then_inc(self.hits_ready, 1)

    def form_slots(self, dve, g, part):
        v, picks = self.nc.vector, [S, GB, TOP, E]
        if part == 0:
            wait_apart(dve, self.e2_ready, g.n + 1, self.passed)
            v.tensor_scalar(self.den[:], self.e2[:], 1.0, None, ALU.add)
            wait_apart(dve, self.misc_emptied, self.job_done(g, "RC"), self.passed)
            self.made(v.tensor_tensor(self.pos[:], self.ranks[:, 0:GB],
                                      self.route.count[:].unsqueeze(1).to_broadcast([S, GB, E]), ALU.add))
        elif part == 1:
            self.after(dve, g, "pos")
            v.tensor_tensor(self.route.count[:], self.route.count[:], self.ranks[:, GB], ALU.add)
            v.reciprocal(self.g0[:], self.den[:])
            self.made(v.tensor_tensor(self.picked_pos[:], self.picked[:], self.pos[:].unsqueeze(2).to_broadcast(picks), ALU.mult))
        elif part == 2:
            self.after(dve, g, "picked_pos")
            self.made(v.tensor_reduce(self.slot_f[:], self.picked_pos[:], AX.X, ALU.add))
        else:
            self.after(dve, g, "slots")
            v.tensor_copy(self.slot[g.par][:], self.slot_f[:]).then_inc(self.slot_ready, 1)
            gates = self.route.gates_all[:, bass.ds(g.n, 1)] if not isinstance(g.pair, int) else self.route.gates_all[:, g.n:g.n + 1]
            v.tensor_copy(gates[:, 0, :, 0], self.g0[:])
            v.tensor_tensor(gates[:, 0, :, 1], self.e2[:], self.g0[:], ALU.mult)
            v.tensor_copy(self.route.slots_f[:, bass.ds(g.n * (GB * TOP), GB * TOP)], self.slot_f[:].rearrange("s b k -> s (b k)"))

    def take(self, act, g, name):
        if name == "RX":
            return self.nc.scalar.copy(self.xnT[:], self.misc[:])
        if name == "RQ":
            return self.nc.scalar.copy(self.qkv[:].rearrange("s b e -> s (b e)"), self.misc[:, 0:GB * 3 * E])
        return self.nc.scalar.copy(self.ranks[:].rearrange("s b e -> s (b e)"), self.misc[:, 0:(GB + 1) * E])

    def exponents(self, act, g):
        act.wait_ge(self.shifted, g.n + 1)
        self.nc.scalar.activation(self.exps[:], self.products[:], ACT.Exp).then_inc(self.exp_ready, 1)

    def gap_exponent(self, act, g):
        act.wait_ge(self.gap_ready, g.n + 1)
        self.nc.scalar.activation(self.e2[:], self.gap[:], ACT.Exp).then_inc(self.e2_ready, 1)

    def fill(self, pe, g, name):
        mm = self.nc.tensor.matmul
        if name == "RX":
            pe.wait_ge(self.normed, g.n + 1)
            for b in range(GB):
                last = self.nc.tensor.transpose(self.misc[:, b * S:(b + 1) * S], self.xn[g.par][:, b], self.route.ident[:])
        elif name == "RQ":
            for b in range(GB):
                last = mm(self.misc[:, b * 3 * E:(b + 1) * 3 * E], self.xnT[:, b * S:(b + 1) * S], self.route.wT[:],
                          start=True, stop=True)
        else:
            pe.wait_ge(self.hits_ready, g.n + 1)
            hits = self.hits[:].rearrange("s b e -> s (b e)")
            for b in range(GB + 1):
                for earlier in range(b):
                    last = mm(self.misc[:, b * E:(b + 1) * E], self.route.ones[:], hits[:, earlier * E:(earlier + 1) * E],
                              start=(earlier == 0), stop=(b == GB and earlier == b - 1))
                if b < GB:
                    last = mm(self.misc[:, b * E:(b + 1) * E], self.route.before[:], hits[:, b * E:(b + 1) * E],
                              start=(b == 0), stop=True)
        return last

    def deviation(self, pool, g):
        wait_apart(pool, self.aggregated, g.n + 1, self.passed)
        self.nc.gpsimd.tensor_scalar(self.rstd[:], self.mv[:, :, 1], EPS, None, ALU.add).then_inc(self.eps_added, 1)
        wait_apart(pool, self.eps_added, g.n + 1, self.passed)
        self.nc.gpsimd.tensor_tensor(self.rstd[:], self.rstd[:], self.route.half_neg[:], ALU.pow).then_inc(self.rstd_ready, 1)

    def scatter(self, pool, g):
        wait_apart(pool, self.slot_ready, g.n + 1, self.passed)
        for b in range(GB):
            for k in range(TOP):
                self.nc.gpsimd.indirect_dma_start(
                    out=self.route.xs, out_offset=bass.IndirectOffsetOnAxis(ap=self.slot[g.par][:, b, k:k + 1], axis=0),
                    in_=self.xn[g.par][:, b], in_offset=None).then_inc(self.scattered[g.par], 16)

    def scattering_done(self, pool):
        for p in range(2):
            pool.wait_ge(self.scattered[p], NG // 2 * GB * TOP * 16)


ROUTE_STAGES = {
    (0, 1): (2, Router.weigh, 0), (0, 2): (2, Router.weigh, 1),
    (0, 3): (2, Router.form_logits, 0), (1, 0): (2, Router.form_logits, 1), (1, 1): (2, Router.form_logits, 2),
    (2, 1): (2, Router.pick, 0), (2, 2): (2, Router.pick, 1), (2, 3): (2, Router.pick, 2),
    (3, 1): (1, Router.statistics, 0), (3, 2): (1, Router.statistics, 1), (3, 3): (1, Router.statistics, 2),
    (4, 0): (2, Router.form_slots, 0), (4, 1): (2, Router.form_slots, 1), (4, 2): (2, Router.form_slots, 2),
    (4, 3): (2, Router.form_slots, 3),
    (5, 1): (1, Router.normalise, 0), (5, 2): (1, Router.normalise, 1),
    (7, 0): (1, Router.form_products, 0), (7, 1): (1, Router.form_products, 1), (7, 2): (1, Router.form_products, 2),
}


class Route:

    def __init__(self, nc, c, xs):
        sb = lambda name, shape, dt=F32: c.enter_context(nc.sbuf_tensor("route_" + name, shape, dt))
        self.xs = xs
        self.gates_all, self.slots_f = sb("gates_all", [S, NG, GB, TOP]), sb("slots_f", [S, NG * GB * TOP])
        self.count, self.region0 = sb("count", [S, E]), sb("region0", [S, E])
        self.iota_e, self.iota_ei = sb("iota_e", [S, E]), sb("iota_ei", [S, E], I32)
        self.slots_all = sb("slots_all", [S, NG, GB, TOP], mybir.dt.uint32)
        self.tile_row, self.tile_expert = sb("tile_row", [1, TILES], I32), sb("tile_expert", [1, TILES], I32)


def expert_tiles(nc, ys, w1, w2, route):
    xs, tile_row, tile_expert = route.xs, route.tile_row, route.tile_expert
    NB1 = E * 2 * F // 128
    with ExitStack() as c:
        sb = lambda name, shape, dt=F32: c.enter_context(nc.sbuf_tensor("M_" + name, shape, dt))
        pb = lambda name, shape, dt=F32: c.enter_context(nc.psum_tensor("M_" + name, shape, dt))
        sem = c.enter_context(phase_semaphores(nc, "M_"))
        two = lambda f: [f(0), f(1)]
        ident = sb("ident", [128, 128])
        w1T, w2T = sb("w1T", [D, E * 2 * F]), sb("w2T", [128, len(FCHUNKS), E * D])
        w1_raw, w2_raw = sb("w1_raw", [128, NB1, D]), sb("w2_raw", [D, E, F])
        NX = 4
        x_t = [sb(f"x{i}", [S, D]) for i in range(NX)]
        xT = two(lambda p: sb(f"xT{p}", [D, S]))
        act_a = two(lambda p: sb(f"act_a{p}", [S, F]))
        h_t = two(lambda p: sb(f"h{p}", [S, F]))
        hT = two(lambda p: sb(f"hT{p}", [128, len(FCHUNKS), S]))
        y_t = [sb(f"y{i}", [S, D]) for i in range(NX)]
        ps_x, ps_y, ps_t = pb("ps_x", [D, 512]), pb("ps_y", [S, 512]), pb("ps_t", [128, 512])
        ps_a, ps_g = two(lambda p: pb(f"ps_a{p}", [S, 512])), two(lambda p: pb(f"ps_g{p}", [S, 512]))

        zeros = sb("zeros", [128, D])
        iota_t, iota_ti = sb("iota_t", [1, TILES]), sb("iota_ti", [1, TILES], I32)
        nf, ni, nt_i, ntf, te, delta = (sb(n, [S, E], dt) for n, dt in
            (("nf", F32), ("ni", I32), ("nt_i", I32), ("ntf", F32), ("te", F32), ("delta", F32)))
        end_row = sb("end_row", [1, E], I32)
        tmask, tm2 = sb("tmask", [1, TILES, E]), sb("tm2", [1, TILES, E])
        tef, trf = sb("tef", [1, TILES]), sb("trf", [1, TILES])
        crossed, moved = sb("crossed", [S, NG * GB * TOP, E - 1]), sb("moved", [S, NG * GB * TOP])
        order, ends_ready, table_ready, zeroed, iotas_made = (sem(n) for n in ("order", "ends_ready", "table_ready", "zeroed", "iotas_made"))

        W1_CHUNKS = 4
        w1_loaded, w2_loaded = [sem(f"w1_loaded{k}") for k in range(W1_CHUNKS)], sem("w2_loaded")
        cleared, made = sem("cleared"), sem("made")
        w_turned, w_copied = sem("w_turned"), sem("w_copied")
        x_loaded = [sem(f"x_loaded{i}") for i in range(NX)]
        x_turned, xT_ready, hidden, silu_ready, h_ready, h_turned, hT_ready, y_done, y_ready = (sem(n) for n in
            ("x_turned", "xT_ready", "hidden", "silu_ready", "h_ready", "h_turned", "hT_ready", "y_done", "y_ready"))
        y_stored = [sem(f"y_stored{i}") for i in range(NX)]
        passed = sem("passed")
        block = c.enter_context(nc.Block())
        U = NX

        def run(eng, step):
            for t in range(-U, U):
                step(t, t % U, 0)
            with eng.Fori(1, TILES // U - 1) as turn:
                for i in range(U):
                    step(turn * U + i, i, turn)
            for t in range(TILES - U, TILES + U):
                step(t, t % U, 0)

        def has(t):
            return not isinstance(t, int) or 0 <= t < TILES

        def row_of(eng, t):
            cell = tile_row[0:1, t:t + 1] if isinstance(t, int) else tile_row[0:1, bass.ds(t, 1)]
            return eng.value_load(cell, min_val=0, max_val=ROUTED_ROWS - S)

        def expert_of(eng, t):
            cell = tile_expert[0:1, t:t + 1] if isinstance(t, int) else tile_expert[0:1, bass.ds(t, 1)]
            return eng.value_load(cell, min_val=0, max_val=E - 1)

        def nth(t, i):
            return (t // U + 1) * 16 if isinstance(t, int) else (t - i + U) * (16 // U)

        @block.sync
        def _(sp):
            for k in range(W1_CHUNKS):
                n = NB1 // W1_CHUNKS
                sp.dma_start(w1_raw[:, k * n:(k + 1) * n],
                             w1.rearrange("e f d -> (e f) d").rearrange("(j p) d -> p j d", p=128)[:, k * n:(k + 1) * n]).then_inc(w1_loaded[k], 16)
            sp.dma_start(w2_raw[:], w2.rearrange("e d f -> d e f")).then_inc(w2_loaded, 16)
            sp.wait_ge(iotas_made, 3)
            for k in range(E):
                sp.dma_start(xs[SPARE + k * S:SPARE + (k + 1) * S], zeros[:]).then_inc(zeroed, 16)
            sp.wait_ge(ends_ready, 1)
            for e in range(E):
                row = sp.value_load(end_row[0:1, e:e + 1], min_val=e * REGION, max_val=e * REGION + TOKENS)
                sp.dma_start(xs[bass.ds(row, S)], zeros[:]).then_inc(zeroed, 16)
            sp.wait_ge(zeroed, 2 * E * 16)
            sp.wait_ge(table_ready, 1)

            def step(t, i, turn):
                tl, tll = t + 3, (i + 3) % U
                if has(tl):
                    wait_apart(sp, x_turned, tl - U + 1, passed)
                    r = row_of(sp, tl)
                    sp.dma_start(x_t[tll][:], xs[bass.ds(r, S)]).then_inc(x_loaded[tll], 16)
            run(sp, step)

        @block.gpsimd
        def _(pool):
            diagonal(nc, pool, ident, cleared, made)
            nc.gpsimd.iota(iota_ti[:], pattern=[[1, TILES]], base=0, channel_multiplier=0).then_inc(iotas_made, 1)
            pool.wait_ge(iotas_made, 1)
            nc.gpsimd.tensor_copy(iota_t[:], iota_ti[:]).then_inc(iotas_made, 1)
            nc.gpsimd.memset(zeros[:], 0.0).then_inc(iotas_made, 1)
            pool.wait_ge(table_ready, 1)

            def step(t, i, turn):
                ts, si = t - 3, (i - 3) % U
                if has(ts):
                    wait_apart(pool, y_ready, ts + 1, passed)
                    pool.dma_start(ys[ts * S:(ts + 1) * S] if isinstance(ts, int) else ys[bass.ds(ts * S, S)], y_t[si][:]).then_inc(y_stored[si], 16)
            run(pool, step)
            for i in range(NX):
                pool.wait_ge(y_stored[i], TILES // NX * 16)

        @block.tensor
        def _(pe):
            pe.wait_ge(made, 1)
            for j in range(NB1 // 4):
                pe.wait_ge(w1_loaded[(4 * j + 3) * W1_CHUNKS // NB1], 16)
                wait(pe, w_copied, j - 1)
                for k in range(4):
                    last = nc.tensor.transpose(ps_a[j % 2][:, k * 128:(k + 1) * 128], w1_raw[:, 4 * j + k], ident[:])
                last.then_inc(w_turned, 1)
            pe.wait_ge(w2_loaded, 16)
            for e in range(E):
                n = NB1 // 4 + e
                wait(pe, w_copied, n - 1)
                for k, (f0, fn) in enumerate(FCHUNKS):
                    last = nc.tensor.transpose(ps_a[n % 2][0:fn, k * 128:(k + 1) * 128], w2_raw[:, e, f0:f0 + fn], ident[:])
                last.then_inc(w_turned, 1)
            pe.wait_ge(w_copied, NB1 // 4 + E)
            pe.wait_ge(table_ready, 1)

            def step(t, i, turn):
                tx, th, tt, ty = t + 2, t + 1, t, t - 1
                if has(th):
                    e_h = expert_of(pe, th)
                if has(ty):
                    e_y = expert_of(pe, ty)
                if has(tx):
                    pe.wait_ge(x_loaded[(i + 2) % U], nth(tx, (i + 2) % U))
                    wait(pe, xT_ready, tx)
                    nc.tensor.transpose(ps_x[:, 0:S], x_t[(i + 2) % U][:], ident[:]).then_inc(x_turned, 1)
                if has(th):
                    p = (i + 1) % 2
                    pe.wait_ge(xT_ready, th + 1)
                    wait(pe, h_ready, th - 1)
                    nc.tensor.matmul(ps_a[p][:, 0:F], xT[p][:], w1T[:, bass.ds(e_h * (2 * F), F)], start=True, stop=True)
                    nc.tensor.matmul(ps_g[p][:, 0:F], xT[p][:], w1T[:, bass.ds(e_h * (2 * F) + F, F)],
                                     start=True, stop=True).then_inc(hidden, 1)
                if has(tt):
                    p = i % 2
                    pe.wait_ge(h_ready, tt + 1)
                    wait(pe, hT_ready, tt)
                    for k, (f0, fn) in enumerate(FCHUNKS):
                        last = nc.tensor.transpose(ps_t[0:fn, k * S:(k + 1) * S], h_t[p][:, f0:f0 + fn], ident[:])
                    last.then_inc(h_turned, 1)
                if has(ty):
                    p = (i - 1) % 2
                    pe.wait_ge(hT_ready, ty + 1)
                    wait(pe, y_ready, ty)
                    for k, (f0, fn) in enumerate(FCHUNKS):
                        last = nc.tensor.matmul(ps_y[:, 0:D], hT[p][0:fn, k], w2T[0:fn, k, bass.ds(e_y * D, D)],
                                                start=(k == 0), stop=(k == len(FCHUNKS) - 1))
                    last.then_inc(y_done, 1)
            run(pe, step)

        @block.scalar
        def _(act):
            for j in range(NB1 // 4):
                act.wait_ge(w_turned, j + 1)
                nc.scalar.copy(w1T[:, j * 512:(j + 1) * 512], ps_a[j % 2][:]).then_inc(w_copied, 1)
            for e in range(E):
                n = NB1 // 4 + e
                act.wait_ge(w_turned, n + 1)
                nc.scalar.copy(w2T[:, 0:2, e * D:(e + 1) * D], ps_a[n % 2][:, 0:256].rearrange("f (k d) -> f k d", d=D))
                nc.scalar.copy(w2T[0:F - 256, 2, e * D:(e + 1) * D], ps_a[n % 2][0:F - 256, 256:384]).then_inc(w_copied, 1)

            def step(t, i, turn):
                th, tt = t + 1, t
                if has(th):
                    p = (i + 1) % 2
                    act.wait_ge(hidden, th + 1)
                    nc.scalar.activation(act_a[p][:], ps_a[p][:, 0:F], ACT.Silu).then_inc(silu_ready, 1)
                if has(tt):
                    p = i % 2
                    act.wait_ge(h_turned, tt + 1)
                    wait(act, y_done, tt - 1)
                    nc.scalar.copy(hT[p][:, 0:2], ps_t[:, 0:2 * S].rearrange("f (k s) -> f k s", s=S))
                    nc.scalar.copy(hT[p][0:F - 256, 2], ps_t[0:F - 256, 2 * S:3 * S]).then_inc(hT_ready, 1)
            run(act, step)

        @block.vector
        def _(dve):
            v = nc.vector
            count, region0, slots_f, slots_all = route.count, route.region0, route.slots_f, route.slots_all
            links = [0]

            def link(ins):
                links[0] += 1
                ins.then_inc(order, 1)
                dve.wait_ge(order, links[0])
            v.tensor_copy(end_row[:], count[0:1]).then_inc(ends_ready, 1)
            link(v.tensor_tensor(nf[:], count[:], region0[:], ALU.subtract))
            link(v.tensor_scalar(ni[:], nf[:], float(S - 1), None, ALU.add))
            link(v.tensor_scalar(nt_i[:], ni[:], S.bit_length() - 1, None, ALU.logical_shift_right))
            link(v.tensor_copy(ntf[:], nt_i[:]))
            link(v.tensor_copy(te[:], ntf[:]))
            for e in range(1, E):
                link(v.tensor_tensor(te[:, e:e + 1], te[:, e - 1:e], ntf[:, e:e + 1], ALU.add))
            table = [1, TILES, E]
            dve.wait_ge(iotas_made, 2)
            link(v.tensor_tensor(tmask[:], iota_t[:].unsqueeze(2).to_broadcast(table), te[0:1].unsqueeze(1).to_broadcast(table), ALU.is_ge))
            link(v.tensor_reduce(tef[:], tmask[:], AX.X, ALU.add))
            link(v.tensor_scalar(tile_expert[:], tef[:], float(E - 1), None, ALU.min))
            link(v.tensor_scalar(delta[:], ntf[:], -float(S), float(REGION), ALU.mult, ALU.add))
            link(v.tensor_tensor(tm2[:], tmask[:], delta[0:1].unsqueeze(1).to_broadcast(table), ALU.mult))
            link(v.tensor_reduce(trf[:], tm2[:], AX.X, ALU.add))
            link(v.scalar_tensor_tensor(trf[:], iota_t[:], float(S), trf[:], ALU.mult, ALU.add))
            v.tensor_copy(tile_row[:], trf[:]).then_inc(table_ready, 1)
            each = [S, NG * GB * TOP, E - 1]
            link(v.tensor_tensor(crossed[:], slots_f[:].unsqueeze(2).to_broadcast(each),
                                 region0[:, 1:E].unsqueeze(1).to_broadcast(each), ALU.is_ge))
            link(v.tensor_tensor(crossed[:], crossed[:], delta[:, 0:E - 1].unsqueeze(1).to_broadcast(each), ALU.mult))
            link(v.tensor_reduce(moved[:], crossed[:], AX.X, ALU.add))
            link(v.tensor_tensor(slots_all[:].rearrange("s n b k -> s (n b k)"), slots_f[:], moved[:], ALU.subtract))

            def step(t, i, turn):
                tx, th, ty = t + 2, t + 1, t - 1
                if has(tx):
                    dve.wait_ge(x_turned, tx + 1)
                    wait(dve, hidden, tx - 1)
                    nc.vector.tensor_copy(xT[i % 2][:], ps_x[:, 0:S]).then_inc(xT_ready, 1)
                if has(th):
                    p = (i + 1) % 2
                    dve.wait_ge(silu_ready, th + 1)
                    wait(dve, h_turned, th - 1)
                    nc.vector.tensor_tensor(h_t[p][:], act_a[p][:], ps_g[p][:, 0:F], ALU.mult).then_inc(h_ready, 1)
                if has(ty):
                    j = (i - 1) % U
                    dve.wait_ge(y_done, ty + 1)
                    wait(dve, y_stored[j], nth(ty, j) - 16)
                    nc.vector.tensor_copy(y_t[j][:], ps_y[:, 0:D]).then_inc(y_ready, 1)
            run(dve, step)


R = 64
ER = E * R
SCALING = 2.0


def adapter_layer(nc, x3, out, Wg, bg, W1, W2):
    x_v, o_v = (t.rearrange("(n b) s d -> n s b d", b=GB) for t in (x3, out))
    with ExitStack() as c:
        sb = lambda name, shape, dt=F32: c.enter_context(nc.sbuf_tensor("F_" + name, shape, dt))
        pb = lambda name, shape, dt=F32: c.enter_context(nc.psum_tensor("F_" + name, shape, dt))
        sem = c.enter_context(phase_semaphores(nc, "F_"))
        two = lambda f: [f(0), f(1)]
        ident, half_neg, euler = sb("ident", [128, 128]), sb("half_neg", [S, GB]), sb("euler", [S, GB])
        iota_e, iota_ei = sb("iota_e", [S, E]), sb("iota_ei", [S, E], I32)
        wg_raw, bg_bc = sb("wg_raw", [E, D]), sb("bg_bc", [S, E])
        w1_raw, w2_raw = sb("w1_raw", [128, ER // 128, D]), sb("w2_raw", [D, E, R])
        wgT, w1T, w2T = sb("wgT", [D, E]), sb("w1T", [D, ER]), sb("w2T", [128, ER // 128, D])
        x_t = two(lambda p: sb(f"x{p}", [S, GB, D]))
        res_t = two(lambda p: sb(f"res{p}", [S, GB, D]))
        stats, mv, rstd, xn = sb("stats", [S, GB, 6]), sb("mv", [S, GB, 2]), sb("rstd", [S, GB]), sb("xn", [S, GB, D])
        xnT = two(lambda p: sb(f"xnT{p}", [D, GB, S]))
        lg, top = sb("lg", [S, GB, E]), sb("top", [S, GB, 8])
        top_i, idx_f = sb("top_i", [S, GB, 8], mybir.dt.uint32), sb("idx_f", [S, GB, TOP])
        diff, e2, den, gates = sb("diff", [S, GB]), sb("e2", [S, GB]), sb("den", [S, GB]), sb("gates", [S, GB, TOP])
        oh = sb("oh", [S, GB, TOP, E])
        gate_e = two(lambda p: sb(f"gate_e{p}", [S, GB, E]))
        h_t, hg = two(lambda p: sb(f"h{p}", [S, ER])), two(lambda p: sb(f"hg{p}", [S, ER]))
        hgT = two(lambda p: sb(f"hgT{p}", [128, ER]))
        out_t = two(lambda p: sb(f"out{p}", [S, GB, D]))
        ps_x, ps_l, ps_y = pb("ps_x", [D, GB, S]), pb("ps_l", [S, GB, E]), pb("ps_y", [S, 512])
        ps_h, ps_t = two(lambda p: pb(f"ps_h{p}", [S, 512])), two(lambda p: pb(f"ps_t{p}", [128, 512]))

        loaded, cleared, made = sem("loaded"), sem("cleared"), sem("made")
        w_turned, w_copied, passed, order = sem("w_turned"), sem("w_copied"), sem("passed"), sem("order")
        x_loaded, res_loaded, stored = (two(lambda p: sem(f"{n}{p}")) for n in ("x_loaded", "res_loaded", "stored"))
        (stats_ready, aggregated, eps_added, rstd_ready, normed, x_turned, xT_ready, logits_done, gap_ready, e2_ready,
         gates_ready, hidden, gelu_ready, gated, h_turned, hT_ready, y_done, summed) = (sem(n) for n in (
            "stats_ready", "aggregated", "eps_added", "rstd_ready", "normed", "x_turned", "xT_ready", "logits_done",
            "gap_ready", "e2_ready", "gates_ready", "hidden", "gelu_ready", "gated", "h_turned", "hT_ready", "y_done", "summed"))
        ORDER = 10
        block = c.enter_context(nc.Block())

        def at(g, b):
            gg, bb = (g + 1, b - GB) if b >= GB else (g + -1, b + GB) if b < 0 else (g, b)
            return gg, bb, gg.n * GB + bb

        @block.sync
        def _(sp):
            sp.dma_start(w1_raw[:], W1.rearrange("e r d -> (e r) d").rearrange("(j p) d -> p j d", p=128)).then_inc(loaded, 16)
            sp.dma_start(w2_raw[:], W2.rearrange("e d r -> d e r")).then_inc(loaded, 16)
            sp.dma_start(wg_raw[:], Wg).then_inc(loaded, 16)
            sp.dma_start(bg_bc[:], bg.unsqueeze(0).to_broadcast([S, E])).then_inc(loaded, 16)

            def step(g):
                g3, gm = g + 3, g + -1
                if g3.exists:
                    wait_apart(sp, normed, g3.n - 1, passed)
                    sp.dma_start(x_t[g3.par][:], x_v[g3.n]).then_inc(x_loaded[g3.par], 16)
                if g.exists:
                    wait_apart(sp, summed, (g.n - 1) * GB, passed)
                    sp.dma_start(res_t[g.par][:], x_v[g.n]).then_inc(res_loaded[g.par], 16)
                if gm.exists:
                    wait_apart(sp, summed, (gm.n + 1) * GB, passed)
                    sp.dma_start(o_v[gm.n], out_t[gm.par][:]).then_inc(stored[gm.par], 16)
            loop_groups(sp, step)
            for p in range(2):
                sp.wait_ge(stored[p], NG // 2 * 16)

        @block.gpsimd
        def _(pool):
            nc.gpsimd.memset(half_neg[:], -0.5).then_inc(cleared, 1)
            pool.wait_ge(cleared, 1)
            nc.gpsimd.memset(ident[:], 0.0).then_inc(cleared, 1)
            pool.wait_ge(cleared, 2)
            nc.gpsimd.affine_select(out=ident[:], in_=ident[:], compare_op=ALU.not_equal, fill=1.0, base=0,
                                    pattern=[[-1, 128]], channel_multiplier=1).then_inc(made, 1)
            nc.gpsimd.iota(iota_ei[:], pattern=[[1, E]], base=0, channel_multiplier=0).then_inc(cleared, 1)
            pool.wait_ge(cleared, 3)
            nc.gpsimd.tensor_copy(iota_e[:], iota_ei[:]).then_inc(made, 1)
            nc.gpsimd.memset(euler[:], float(np.e)).then_inc(cleared, 1)
            pool.wait_ge(cleared, 4)

            def step(g):
                g1, g2 = g + 1, g + 2
                if g2.exists:
                    wait_apart(pool, aggregated, g2.n + 1, passed)
                    nc.gpsimd.tensor_scalar(rstd[:], mv[:, :, 1], EPS, None, ALU.add).then_inc(eps_added, 1)
                    wait_apart(pool, eps_added, g2.n + 1, passed)
                    nc.gpsimd.tensor_tensor(rstd[:], rstd[:], half_neg[:], ALU.pow).then_inc(rstd_ready, 1)
                if g1.exists:
                    wait_apart(pool, gap_ready, g1.n + 1, passed)
                    nc.gpsimd.tensor_tensor(e2[:], euler[:], diff[:], ALU.pow).then_inc(e2_ready, 1)
            loop_groups(pool, step)

        @block.tensor
        def _(pe):
            pe.wait_ge(loaded, 16 * 4)
            pe.wait_ge(made, 1)
            for j in range(ER // 128):
                last = nc.tensor.transpose(ps_h[0][:, j * 128:(j + 1) * 128], w1_raw[:, j], ident[:])
            last.then_inc(w_turned, 1)
            w2_rows = w2_raw[:].rearrange("d e r -> d (e r)")
            for j in range(ER // 128):
                last = nc.tensor.transpose(ps_h[1][:, j * 128:(j + 1) * 128], w2_rows[:, j * 128:(j + 1) * 128], ident[:])
            last.then_inc(w_turned, 1)
            nc.tensor.transpose(ps_y[:, 0:E], wg_raw[:], ident[0:E, 0:E]).then_inc(w_turned, 1)
            pe.wait_ge(w_copied, 3)

            def step(g):
                g1 = g + 1
                for b in range(GB):
                    if b == 0 and g1.exists:
                        pe.wait_ge(normed, g1.n + 1)
                        wait(pe, xT_ready, g1.n)
                        for j in range(GB):
                            last = nc.tensor.transpose(ps_x[:, j], xn[:, j], ident[:])
                        last.then_inc(x_turned, 1)
                    if b == 1 and g1.exists:
                        pe.wait_ge(xT_ready, g1.n + 1)
                        wait(pe, gap_ready, g1.n)
                        for j in range(GB):
                            last = nc.tensor.matmul(ps_l[:, j], xnT[g1.par][:, j], wgT[:], start=True, stop=True)
                        last.then_inc(logits_done, 1)
                    gh, bh, vh = at(g, b + 1)
                    if gh.exists:
                        if bh == 0:
                            pe.wait_ge(xT_ready, gh.n + 1)
                        wait(pe, gelu_ready, vh - 1)
                        nc.tensor.matmul(ps_h[bh % 2][:], xnT[gh.par][:, bh], w1T[:], start=True, stop=True).then_inc(hidden, 1)
                    if g.exists:
                        v = g.n * GB + b
                        pe.wait_ge(gated, v + 1)
                        wait(pe, hT_ready, v - 1)
                        for j in range(ER // 128):
                            last = nc.tensor.transpose(ps_t[b % 2][:, j * 128:(j + 1) * 128], hg[b % 2][:, j * 128:(j + 1) * 128], ident[:])
                        last.then_inc(h_turned, 1)
                    gy, by, vy = at(g, b - 1)
                    if gy.exists:
                        pe.wait_ge(hT_ready, vy + 1)
                        wait(pe, summed, vy)
                        for j in range(ER // 128):
                            last = nc.tensor.matmul(ps_y[:, 0:D], hgT[by % 2][:, j * 128:(j + 1) * 128], w2T[:, j],
                                                    start=(j == 0), stop=(j == ER // 128 - 1))
                        last.then_inc(y_done, 1)
            loop_groups(pe, step)

        @block.scalar
        def _(act):
            def step(g):
                g1 = g + 1
                for b in range(GB):
                    if b == 0 and g1.exists:
                        act.wait_ge(x_turned, g1.n + 1)
                        wait(act, hidden, (g1.n - 1) * GB)
                        nc.scalar.copy(xnT[g1.par][:], ps_x[:]).then_inc(xT_ready, 1)
                    gh, bh, vh = at(g, b + 1)
                    if gh.exists:
                        act.wait_ge(hidden, vh + 1)
                        wait(act, gated, vh - 1)
                        nc.scalar.activation(h_t[bh % 2][:], ps_h[bh % 2][:], ACT.Gelu).then_inc(gelu_ready, 1)
                    if g.exists:
                        v = g.n * GB + b
                        act.wait_ge(h_turned, v + 1)
                        wait(act, y_done, v - 1)
                        nc.scalar.copy(hgT[b % 2][:], ps_t[b % 2][:]).then_inc(hT_ready, 1)
            loop_groups(act, step)

        @block.vector
        def _(dve):
            v_ = nc.vector
            dve.wait_ge(w_turned, 3)
            dve.wait_ge(made, 2)
            v_.tensor_copy(w1T[:], ps_h[0][:]).then_inc(w_copied, 1)
            v_.tensor_copy(w2T[:].rearrange("p j d -> p (j d)"), ps_h[1][:]).then_inc(w_copied, 1)
            v_.tensor_copy(wgT[:], ps_y[:, 0:E]).then_inc(w_copied, 1)

            def step(g):
                g1, g2 = g + 1, g + 2
                links = [0]

                def link(ins):
                    links[0] += 1
                    ins.then_inc(order, 1)
                    wait_apart(dve, order, g1.n * ORDER + links[0], passed)
                for b in range(GB):
                    if b == 0 and g2.exists:
                        wait_apart(dve, x_loaded[g2.par], (g2.pair + 1) * 16, passed)
                        for j in range(GB):
                            v_.bn_stats(stats[:, j], x_t[g2.par][:, j]).then_inc(stats_ready, 1)
                        wait_apart(dve, stats_ready, (g2.n + 1) * GB, passed)
                        for j in range(GB):
                            last = v_.bn_aggr(mv[:, j], stats[:, j])
                        last.then_inc(aggregated, 1)
                    if b == 3 and g2.exists:
                        wait_apart(dve, rstd_ready, g2.n + 1, passed)
                        wait_apart(dve, x_turned, g2.n, passed)
                        for j in range(GB):
                            last = v_.tensor_scalar(xn[:, j], x_t[g2.par][:, j], mv[:, j, 0:1], rstd[:, j:j + 1],
                                                    ALU.subtract, ALU.mult)
                        last.then_inc(normed, 1)
                    if b == 1 and g1.exists:
                        wait_apart(dve, logits_done, g1.n + 1, passed)
                        link(v_.tensor_tensor(lg[:], ps_l[:], bg_bc[:].unsqueeze(1).to_broadcast([S, GB, E]), ALU.add))
                        for j in range(GB):
                            last = v_.max(top[:, j], lg[:, j])
                        link(last)
                        for j in range(GB):
                            last = v_.max_index(top_i[:, j], top[:, j], lg[:, j])
                        link(last)
                        v_.tensor_tensor(diff[:], top[:, :, 1], top[:, :, 0], ALU.subtract).then_inc(gap_ready, 1)
                        link(v_.tensor_copy(idx_f[:], top_i[:, :, 0:TOP]))
                        picks = [S, GB, TOP, E]
                        link(v_.tensor_tensor(oh[:], iota_e[:].unsqueeze(1).unsqueeze(1).to_broadcast(picks),
                                              idx_f[:].unsqueeze(3).to_broadcast(picks), ALU.is_equal))
                    if b == 2 and g1.exists:
                        wait_apart(dve, e2_ready, g1.n + 1, passed)
                        link(v_.tensor_scalar(den[:], e2[:], 1.0, None, ALU.add))
                        link(v_.reciprocal(gates[:, :, 0], den[:]))
                        link(v_.tensor_tensor(gates[:, :, 1], e2[:], gates[:, :, 0], ALU.mult))
                        link(v_.tensor_tensor(oh[:], oh[:], gates[:].unsqueeze(3).to_broadcast(picks), ALU.mult))
                        link(v_.tensor_tensor(gate_e[g1.par][:], oh[:, :, 0], oh[:, :, 1], ALU.add))
                        assert links[0] == ORDER
                    gh, bh, vh = at(g, b + 1)
                    if gh.exists:
                        dve.wait_ge(gelu_ready, vh + 1)
                        wait(dve, h_turned, vh - 1)
                        v_.tensor_tensor(hg[bh % 2][:].rearrange("s (e r) -> s e r", r=R),
                                         h_t[bh % 2][:].rearrange("s (e r) -> s e r", r=R),
                                         gate_e[gh.par][:, bh].unsqueeze(2).to_broadcast([S, E, R]), ALU.mult).then_inc(gated, 1)
                    gy, by, vy = at(g, b - 1)
                    if gy.exists:
                        dve.wait_ge(y_done, vy + 1)
                        if by == 0:
                            wait_apart(dve, res_loaded[gy.par], (gy.pair + 1) * 16, passed)
                            wait_apart(dve, stored[gy.par], gy.pair * 16, passed)
                        v_.scalar_tensor_tensor(out_t[gy.par][:, by], ps_y[:, 0:D], SCALING, res_t[gy.par][:, by],
                                                ALU.mult, ALU.add).then_inc(summed, 1)
            loop_groups(dve, step)


def encoder(nc, a, out):
    x1, x3 = (nc.dram_tensor(n, (B, S, D), F32, kind="Internal").ap() for n in ("x1", "x3"))
    xs = nc.dram_tensor("routed_in", (ROUTED_ROWS, D), F32, kind="Internal").ap()
    ys = nc.dram_tensor("routed_out", (TILES * S, D), F32, kind="Internal").ap()
    with ExitStack() as c:
        route = Route(nc, c, xs)
        w = [[a["L0_xattn_" + n] for n in ("Wq", "bq", "Wk", "bk", "Wv", "bv", "Wp", "bp")],
             [a["L1_xattn_" + n] for n in ("W_q", "b_q", "W_k", "b_k", "W_v", "b_v", "W_o", "b_o")]]
        consts = constants(nc, c, w, a["L0_ffn_wqkv"], route)
        attention_layer(nc, a["x"], x1, a["fside_BxSxS_0"], a["ctx_1024"], 0, consts[0], route)
        expert_tiles(nc, ys, a["L0_ffn_w1"], a["L0_ffn_w2"], route)
        attention_layer(nc, x1, x3, a["fside_BxSxS_0"], a["ctx_1024"], 1, consts[1], route, ys)
    adapter_layer(nc, x3, out, a["L1_ffn_Wg"], a["L1_ffn_bg"], a["L1_ffn_W1"], a["L1_ffn_W2"])


INPUTS = ["x", "fside_BxSxS_0", "ctx_1024"] + ["L0_xattn_" + n for n in ("Wq", "bq", "Wk", "bk", "Wv", "bv", "Wp", "bp")] \
    + ["L0_ffn_" + n for n in ("wqkv", "w1", "w2")] \
    + ["L1_xattn_" + n for n in ("W_q", "b_q", "W_k", "b_k", "W_v", "b_v", "W_o", "b_o")] \
    + ["L1_ffn_" + n for n in ("Wg", "bg", "W1", "W2")]


def kernel(**inputs):
    import concourse.bacc as bacc
    from concourse.bass_utils import run_bass_kernel_spmd as run

    nc = bacc.Bacc("TRN2", target_bir_lowering=False, num_devices=1)
    arrays, tensors = {}, {}
    for name in INPUTS:
        array = np.ascontiguousarray(inputs[name])
        arrays["in_" + name] = array
        tensors[name] = nc.dram_tensor("in_" + name, array.shape, mybir.dt.from_np(array.dtype), kind="ExternalInput").ap()
    out = nc.dram_tensor("out_0", (B, S, D), F32, kind="ExternalOutput").ap()
    encoder(nc, tensors, out)
    return run(nc, [arrays], core_ids=[0]).results[0]["out_0"]
```
